# Optimizing a Trainium2 kernel written in Bass

```python
import numpy as np
import jax
import jax.numpy as jnp

def _softmax(x, axis=-1):
    return jax.nn.softmax(x, axis=axis)

def _gelu(x):
    return jax.nn.gelu(x, approximate=True)

def _silu(x):
    return jax.nn.silu(x)

def _sigmoid(x):
    return jax.nn.sigmoid(x)

def _layernorm(x, axis=-1, eps=1e-05):
    m = jnp.mean(x, axis=axis, keepdims=True)
    v = jnp.var(x, axis=axis, keepdims=True)
    return (x - m) / jnp.sqrt(v + eps)

def _scatter_add(tgt, idx, src, axis=0):
    return tgt.at[idx].add(src)

def _segment_sum(src, seg, n):
    return jax.ops.segment_sum(src, seg, n)
kernel_name = 'mk_seq_preln_d2_jaxref_r8_dcc225'

def setup_inputs(seed: int=0):
    np.random.seed(seed)
    _w = jnp.asarray

    def _L0_attn_setup():
        import jax, jax.numpy as jnp
        import numpy as np
        HIDDEN = 128
        HEADS = 16
        CHUNK = 128
        NEG_INF = -10000000000.0
        key = jax.random.key(seed)
        k1, k2, k3 = jax.random.split(key, 3)
        B, S = (2, 512)
        x = jax.random.normal(k1, (B, S, HIDDEN), dtype=jnp.float32)
        w_qkv = jax.random.normal(k2, (HIDDEN, 3 * HIDDEN), dtype=jnp.float32) / np.sqrt(HIDDEN).astype(np.float32)
        w_out = jax.random.normal(k3, (HIDDEN, HIDDEN), dtype=jnp.float32) / np.sqrt(HIDDEN).astype(np.float32)
        return {'x': x, 'w_qkv': w_qkv, 'w_out': w_out}
    _L0_attn_in = _L0_attn_setup()

    def _L0_ffn_setup():
        import jax, jax.numpy as jnp
        import numpy as np
        NUM_EXPERTS = 8
        N_EMBD = 128
        D_FF = 4 * N_EMBD
        B, S = (4, 256)
        key = jax.random.key(seed)
        ks = jax.random.split(key, 6)
        x = jax.random.normal(ks[0], (B, S, N_EMBD), dtype=jnp.float32)
        gate_w = jax.random.normal(ks[1], (N_EMBD, NUM_EXPERTS), dtype=jnp.float32) * 0.02
        w1 = jax.random.normal(ks[2], (NUM_EXPERTS, N_EMBD, D_FF), dtype=jnp.float32) * 0.02
        b1 = jnp.zeros((NUM_EXPERTS, D_FF), dtype=jnp.float32)
        w2 = jax.random.normal(ks[3], (NUM_EXPERTS, D_FF, N_EMBD), dtype=jnp.float32) * 0.02
        b2 = jnp.zeros((NUM_EXPERTS, N_EMBD), dtype=jnp.float32)
        return {'x': x, 'gate_w': gate_w, 'w1': w1, 'b1': b1, 'w2': w2, 'b2': b2}
    _L0_ffn_in = _L0_ffn_setup()

    def _L1_attn_setup():
        import jax, jax.numpy as jnp
        import numpy as np
        import math
        _OFFSETS = sorted(set(range(0, 33)) | {48, 64, 96, 128, 192, 32, 48, 64, 96, 128, 192})
        B, N, D, H, FFN = (1, 256, 128, 16, 352)
        EPS = 1e-06

        def _rmsnorm(x, scale):
            rms = jnp.sqrt(jnp.mean(x * x, axis=-1, keepdims=True) + EPS)
            return scale * (x / rms)
        key = jax.random.key(seed)
        ks = jax.random.split(key, 8)
        s = 0.02
        alphas = jnp.linspace(0.2, 2.0, H)
        delta_vals = jnp.array([math.log(1.0 + max(d, 0.2)) for d in _OFFSETS], dtype=jnp.float32)
        pos_bias = -delta_vals[:, None] * alphas[None, :]
        return {'x': jax.random.normal(ks[0], (B, N, D), jnp.float32), 'norm1_scale': jnp.ones((D,), jnp.float32), 'norm2_scale': jnp.ones((D,), jnp.float32), 'w_qkv': jax.random.normal(ks[1], (D, 3 * D), jnp.float32) * s, 'w_out': jax.random.normal(ks[2], (D, D), jnp.float32) * s, 'w_gate': jax.random.normal(ks[3], (D, D), jnp.float32) * s, 'b_gate': jnp.full((D,), 2.0, jnp.float32), 'pos_bias': pos_bias, 'w_ffn_gate': jax.random.normal(ks[4], (D, FFN), jnp.float32) * s, 'w_ffn_up': jax.random.normal(ks[5], (D, FFN), jnp.float32) * s, 'w_ffn_down': jax.random.normal(ks[6], (FFN, D), jnp.float32) * s, 'offsets': jnp.array(_OFFSETS, dtype=jnp.int32)}
    _L1_attn_in = _L1_attn_setup()

    def _L1_ffn_setup():
        import jax, jax.numpy as jnp
        import numpy as np
        DIM = 128
        NUM_HEAVY = 128
        N_ITERS = 50
        EPS = 1.0
        FETCH_K_RATIO = 9.0 / 8.0

        def rms_norm(x, gamma):
            norm = jnp.maximum(jnp.linalg.norm(x, axis=-1, keepdims=True), 1e-12)
            return x / norm * x.shape[-1] ** 0.5 * gamma

        def feed_forward(x, gamma, w1, b1, w2, b2):
            h = jax.nn.gelu(rms_norm(x, gamma) @ w1 + b1, approximate=False)
            return h @ w2 + b2

        def coor_descent(s, k, n_iters, eps):
            logk = jnp.log(jnp.asarray(k, dtype=s.dtype))

            def step(ab, _):
                a, b = ab
                sb = (s + b) / eps
                a = eps * (logk - jax.scipy.special.logsumexp(sb, axis=-1, keepdims=True))
                b = -jax.nn.relu(s + a)
                return ((a, b), None)
            a0 = jnp.zeros_like(s[..., :1])
            b0 = -s
            (a, b), _ = jax.lax.scan(step, (a0, b0), None, length=n_iters)
            return jnp.exp((s + a + b) / eps)
        key = jax.random.key(seed)
        ks = jax.random.split(key, 8)
        b, n, d = (4, 1024, DIM)
        dl, dh = (int(d * 0.5), d * 4)
        u = lambda k, shape, fan_in: jax.random.uniform(k, shape, jnp.float32, -1.0, 1.0) / np.sqrt(fan_in)
        return {'x': jax.random.normal(ks[0], (b, n, d), jnp.float32), 'routing_token': jax.random.normal(ks[1], (d,), jnp.float32), 'light_gamma': jnp.ones((d,), jnp.float32), 'light_w1': u(ks[2], (d, dl), d), 'light_b1': jnp.zeros((dl,), jnp.float32), 'light_w2': u(ks[3], (dl, d), dl), 'light_b2': jnp.zeros((d,), jnp.float32), 'heavy_gamma': jnp.ones((d,), jnp.float32), 'heavy_w1': u(ks[4], (d, dh), d), 'heavy_b1': jnp.zeros((dh,), jnp.float32), 'heavy_w2': u(ks[5], (dh, d), dh), 'heavy_b2': jnp.zeros((d,), jnp.float32)}
    _L1_ffn_in = _L1_ffn_setup()
    _d = {'L0_attn_x': _L0_attn_in['x'], 'L0_attn_w_qkv': _L0_attn_in['w_qkv'], 'L0_attn_w_out': _L0_attn_in['w_out'], 'L0_ffn_gate_w': _L0_ffn_in['gate_w'], 'L0_ffn_w1': _L0_ffn_in['w1'], 'L0_ffn_b1': _L0_ffn_in['b1'], 'L0_ffn_w2': _L0_ffn_in['w2'], 'L0_ffn_b2': _L0_ffn_in['b2'], 'L1_attn_norm1_scale': _L1_attn_in['norm1_scale'], 'L1_attn_norm2_scale': _L1_attn_in['norm2_scale'], 'L1_attn_w_qkv': _L1_attn_in['w_qkv'], 'L1_attn_w_out': _L1_attn_in['w_out'], 'L1_attn_w_gate': _L1_attn_in['w_gate'], 'L1_attn_b_gate': _L1_attn_in['b_gate'], 'L1_attn_pos_bias': _L1_attn_in['pos_bias'], 'L1_attn_w_ffn_gate': _L1_attn_in['w_ffn_gate'], 'L1_attn_w_ffn_up': _L1_attn_in['w_ffn_up'], 'L1_attn_w_ffn_down': _L1_attn_in['w_ffn_down'], 'L1_attn_offsets': _L1_attn_in['offsets'], 'L1_ffn_routing_token': _L1_ffn_in['routing_token'], 'L1_ffn_light_gamma': _L1_ffn_in['light_gamma'], 'L1_ffn_light_w1': _L1_ffn_in['light_w1'], 'L1_ffn_light_b1': _L1_ffn_in['light_b1'], 'L1_ffn_light_w2': _L1_ffn_in['light_w2'], 'L1_ffn_light_b2': _L1_ffn_in['light_b2'], 'L1_ffn_heavy_gamma': _L1_ffn_in['heavy_gamma'], 'L1_ffn_heavy_w1': _L1_ffn_in['heavy_w1'], 'L1_ffn_heavy_b1': _L1_ffn_in['heavy_b1'], 'L1_ffn_heavy_w2': _L1_ffn_in['heavy_w2'], 'L1_ffn_heavy_b2': _L1_ffn_in['heavy_b2']}
    _x0 = _d['L0_attn_x']
    _d['L0_attn_x'] = jax.random.normal(jax.random.fold_in(jax.random.key(seed), 1), (8, 1024, 128), dtype=_x0.dtype)
    del _x0
    return _d

def reference(L0_attn_x, L0_attn_w_qkv, L0_attn_w_out, L0_ffn_gate_w, L0_ffn_w1, L0_ffn_b1, L0_ffn_w2, L0_ffn_b2, L1_attn_norm1_scale, L1_attn_norm2_scale, L1_attn_w_qkv, L1_attn_w_out, L1_attn_w_gate, L1_attn_b_gate, L1_attn_pos_bias, L1_attn_w_ffn_gate, L1_attn_w_ffn_up, L1_attn_w_ffn_down, L1_attn_offsets, L1_ffn_routing_token, L1_ffn_light_gamma, L1_ffn_light_w1, L1_ffn_light_b1, L1_ffn_light_w2, L1_ffn_light_b2, L1_ffn_heavy_gamma, L1_ffn_heavy_w1, L1_ffn_heavy_b1, L1_ffn_heavy_w2, L1_ffn_heavy_b2):

    def _L0_attn_ref(x, w_qkv, w_out):
        import jax, jax.numpy as jnp
        import numpy as np
        HIDDEN = 128
        HEADS = 16
        CHUNK = 128
        NEG_INF = -10000000000.0
        B, S, _ = x.shape
        H, D = (HEADS, HIDDEN // HEADS)
        qkv = (x @ w_qkv).reshape(B, S, 3, H, D)
        q, k, v = (qkv[:, :, 0], qkv[:, :, 1], qkv[:, :, 2])
        scale = jnp.sqrt(jnp.asarray(D, x.dtype))
        n_chunks = S // CHUNK
        q_chunks = q.reshape(B, n_chunks, CHUNK, H, D).transpose(1, 0, 2, 3, 4)
        starts = jnp.arange(n_chunks) * CHUNK

        def step(carry, inp):
            qc, start = inp
            scores = jnp.einsum('bqhd,bkhd->bhqk', qc, k) / scale
            causal = jnp.arange(CHUNK)[:, None] + start >= jnp.arange(S)[None, :]
            scores = jnp.where(causal[None, None], scores, NEG_INF)
            attn = jax.nn.softmax(scores, axis=-1)
            out_c = jnp.einsum('bhqk,bkhd->bqhd', attn, v).reshape(B, CHUNK, H * D)
            return (carry, out_c)
        _, outs = jax.lax.scan(step, None, (q_chunks, starts))
        out = outs.transpose(1, 0, 2, 3).reshape(B, S, H * D)
        return out @ w_out

    def _L0_ffn_ref(x, gate_w, w1, b1, w2, b2):
        import jax, jax.numpy as jnp
        import numpy as np
        NUM_EXPERTS = 8
        N_EMBD = 128
        D_FF = 4 * N_EMBD
        B, S = (4, 256)
        Bb, Ss, D = x.shape
        x_flat = x.reshape(-1, D)
        router_logits = x_flat @ gate_w
        router_probs = jax.nn.softmax(router_logits, axis=-1)
        expert_idx = jnp.argmax(router_probs, axis=-1)
        expert_w = jnp.take_along_axis(router_probs, expert_idx[:, None], axis=1)[:, 0]
        out = jnp.zeros_like(x_flat)
        for e in range(NUM_EXPERTS):
            h = jax.nn.gelu(x_flat @ w1[e] + b1[e], approximate=False)
            y = h @ w2[e] + b2[e]
            sel = expert_idx == e
            out = out + jnp.where(sel, expert_w, 0.0)[:, None] * y
        return out.reshape(Bb, Ss, D)

    def _L1_attn_ref(x, norm1_scale, norm2_scale, w_qkv, w_out, w_gate, b_gate, pos_bias, w_ffn_gate, w_ffn_up, w_ffn_down, offsets):
        import jax, jax.numpy as jnp
        import numpy as np
        import math
        _OFFSETS = sorted(set(range(0, 33)) | {48, 64, 96, 128, 192, 32, 48, 64, 96, 128, 192})
        B, N, D, H, FFN = (1, 256, 128, 16, 352)
        EPS = 1e-06

        def _rmsnorm(x, scale):
            rms = jnp.sqrt(jnp.mean(x * x, axis=-1, keepdims=True) + EPS)
            return scale * (x / rms)
        Bx, Nx, Dx = x.shape
        HD = Dx // H
        xn = _rmsnorm(x, norm1_scale)
        qkv = xn @ w_qkv
        q, k, v = jnp.split(qkv, 3, axis=-1)
        to_heads = lambda t: t.reshape(Bx, Nx, H, HD).transpose(0, 2, 1, 3)
        q, k, v = (to_heads(q), to_heads(k), to_heads(v))
        t_idx = jnp.arange(Nx)
        src = jnp.clip(t_idx[:, None] - offsets[None, :], 0, None)
        Kg = k[:, :, src, :]
        Vg = v[:, :, src, :]
        scale = HD ** (-0.5)
        scores = jnp.einsum('bhnd,bhnod->bhno', q, Kg) * scale
        scores = scores + pos_bias.T[None, :, None, :]
        invalid = t_idx[:, None] < offsets[None, :]
        scores = jnp.where(invalid[None, None], -jnp.inf, scores)
        alpha = jax.nn.softmax(scores, axis=-1)
        out = jnp.einsum('bhno,bhnod->bhnd', alpha, Vg)
        out = out.transpose(0, 2, 1, 3).reshape(Bx, Nx, Dx)
        gate = jax.nn.sigmoid(xn @ w_gate + b_gate)
        x = x + out * gate @ w_out
        xn2 = _rmsnorm(x, norm2_scale)
        x = x + jax.nn.silu(xn2 @ w_ffn_gate) * (xn2 @ w_ffn_up) @ w_ffn_down
        return x

    def _L1_ffn_ref(x, routing_token, light_gamma, light_w1, light_b1, light_w2, light_b2, heavy_gamma, heavy_w1, heavy_b1, heavy_w2, heavy_b2):
        import jax, jax.numpy as jnp
        import numpy as np
        DIM = 128
        NUM_HEAVY = 128
        N_ITERS = 50
        EPS = 1.0
        FETCH_K_RATIO = 9.0 / 8.0

        def rms_norm(x, gamma):
            norm = jnp.maximum(jnp.linalg.norm(x, axis=-1, keepdims=True), 1e-12)
            return x / norm * x.shape[-1] ** 0.5 * gamma

        def feed_forward(x, gamma, w1, b1, w2, b2):
            h = jax.nn.gelu(rms_norm(x, gamma) @ w1 + b1, approximate=False)
            return h @ w2 + b2

        def coor_descent(s, k, n_iters, eps):
            logk = jnp.log(jnp.asarray(k, dtype=s.dtype))

            def step(ab, _):
                a, b = ab
                sb = (s + b) / eps
                a = eps * (logk - jax.scipy.special.logsumexp(sb, axis=-1, keepdims=True))
                b = -jax.nn.relu(s + a)
                return ((a, b), None)
            a0 = jnp.zeros_like(s[..., :1])
            b0 = -s
            (a, b), _ = jax.lax.scan(step, (a0, b0), None, length=n_iters)
            return jnp.exp((s + a + b) / eps)
        b, n, d = x.shape
        light_out = feed_forward(x, light_gamma, light_w1, light_b1, light_w2, light_b2)
        s = jnp.einsum('bnd,d->bn', x, routing_token)
        effective_k = min(NUM_HEAVY * FETCH_K_RATIO, n)
        scores = coor_descent(s, effective_k, N_ITERS, EPS)
        sel_scores, sel_idx = jax.lax.top_k(scores, NUM_HEAVY)
        sel_scores = sel_scores + jax.lax.stop_gradient(1.0 - sel_scores)
        routed = jnp.take_along_axis(x, sel_idx[..., None], axis=1)
        routed_out = feed_forward(routed, heavy_gamma, heavy_w1, heavy_b1, heavy_w2, heavy_b2)
        routed_out = routed_out * sel_scores[..., None]
        batch_idx = jnp.arange(b)[:, None]
        heavy_out = jnp.zeros_like(x).at[batch_idx, sel_idx].set(routed_out)
        return light_out + heavy_out
    x = L0_attn_x
    x = x + _L0_attn_ref(_layernorm(x, axis=-1), L0_attn_w_qkv, L0_attn_w_out)
    x = x + _L0_ffn_ref(_layernorm(x, axis=-1), L0_ffn_gate_w, L0_ffn_w1, L0_ffn_b1, L0_ffn_w2, L0_ffn_b2)
    x = x + _L1_attn_ref(_layernorm(x, axis=-1), L1_attn_norm1_scale, L1_attn_norm2_scale, L1_attn_w_qkv, L1_attn_w_out, L1_attn_w_gate, L1_attn_b_gate, L1_attn_pos_bias, L1_attn_w_ffn_gate, L1_attn_w_ffn_up, L1_attn_w_ffn_down, L1_attn_offsets)
    x = x + _L1_ffn_ref(_layernorm(x, axis=-1), L1_ffn_routing_token, L1_ffn_light_gamma, L1_ffn_light_w1, L1_ffn_light_b1, L1_ffn_light_w2, L1_ffn_light_b2, L1_ffn_heavy_gamma, L1_ffn_heavy_w1, L1_ffn_heavy_b1, L1_ffn_heavy_w2, L1_ffn_heavy_b2)
    return x

_drawn_inputs = setup_inputs


def setup_inputs(seed=0):
    import zlib

    import numpy as np

    out = dict(_drawn_inputs(seed))
    spreads = {'L0_ffn_b1': (0.0, 0.8),
     'L0_ffn_b2': (0.0, 0.451),
     'L1_attn_norm1_scale': (1.0, 0.6),
     'L1_attn_norm2_scale': (1.0, 0.6),
     'L1_attn_b_gate': (2.0, 0.6),
     'L1_ffn_light_gamma': (1.0, 0.6),
     'L1_ffn_light_b1': (0.0, 2.0),
     'L1_ffn_light_b2': (0.0, 0.8),
     'L1_ffn_heavy_gamma': (1.0, 0.6),
     'L1_ffn_heavy_b1': (0.0, 2.0),
     'L1_ffn_heavy_b2': (0.0, 2.0)}
    factors = {'L0_ffn_gate_w': 2.936,
     'L0_ffn_w1': 5.714,
     'L0_ffn_w2': 5.184,
     'L1_attn_w_qkv': 5.95,
     'L1_attn_w_out': 5.922,
     'L1_attn_w_gate': 8.0,
     'L1_attn_pos_bias': 6.479,
     'L1_attn_w_ffn_gate': 8.0,
     'L1_attn_w_ffn_up': 8.0,
     'L1_attn_w_ffn_down': 8.0,
     'L1_ffn_routing_token': 4.006,
     'L1_ffn_heavy_w1': 8.0,
     'L1_ffn_heavy_w2': 5.574}
    for name, (base, spread) in spreads.items():
        noise = np.random.default_rng([zlib.crc32(name.encode()), seed]).standard_normal(out[name].shape)
        drawn = base * np.exp(spread * noise) if base else spread * noise
        out[name] = jnp.asarray(drawn.astype(out[name].dtype))
    for name, factor in factors.items():
        out[name] = (out[name] * factor).astype(out[name].dtype)
    return out
```

```python
from contextlib import ExitStack
import math

import concourse.bass as bass
from concourse import mybir

F32 = mybir.dt.float32
BF16 = mybir.dt.bfloat16
I32 = mybir.dt.int32
ACT = mybir.ActivationFunctionType
ALU = mybir.AluOpType
AX = mybir.AxisListType

P = 128
B, S, D = 8, 1024, 128
T = B * S
H, HD = 16, 8
TB = S // P
NT = T // P
GT = 4
GW = GT * P
NG = T // GW
HG = 4
NHG = H // HG
SPLIT_ROWS = 6 * HD
PAD_ROWS = 96
ALL_ROWS = PAD_ROWS + 3
Q_PARTS = (0, 1, 2, 0, 1, 0)
K_PARTS = (0, 0, 0, 1, 1, 2)
MASKED = -1.0e30
NE, FF = 8, 512
NOFF = 38
WINDOW = 256
WB = WINDOW // P + 1
FFN1 = 352
F_CHUNKS = ((0, 128), (128, 128), (256, 96))
LN_EPS, RMS_EPS = 1e-5, 1e-6
TINY = 1e-24 / D


class Count:

    def __init__(self, sem, per, credits=0):
        self.sem, self.per, self.credits, self.base, self.c = sem, per, credits, 0, 0

    def start(self, n):
        self.base, self.c = (n + self.credits) * self.per, 0

    def inc(self, ins, k=1):
        ins.then_inc(self.sem, k)
        self.c += k

    def wait(self, eng):
        eng.wait_ge(self.sem, self.base + self.c)

    def wait_apart(self, eng, divider):
        wait_apart(eng, divider, (self.sem, self.base + self.c))

    def end(self):
        assert self.c == self.per, (self.c, self.per)


class Phase:

    def __init__(self, nc, name):
        self.nc, self.name, self.ctx = nc, name, ExitStack()

    def __enter__(self):
        self.ctx.__enter__()
        return self

    def __exit__(self, *a):
        return self.ctx.__exit__(*a)

    def sb(self, name, shape, dt=F32):
        return self.ctx.enter_context(self.nc.sbuf_tensor(f"{self.name}_{name}", shape, dt))

    def ps(self, name, shape=(P, 512), dt=F32):
        return self.ctx.enter_context(self.nc.psum_tensor(f"{self.name}_{name}", list(shape), dt))

    def block(self):
        return self.ctx.enter_context(self.nc.Block())


def wait_apart(eng, divider, *waits):
    for sem, value in waits:
        eng.wait_ge(sem, value)
    eng.sem_inc(divider, 1)


def rows_of(dram, n):
    return dram[bass.ds(n * GW, GW), :].rearrange("(t p) c -> p t c", p=P)


def bc_rows(vec, width):
    return bass.AP(tensor=vec.tensor, offset=vec.offset, ap=[[0, P], [1, width]])


def emit_identity(nc, eng, ident, sem):
    eng.memset(ident[:, :], 0.0).then_inc(sem, 1)
    eng.wait_ge(sem, 1)
    eng.affine_select(out=ident[:, :], in_=ident[:, :], compare_op=ALU.not_equal, fill=1.0, base=0,
                      pattern=[[-1, P]], channel_multiplier=1).then_inc(sem, 1)


def emit_stats(nc, v, ch, x, st, mv, divider):
    for t in range(GT):
        ch.inc(nc.vector.bn_stats(st[:, t, :], x[:, t, :]))
    ch.wait_apart(v, divider)
    for t in range(GT):
        ch.inc(nc.vector.bn_aggr(mv[:, t, :], st[:, t, :]))


def emit_rstd(nc, g, ch, mv, rstd, power, divider, eps=LN_EPS, rms=None):
    ch.inc(nc.gpsimd.tensor_scalar(rstd[:, :], mv[:, :, 1], eps, None, ALU.add))
    ch.wait(g)
    ch.inc(nc.gpsimd.tensor_tensor(rstd[:, :], rstd[:, :], power[:, :], ALU.pow))
    if rms is not None:
        rms_eps, r = rms
        ch.wait(g)
        ch.inc(nc.gpsimd.tensor_tensor(r[:, :], mv[:, :, 1], rstd[:, :], ALU.mult))
        ch.wait(g)
        ch.inc(nc.gpsimd.tensor_tensor(r[:, :], r[:, :], rstd[:, :], ALU.mult))
        ch.wait_apart(g, divider)
        if rms_eps is None:
            ch.inc(nc.gpsimd.tensor_scalar(r[:, :], r[:, :], TINY, None, ALU.max))
        else:
            ch.inc(nc.gpsimd.tensor_scalar(r[:, :], r[:, :], rms_eps, None, ALU.add))
        ch.wait(g)
        ch.inc(nc.gpsimd.tensor_tensor(r[:, :], r[:, :], power[:, :], ALU.pow))


RSTD_STEPS, RMS_STEPS = 2, 6


def emit_apply(nc, ch, x, y, mv, rstd):
    for t in range(GT):
        ch.inc(nc.vector.tensor_scalar(y[:, t, :], x[:, t, :], mv[:, t, 0:1], rstd[:, t:t + 1],
                                       ALU.subtract, ALU.mult))


STATS_STEPS = 2 * GT


def qkv_phase(nc, sem, name, x_dram, w_qkv, q_scale, qd, kd, vd, norm_scale=None):
    rms = norm_scale is not None
    with Phase(nc, name) as ph:
        x_in = [ph.sb(f"x{s}", [P, GT, D]) for s in range(2)]
        xn = [ph.sb(f"xn{s}", [P, GT, D]) for s in range(2)]
        xr = [ph.sb(f"xr{s}", [P, GT, D]) for s in range(2)] if rms else xn
        xnT = [ph.sb(f"xnT{s}", [P, GW]) for s in range(2)]
        st = [ph.sb(f"st{s}", [P, GT, 6]) for s in range(2)]
        mv = [ph.sb(f"mv{s}", [P, GT, 2]) for s in range(2)]
        rstd = [ph.sb(f"rstd{s}", [P, GT]) for s in range(2)]
        rr = [ph.sb(f"rr{s}", [P, GT]) for s in range(2)]
        power = ph.sb("power", [P, GT])
        w = ph.sb("w", [P, 3 * D])
        ident = ph.sb("ident", [P, P])
        nscale = ph.sb("nscale", [P, 1])
        parts = [[[ph.sb(f"part{s}{a}{j}", [P, GW], BF16) for j in range(3)] for a in range(2)] for s in range(2)]
        rest = [[ph.sb(f"rest{s}{a}", [P, GW]) for a in range(2)] for s in range(2)]
        v_out = [ph.sb(f"v{s}", [P, GT, D]) for s in range(2)]
        ps_t = [ph.ps(f"pst{s}") for s in range(2)]
        ps_q = [[ph.ps(f"psq{s}{a}") for a in range(2)] for s in range(2)]
        ps_v = [ph.ps(f"psv{s}") for s in range(2)]

        setup, divider = sem("setup"), sem("divider")
        w_ready = sem("w_ready")
        w_scaled = sem("w_scaled")
        x_loaded = [sem(f"x_loaded{s}") for s in range(2)]
        norm_chain = sem("norm_chain")
        t_done = sem("t_done")
        xnT_ready = sem("xnT_ready")
        qk_done = sem("qk_done")
        v_done = sem("v_done")
        high_ready = sem("high_ready")
        v_copied = sem("v_copied")
        split_chain = sem("split_chain")
        parts_stored = [sem(f"parts_stored{s}") for s in range(2)]
        v_stored = [sem(f"v_stored{s}") for s in range(2)]
        n_consts = 32 if rms else 16
        NSTORE = 16 * 12
        KN = 2 * GT if rms else GT
        KR = RMS_STEPS if rms else RSTD_STEPS
        rstd_chain = sem("rstd_chain")
        stats_chain = sem("stats_chain")
        SPLIT_STEPS = 5

        block = ph.block()

        @block.gpsimd
        def _(g):
            emit_identity(nc, g, ident, setup)
            g.memset(power[:, :], -0.5).then_inc(setup, 1)
            g.wait_ge(setup, 3)
            rc = Count(rstd_chain, KR)
            with g.Fori(0, NG // 2) as i:
                for s in range(2):
                    n = 2 * i + s
                    wait_apart(g, divider, (stats_chain, (n + 1) * STATS_STEPS), (norm_chain, (n + 1) * KN))
                    rc.start(n)
                    emit_rstd(nc, g, rc, mv[s], rstd[s], power, divider, rms=(RMS_EPS, rr[s]) if rms else None)
                    rc.end()

        @block.sync
        def _(sp):
            sp.dma_start(w[:, :], w_qkv).then_inc(w_ready, 16)
            if rms:
                sp.dma_start(nscale[:, :], norm_scale.rearrange("(c a) -> c a", a=1)).then_inc(w_ready, 16)

            def load(i, s):
                n = 2 * i + s
                sp.wait_ge(norm_chain, (n + 1) * KN)
                sp.dma_start(x_in[s][:, :, :], rows_of(x_dram, n)).then_inc(x_loaded[s], 16)

            def store(i, s):
                n = 2 * i + s
                sp.wait_ge(split_chain, (n + 1) * SPLIT_STEPS)
                for a, (dst, which) in enumerate(((qd, Q_PARTS), (kd, K_PARTS))):
                    for blk, part in enumerate(which):
                        sp.dma_start(dst[:, blk * HD:(blk + 1) * HD, bass.ds(n * GW, GW)],
                                     parts[s][a][part][:, :]).then_inc(parts_stored[s], 16)

            load(0, 0)
            load(0, 1)
            with sp.Fori(0, NG // 2 - 1) as i:
                load(i + 1, 0)
                store(i, 0)
                load(i + 1, 1)
                store(i, 1)
            store(NG // 2 - 1, 0)
            store(NG // 2 - 1, 1)
            for s in range(2):
                sp.wait_ge(parts_stored[s], NSTORE * (NG // 2 + 1))

        @block.vector
        def _(v):
            v.sem_inc(norm_chain, 2 * KN)
            sc0 = Count(stats_chain, STATS_STEPS)
            ch = Count(norm_chain, KN, 2)
            sc = Count(split_chain, SPLIT_STEPS)
            v.wait_ge(w_ready, n_consts)
            nc.vector.tensor_scalar(w[:, 0:D], w[:, 0:D], q_scale, None, ALU.mult).then_inc(w_scaled, 1)

            def stats(i, s):
                sc0.start(2 * i + s)
                v.wait_ge(x_loaded[s], 16 * (i + 1))
                emit_stats(nc, v, sc0, x_in[s], st[s], mv[s], divider)
                sc0.end()

            def norm(i, s):
                n = 2 * i + s
                ch.start(n)
                v.wait_ge(rstd_chain, (n + 1) * KR)
                v.wait_ge(t_done, n + 1)
                emit_apply(nc, ch, x_in[s], xn[s], mv[s], rstd[s])
                if rms:
                    ch.wait(v)
                    for t in range(GT):
                        ins = nc.vector.tensor_scalar(xr[s][:, t, :], xn[s][:, t, :], rr[s][:, t:t + 1], None, ALU.mult)
                        ch.inc(ins)
                ch.end()

            def split(i, s):
                n = 2 * i + s
                sc.start(n)
                v.wait_ge(high_ready, 2 * n + 2)
                v.wait_ge(parts_stored[s], NSTORE * (i + 1))
                for a in range(2):
                    sc.inc(nc.vector.tensor_tensor(rest[s][a][:, :], ps_q[s][a][:, :], parts[s][a][0][:, :],
                                                   ALU.subtract))
                sc.wait(v)
                for a in range(2):
                    sc.inc(nc.vector.tensor_copy(parts[s][a][1][:, :], rest[s][a][:, :]))
                sc.wait(v)
                nc.vector.tensor_tensor(parts[s][0][2][:, :], rest[s][0][:, :], parts[s][0][1][:, :], ALU.subtract)
                sc.inc(nc.vector.tensor_tensor(parts[s][1][2][:, :], rest[s][1][:, :], parts[s][1][1][:, :],
                                               ALU.subtract))
                sc.end()

            stats(0, 0)
            norm(0, 0)
            stats(0, 1)
            with v.Fori(0, NG // 2 - 1) as i:
                norm(i, 1)
                stats(i + 1, 0)
                split(i, 0)
                norm(i + 1, 0)
                stats(i + 1, 1)
                split(i, 1)
            norm(NG // 2 - 1, 1)
            split(NG // 2 - 1, 0)
            split(NG // 2 - 1, 1)

        @block.scalar
        def _(a_):
            a_.wait_ge(w_ready, n_consts)

            a_.sem_inc(xnT_ready, 2)
            a_.sem_inc(v_copied, 2)

            with a_.Fori(0, NG // 2) as i:
                for s in range(2):
                    n = 2 * i + s
                    a_.wait_ge(t_done, n + 3)
                    a_.wait_ge(v_done, n + 1)
                    if rms:
                        nc.scalar.activation(xnT[s][:, :], ps_t[s][:, :], ACT.Copy, scale=nscale[:, 0:1])\
                            .then_inc(xnT_ready, 1)
                    else:
                        nc.scalar.activation(xnT[s][:, :], ps_t[s][:, :], ACT.Copy).then_inc(xnT_ready, 1)
                    a_.wait_ge(parts_stored[s], NSTORE * (i + 1))
                    for a in range(2):
                        a_.wait_ge(qk_done, 2 * n + a + 1)
                        nc.scalar.activation(parts[s][a][0][:, :], ps_q[s][a][:, :], ACT.Copy).then_inc(high_ready, 1)
                    a_.wait_ge(v_done, n + 3)
                    a_.wait_ge(v_stored[s], 16 * (i + 1))
                    nc.scalar.activation(v_out[s][:, :, :], ps_v[s][:, :].rearrange("p (t c) -> p t c", t=GT),
                                         ACT.Copy).then_inc(v_copied, 1)
                    a_.wait_ge(v_copied, n + 3)
                    a_.dma_start(rows_of(vd, n), v_out[s][:, :, :]).then_inc(v_stored[s], 16)
            for s in range(2):
                a_.wait_ge(v_stored[s], 16 * (NG // 2 + 1))

        @block.tensor
        def _(t_):
            t_.sem_inc(t_done, 2)
            t_.sem_inc(v_done, 2)
            for s in range(2):
                t_.sem_inc(v_stored[s], 16)
                t_.sem_inc(parts_stored[s], NSTORE)
            t_.wait_ge(setup, 2)
            t_.wait_ge(w_scaled, 1)

            def transposes(n, s):
                t_.wait_ge(norm_chain, (n + 3) * KN)
                t_.wait_ge(xnT_ready, n + 1)
                for t in range(GT):
                    last = nc.tensor.transpose(ps_t[s][:, t * P:(t + 1) * P], xr[s][:, t, :], ident[:, :])
                last.then_inc(t_done, 1)

            def products(n, s, i):
                t_.wait_ge(xnT_ready, n + 3)
                t_.wait_ge(parts_stored[s], NSTORE * (i + 1))
                for a in range(2):
                    nc.tensor.matmul(ps_q[s][a][:, :], w[:, a * D:(a + 1) * D], xnT[s][:, :], start=True, stop=True)\
                        .then_inc(qk_done, 1)
                t_.wait_ge(v_copied, n + 1)
                for t in range(GT):
                    last = nc.tensor.matmul(ps_v[s][:, t * D:(t + 1) * D], xnT[s][:, t * P:(t + 1) * P],
                                            w[:, 2 * D:3 * D], start=True, stop=True)
                last.then_inc(v_done, 1)

            transposes(0, 0)
            with t_.Fori(0, NG // 2 - 1) as i:
                transposes(2 * i + 1, 1)
                products(2 * i, 0, i)
                transposes(2 * i + 2, 0)
                products(2 * i + 1, 1, i)
            transposes(NG - 1, 1)
            products(NG - 2, 0, NG // 2 - 1)
            products(NG - 1, 1, NG // 2 - 1)


class Attention:

    def __init__(self, causal):
        self.causal = causal
        self.tiles = []
        for qb in range(TB):
            if not causal:
                k0 = max(0, qb - WB + 1)
                self.tiles += [(h, qb, k0 * P, (qb + 1 - k0) * P, True) for h in range(HG)]
            elif qb < 4:
                self.tiles += [(h, qb, 0, (qb + 1) * P, True) for h in range(HG)]
            else:
                self.tiles += [(h, qb, 0, 4 * P, False) for h in range(HG)]
                self.tiles += [(h, qb, 4 * P, (qb - 3) * P, True) for h in range(HG)]
        self.slots = []
        if causal:
            for half in range(2):
                for kb in range(4 * half + 4):
                    q0 = max(512 * half, P * kb)
                    for pair in range(2):
                        self.slots.append((kb, pair, q0, 512 * (half + 1) - q0))
        else:
            for kb in range(TB):
                q0 = kb * P
                for pair in range(2):
                    self.slots.append((kb, pair, q0, min(WB * P, S - q0)))
        self.masked = [k for k, (kb, _, q0, _) in enumerate(self.slots) if causal and q0 == kb * P]
        self.bank_end = [max(k for k, sl in enumerate(self.slots) if self.banks(sl)[b]) for b in range(2)]
        self.bank_start = [min(k for k, sl in enumerate(self.slots) if self.banks(sl)[b]) for b in range(2)]
        self.n_tiles, self.n_slots = len(self.tiles), len(self.slots)
        assert self.n_tiles % 2 == 0 and self.n_slots % 4 == 0
        total = sum(t[3] for t in self.tiles)
        last = self.n_slots - (6 if causal else 4)
        self.last = last
        self.with_slot = [[] for _ in range(self.n_slots)]
        done = 0
        for j, t in enumerate(self.tiles):
            self.with_slot[min(last, done * (last + 1) // total)].append(j)
            done += t[3]

    @staticmethod
    def banks(slot):
        _, _, q0, n = slot
        out = []
        for b in range(2):
            lo, hi = max(q0, 512 * b), min(q0 + n, 512 * (b + 1))
            out.append((lo, hi) if lo < hi else None)
        return out


TABLE_PARTS = tuple((src, half) for src in range(2) for half in range(2))
PV_LAG = 3
P_BUFS = 4


def attention_phase(nc, sem, name, qd, kd, vd, att_dram, causal, bias_k=None, bias_q=None):
    plan = Attention(causal)
    NTL, NSL = plan.n_tiles, plan.n_slots
    TILES = NTL + 2
    NMASK = len(plan.masked)
    NGR = B * NHG
    ML = 4
    with Phase(nc, name) as ph:
        Q = [ph.sb(f"Q{g}", [P, HG, S], BF16) for g in range(NHG)]
        K = [ph.sb(f"K{g}", [P, HG, S], BF16) for g in range(NHG)]
        v_in = ph.sb("v", [P, TB, D])
        V = [ph.sb(f"V{s}", [P, TB, HG, 32]) for s in range(2)]
        probs = [ph.sb(f"probs{s}", [P, 2, 512]) for s in range(P_BUFS)]
        O = [ph.sb(f"O{b}", [P, 512]) for b in range(2)]
        att = ph.sb("att", [P, TB, D])
        rec = [ph.sb(f"rec{b}", [P, GT, HG, 1]) for b in range(2)]
        part_max = ph.sb("part_max", [P, HG])
        mx = ph.sb("mx", [P, HG, TB])
        mrest = ph.sb("mrest", [P, HG * TB])
        mparts = ph.sb("mparts", [P, 3, HG * TB], BF16)
        mT = ph.sb("mT", [3 * HG * TB, P], BF16)
        ident = ph.sb("ident", [P, P])
        identb = ph.sb("identb", [P, P], BF16)
        if causal:
            mask = ph.sb("mask", [P, 512])
        else:
            tab_k = ph.sb("tab_k", [P, H, WB * P])
            tab_q = ph.sb("tab_q", [P, H, WB * P])
            raw = [ph.sb(f"raw{s}", [P, H // 2, WB * P]) for s in range(2)]
            raw_loaded = [sem(f"raw_loaded{s}") for s in range(2)]
        ps1 = [ph.ps(f"ps1{s}") for s in range(2)]
        ps2 = [ph.ps(f"ps2{s}", [P, 2, 512]) for s in range(2)]
        psO = [ph.ps(f"psO{b}") for b in range(2)]
        psT = ps1[0][:, 0:P // 2].bitcast(BF16)

        setup, divider = sem("setup"), sem("divider")
        pads = sem("pads")
        identb_ready = sem("identb_ready")
        tabs = sem("tabs")
        qk_loaded = [sem(f"qk_loaded{g}") for g in range(NHG)]
        v_loaded = sem("v_loaded")
        v_spread = sem("v_spread")
        t1_done = sem("t1_done")
        t1_read = sem("t1_read")
        m_chain = sem("m_chain")
        m_sent = [sem(f"m_sent{g}") for g in range(NHG)]
        s2_done = sem("s2_done")
        s2_read = sem("s2_read")
        exp_done = sem("exp_done")
        masked = sem("masked")
        pv_done = sem("pv_done")
        o_copied = sem("o_copied")
        oT_done = sem("oT_done")
        o_chain = sem("o_chain")
        att_stored = sem("att_stored")
        NSET = 4
        block = ph.block()

        @block.sync
        def _(sp):
            sp.sem_inc(att_stored, 16)
            sp.wait_ge(setup, NSET)
            sp.wait_ge(pads, 1)
            if not causal:
                for i, (src, half) in enumerate(TABLE_PARTS):
                    if i >= 2:
                        sp.wait_ge(tabs, i - 1)
                    sp.dma_start(raw[half][:, :, :], shifted_rows((bias_k, bias_q)[src], half * H // 2, H // 2))\
                        .then_inc(raw_loaded[half], 16)

            def load(n, b, g):
                sp.wait_ge(pv_done, NSL * (n + 1))
                for dst, src in ((Q[g], qd), (K[g], kd)):
                    sp.dma_start(dst[0:SPLIT_ROWS, :, :],
                                 src[g * HG:(g + 1) * HG, :, bass.ds(b * S, S)].rearrange("h r t -> r h t"))\
                        .then_inc(qk_loaded[g], 16)

            def load_v(b):
                sp.wait_ge(v_spread, NHG * (b + 1))
                sp.dma_start(v_in[:, :, :], vd[bass.ds(b * S, S), :].rearrange("(t p) c -> p t c", p=P))\
                    .then_inc(v_loaded, 16)

            def store(b):
                sp.wait_ge(o_chain, 4 * (NHG * b + NHG) + 4)
                sp.dma_start(att_dram[bass.ds(b * S, S), :].rearrange("(t p) c -> p t c", p=P), att[:, :, :])\
                    .then_inc(att_stored, 16)

            def body(b, first=False, last=False):
                for g in range(NHG):
                    n = NHG * b + g
                    sp.wait_ge(t1_read, (n + 1) * TILES + 2)
                    for part in range(3):
                        sp.dma_start(Q[g][PAD_ROWS + part:PAD_ROWS + part + 1, :, :].rearrange("r h t -> r (h t)"),
                                     mT[part * HG * TB:(part + 1) * HG * TB, :]).then_inc(m_sent[g], 16)
                    if g == NHG - 1 and not last:
                        load_v(b + 1)
                    if not (last and g >= 1):
                        load(n + 3, b + (g + 3) // NHG, (g + 3) % NHG)
                    if g == 0 and not first:
                        store(b - 1)

            load(0, 0, 0)
            load_v(0)
            load(1, 0, 1)
            load(2, 0, 2)
            body(0, first=True)
            with sp.Fori(1, B - 1) as b:
                body(b)
            body(B - 1, last=True)
            store(B - 1)
            sp.wait_ge(att_stored, 16 * (B + 1))

        @block.gpsimd
        def _(g_):
            g_.sem_inc(v_spread, NHG)
            emit_identity(nc, g_, ident, setup)
            g_.memset(V[0][:, :, :, :], 0.0)
            g_.memset(V[1][:, :, :, :], 0.0).then_inc(setup, 1)
            g_.wait_ge(setup, 3)
            g_.memset(V[0][:, :, :, HD:HD + 1], 1.0)
            g_.memset(V[1][:, :, :, HD:HD + 1], 1.0).then_inc(setup, 1)
            if causal:
                g_.memset(mask[:, :], 0.0).then_inc(tabs, 1)
                g_.wait_ge(tabs, 1)
                g_.affine_select(out=mask[:, 512 - P:512], in_=mask[:, 512 - P:512], compare_op=ALU.is_ge,
                                 fill=MASKED, base=0, pattern=[[-1, P]], channel_multiplier=1).then_inc(tabs, 1)
            with g_.Fori(0, B) as b:
                g_.wait_ge(v_loaded, 16 * (b + 1))
                for g in range(NHG):
                    n = NHG * b + g
                    wait_apart(g_, divider, (pv_done, NSL * (n + 3)))
                    nc.gpsimd.tensor_copy(V[g % 2][:, :, :, 0:HD],
                                          v_in[:, :, g * HG * HD:(g + 1) * HG * HD]
                                          .rearrange("p t (h d) -> p t h d", d=HD)).then_inc(v_spread, 1)
                    for k in plan.masked:
                        wait_apart(g_, divider, (exp_done, n * NSL + k + 3))
                        pt = probs[k % P_BUFS]
                        nc.gpsimd.affine_select(out=pt[:, :, 0:P], in_=pt[:, :, 0:P], compare_op=ALU.is_ge,
                                                fill=0.0, base=0, pattern=[[0, 2], [1, P]],
                                                channel_multiplier=-1).then_inc(masked, 1)

        @block.scalar
        def _(a_):
            a_.sem_inc(exp_done, 2)
            if not causal:
                for i, (src, half) in enumerate(TABLE_PARTS):
                    a_.wait_ge(raw_loaded[half], 16 * (i // 2 + 1))
                    nc.scalar.activation((tab_k, tab_q)[src][:, half * H // 2:(half + 1) * H // 2, :],
                                         backwards(raw[half], H // 2), ACT.Copy).then_inc(tabs, 1)

            def copy_o(n, bank):
                a_.wait_ge(pv_done, NSL * (n + 4) + plan.bank_end[bank] + 1)
                a_.wait_ge(oT_done, 2 * n + bank + 1)
                nc.scalar.activation(O[bank][:, :], psO[bank][:, :], ACT.Copy).then_inc(o_copied, 1)

            def group(n, first=False):
                for k, (kb, pair, q0, w) in enumerate(plan.slots):
                    if causal:
                        a_.wait_ge(s2_done, n * NSL + k + 1)
                    else:
                        a_.wait_ge(s2_read, n * NSL + k + 3)
                    a_.wait_ge(pv_done, NSL * (n + 4) + k - P_BUFS + 1)
                    pt = probs[k % P_BUFS]
                    src = ps2[k % 2] if causal else pt
                    nc.scalar.activation(pt[:, :, 0:w], src[:, :, 0:w], ACT.Exp).then_inc(exp_done, 1)
                    if k == 3 and not first:
                        copy_o(n - 1, 1)
                    if k == plan.bank_end[0] + PV_LAG + 1:
                        copy_o(n, 0)

            group(0, first=True)
            with a_.Fori(0, B - 1) as b:
                for g in range(1, NHG + 1):
                    group(NHG * b + g)
            for g in range(1, NHG):
                group(NHG * (B - 1) + g)
            copy_o(NGR - 1, 1)

        @block.vector
        def _(v):
            v.sem_inc(t1_read, 2)
            v.sem_inc(s2_read, 2)
            v.sem_inc(o_chain, 4)
            for g in range(NHG):
                for part in (slice(32, 64), slice(64, 96)):
                    nc.vector.memset(Q[g][part, :, :], 0.0)
                    nc.vector.memset(K[g][part, :, :], 0.0)
                last = nc.vector.memset(K[g][PAD_ROWS:P, :, :], 1.0)
            last.then_inc(pads, 1)
            v.wait_ge(setup, NSET)
            nc.vector.tensor_copy(identb[:, :], ident[:, :]).then_inc(identb_ready, 1)
            v.wait_ge(tabs, 2 if causal else len(TABLE_PARTS))
            mc = Count(m_chain, ML)

            def tile(n, g, j):
                h, qb, k0, w, with_mask = plan.tiles[j]
                wait_apart(v, divider, (t1_done, n * TILES + j + 1))
                src = ps1[j % 2]
                if not with_mask:
                    nc.vector.tensor_reduce(part_max[:, h:h + 1], src[:, 0:w], AX.X, ALU.max).then_inc(t1_read, 1)
                    return
                start = part_max[:, h:h + 1] if causal and k0 else 3 * MASKED
                table = mask[:, 512 - w:512] if causal else tab_q[:, g * HG + h, WB * P - w:WB * P]
                nc.vector.tensor_tensor_reduce(out=src[:, 0:w], in0=src[:, 0:w], in1=table, scale=1.0, scalar=start,
                                               op0=ALU.add, op1=ALU.max, accum_out=mx[:, h, qb:qb + 1])\
                    .then_inc(t1_read, 1)

            def maxima(n):
                mc.start(n)
                v.wait_ge(t1_read, n * TILES + NTL + 2)
                m2 = mx[:, :, :].rearrange("p h t -> p (h t)")
                mc.inc(nc.vector.tensor_scalar(mparts[:, 0, :], m2, -1.0, None, ALU.mult))
                mc.wait(v)
                mc.inc(nc.vector.scalar_tensor_tensor(out=mrest[:, :], in0=m2, scalar=-1.0, in1=mparts[:, 0, :],
                                                      op0=ALU.mult, op1=ALU.subtract))
                mc.wait(v)
                mc.inc(nc.vector.tensor_copy(mparts[:, 1, :], mrest[:, :]))
                mc.wait(v)
                mc.inc(nc.vector.tensor_tensor(mparts[:, 2, :], mrest[:, :], mparts[:, 1, :], ALU.subtract))
                mc.end()

            def copy_maxima(n, b, g):
                v.wait_ge(t1_done, n * TILES + NTL + 2)
                if g > 0:
                    v.wait_ge(m_sent[g - 1], 48 * (b + 1))
                elif not (isinstance(b, int) and b == 0):
                    v.wait_ge(m_sent[NHG - 1], 48 * b)
                nc.vector.tensor_copy(mT[:, :], psT[0:3 * HG * TB, :]).then_inc(t1_read, 2)

            def add_bias(n, g, k):
                kb, pair, q0, w = plan.slots[k]
                v.wait_ge(s2_done, n * NSL + k + 1)
                v.wait_ge(pv_done, NSL * (n + 4) + k - P_BUFS + 1)
                h = g * HG + 2 * pair
                nc.vector.tensor_tensor(probs[k % P_BUFS][:, :, 0:w], ps2[k % 2][:, :, 0:w], tab_k[:, h:h + 2, 0:w],
                                        ALU.add).then_inc(s2_read, 1)

            def norm(n, b, g, bank):
                v.wait_ge(oT_done, 2 * n + bank + 3)
                if g == 0 and bank == 0:
                    v.wait_ge(att_stored, 16 * (b + 1))
                src = psO[bank][:, :].rearrange("p (t h e) -> p t h e", t=GT, h=HG)
                nc.vector.reciprocal(rec[bank][:, :, :, :], src[:, :, :, HD:HD + 1]).then_inc(o_chain, 1)
                v.wait_ge(o_chain, 4 * (n + 1) + 2 * bank + 1)
                nc.vector.tensor_tensor(att[:, GT * bank:GT * (bank + 1), g * HG * HD:(g + 1) * HG * HD]
                                        .rearrange("p t (h d) -> p t h d", d=HD),
                                        src[:, :, :, 0:HD], rec[bank][:, :, :, :].to_broadcast([P, GT, HG, HD]),
                                        ALU.mult).then_inc(o_chain, 1)

            def group(n, b, g, nxt, prev):
                for k in range(NSL):
                    if not causal:
                        add_bias(n, g, k)
                    if nxt and k == plan.last + 1:
                        copy_maxima(*nxt)
                    if nxt:
                        for j in plan.with_slot[k]:
                            tile(nxt[0], nxt[2], j)
                        if k == plan.last:
                            maxima(nxt[0])
                    if prev and k == 5:
                        norm(*prev, 1)
                    if k == plan.bank_end[0] + PV_LAG + 4:
                        norm(n, b, g, 0)

            walk(plan, B, group, before=lambda: (
                [tile(0, 0, j) for j in range(NTL)], maxima(0), copy_maxima(0, 0, 0)), after=lambda: norm(
                NGR - 1, B - 1, NHG - 1, 1), fori=v.Fori)

        @block.tensor
        def _(t_):
            t_.sem_inc(pv_done, 4 * NSL)
            t_.sem_inc(oT_done, 2)
            t_.wait_ge(setup, NSET)
            t_.wait_ge(identb_ready, 1)

            def tile(n, b, g, j):
                h, qb, k0, w, _ = plan.tiles[j]
                if j == 0:
                    t_.wait_ge(qk_loaded[g], 32 * (b + 1))
                t_.wait_ge(t1_read, n * TILES + j + 1)
                nc.tensor.matmul(ps1[j % 2][:, 0:w], Q[g][0:PAD_ROWS, h, qb * P:(qb + 1) * P],
                                 K[g][0:PAD_ROWS, h, k0:k0 + w], start=True, stop=True).then_inc(t1_done, 1)

            def turn_maxima(n):
                t_.wait_ge(m_chain, ML * (n + 1))
                t_.wait_ge(t1_read, n * TILES + NTL + 1)
                nc.tensor.transpose(psT[0:3 * HG * TB, :], mparts[:, :, :].rearrange("p a b -> p (a b)"),
                                    identb[:, :]).then_inc(t1_done, 2)

            def slot(n, b, g, k):
                kb, pair, q0, w = plan.slots[k]
                if k == 0:
                    t_.wait_ge(m_sent[g], 48 * (b + 1))
                t_.wait_ge(exp_done if causal else s2_read, n * NSL + k + 1)
                for hh in range(2):
                    h = 2 * pair + hh
                    last = nc.tensor.matmul(ps2[k % 2][:, hh, 0:w], K[g][0:ALL_ROWS, h, kb * P:(kb + 1) * P],
                                            Q[g][0:ALL_ROWS, h, q0:q0 + w], start=True, stop=True)
                last.then_inc(s2_done, 1)

            def values(n, g, k):
                kb, pair, q0, w = plan.slots[k]
                if k in plan.masked:
                    t_.wait_ge(masked, n * NMASK + plan.masked.index(k) + 1)
                else:
                    t_.wait_ge(exp_done, n * NSL + k + 3)
                if k == 0:
                    t_.wait_ge(v_spread, n + NHG + 1)
                for bank in range(2):
                    if k == plan.bank_start[bank]:
                        t_.wait_ge(o_chain, 4 * n + 2 * (bank + 1))
                for bank, part in enumerate(plan.banks(plan.slots[k])):
                    if part is None:
                        continue
                    for hh in range(2):
                        h = 2 * pair + hh
                        last = nc.tensor.matmul(psO[bank][32 * h:32 * h + 32, part[0] - 512 * bank:part[1] - 512 * bank],
                                                V[g % 2][:, kb, h, :], probs[k % P_BUFS][:, hh, part[0] - q0:part[1] - q0],
                                                start=(k - pair == plan.bank_start[bank]),
                                                stop=(k - pair == plan.bank_end[bank] - 1), skip_group_check=True)
                last.then_inc(pv_done, 1)

            def turn_outputs(n, bank):
                t_.wait_ge(o_copied, 2 * n + bank + 1)
                for t in range(GT):
                    last = nc.tensor.transpose(psO[bank][:, t * P:(t + 1) * P], O[bank][:, t * P:(t + 1) * P],
                                               ident[:, :])
                last.then_inc(oT_done, 1)

            def group(n, b, g, nxt, prev):
                for k in range(NSL):
                    slot(n, b, g, k)
                    if k < PV_LAG:
                        if prev:
                            values(prev[0], prev[2], NSL - PV_LAG + k)
                    else:
                        values(n, g, k - PV_LAG)
                    if prev and k == PV_LAG + 1:
                        turn_outputs(prev[0], 1)
                    if k == plan.bank_end[0] + PV_LAG + 3:
                        turn_outputs(n, 0)
                    if nxt and k == plan.last + 1:
                        turn_maxima(nxt[0])
                    if nxt:
                        for j in plan.with_slot[k]:
                            tile(nxt[0], nxt[1], nxt[2], j)

            def finish():
                for k in range(NSL - PV_LAG, NSL):
                    values(NGR - 1, NHG - 1, k)
                turn_outputs(NGR - 1, 1)

            walk(plan, B, group, before=lambda: ([tile(0, 0, 0, j) for j in range(NTL)], turn_maxima(0)),
                 after=finish, fori=t_.Fori)


def walk(plan, n_seq, group, before, after, fori):
    def at(b, g):
        if g < 0:
            return (NHG * b + g, b - 1, NHG + g)
        return (NHG * b + g, b + g // NHG, g % NHG)

    before()
    group(*at(0, 0), at(0, 1), None)
    with fori(0, n_seq - 1) as b:
        for g in range(1, NHG + 1):
            group(*at(b, g), at(b, g + 1), at(b, g - 1))
    for g in range(1, NHG):
        group(*at(n_seq - 1, g), at(n_seq - 1, g + 1) if g < NHG - 1 else None, at(n_seq - 1, g - 1))
    after()


def skewed(fori, count, stages):
    most = max(lag for _, lag in stages)
    first = most + most % 2

    def step(half, r, fixed):
        for fn, lag in stages:
            s = (r - lag) % 2
            n = 2 * (half + (r - lag - s) // 2) + s
            if not fixed or 0 <= n < count:
                fn(n, s)

    for j in range(first):
        step(j // 2, j % 2, True)
    with fori(first // 2, count // 2) as i:
        for r in range(2):
            step(i, r, False)
    for j in range(count, count + most):
        step(j // 2, j % 2, True)


def uses(n, s):
    return (n - s) // 2 + 1 if isinstance(n, int) else (n + (2 - s)) // 2


def mix_phase(nc, sem, x_dram, att_dram, w_out, gate_w, x1_dram, xn_dram, onehot_all, weight_all):
    with Phase(nc, "mix") as ph:
        def two(name, shape, dt=F32):
            return [ph.sb(f"{name}{s}", shape, dt) for s in range(2)]
        x_in, a_in = two("x", [P, GT, D]), two("a", [P, GT, D])
        aT, x1, xn, xnT = two("aT", [P, GW]), two("x1", [P, GT, D]), two("xn", [P, GT, D]), two("xnT", [P, GW])
        st, mv, rstd = two("st", [P, GT, 6]), two("mv", [P, GT, 2]), two("rstd", [P, GT])
        top, diff, ex = two("top", [P, GT, 1]), two("diff", [P, GT, NE]), two("ex", [P, GT, NE])
        tot, pick, best = two("tot", [P, GT, 1]), two("pick", [P, GT, NE]), two("best", [P, GT, 1])
        wo, gw = ph.sb("wo", [P, D]), ph.sb("gw", [P, NE])
        ident, power = ph.sb("ident", [P, P]), ph.sb("power", [P, GT])
        order_i, order = ph.sb("order_i", [P, GT, NE], I32), ph.sb("order", [P, GT, NE])
        psA, psO, psT, psR = [[ph.ps(f"{k}{s}") for s in range(2)] for k in "AOTR"]

        setup, weights = sem("setup"), sem("weights")
        divider = sem("divider")
        in_loaded = [sem(f"in_loaded{s}") for s in range(2)]
        aT_done, aT_copied, out_done = sem("aT_done"), sem("aT_copied"), sem("out_done")
        norm_chain, rstd_chain, apply_done = sem("norm_chain"), sem("rstd_chain"), sem("apply_done")
        xT_done, xT_copied, logits_done = sem("xT_done"), sem("xT_copied"), sem("logits_done")
        diff_chain, ex_done, pick_chain = sem("diff_chain"), sem("ex_done"), sem("pick_chain")
        stored = [sem(f"stored{s}") for s in range(2)]
        NST = 1 + STATS_STEPS
        NPICK = 5
        block = ph.block()

        @block.sync
        def _(sp):
            for s in range(2):
                sp.sem_inc(stored[s], 32)
            sp.dma_start(wo[:, :], w_out).then_inc(weights, 16)
            sp.dma_start(gw[:, :], gate_w).then_inc(weights, 16)

            def load(n, s):
                sp.wait_ge(norm_chain, (n + 1) * NST)
                sp.wait_ge(aT_done, n + 1)
                sp.dma_start(x_in[s][:, :, :], rows_of(x_dram, n)).then_inc(in_loaded[s], 16)
                sp.dma_start(a_in[s][:, :, :], rows_of(att_dram, n)).then_inc(in_loaded[s], 16)

            def store(n, s):
                sp.wait_ge(apply_done, n + 3)
                sp.dma_start(rows_of(x1_dram, n), x1[s][:, :, :]).then_inc(stored[s], 16)
                sp.dma_start(rows_of(xn_dram, n), xn[s][:, :, :]).then_inc(stored[s], 16)

            skewed(sp.Fori, NG, [(store, 2), (load, 0)])
            for s in range(2):
                sp.wait_ge(stored[s], 32 * (NG // 2 + 1))

        @block.gpsimd
        def _(g):
            emit_identity(nc, g, ident, setup)
            g.memset(power[:, :], -0.5).then_inc(setup, 1)
            g.iota(order_i[:, :, :], pattern=[[0, GT], [-1, NE]], base=NE, channel_multiplier=0).then_inc(setup, 1)
            g.wait_ge(setup, 4)
            g.tensor_copy(order[:, :, :], order_i[:, :, :]).then_inc(setup, 1)
            rc = Count(rstd_chain, RSTD_STEPS)

            def rstds(n, s):
                wait_apart(g, divider, (norm_chain, (n + 3) * NST), (apply_done, n + 1))
                rc.start(n)
                emit_rstd(nc, g, rc, mv[s], rstd[s], power, divider)
                rc.end()

            skewed(g.Fori, NG, [(rstds, 2)])

        @block.scalar
        def _(a_):
            def copy_a(n, s):
                a_.wait_ge(aT_done, n + 3)
                a_.wait_ge(out_done, n + 1)
                nc.scalar.activation(aT[s][:, :], psA[s][:, :], ACT.Copy).then_inc(aT_copied, 1)

            def copy_x(n, s):
                a_.wait_ge(xT_done, n + 3)
                a_.wait_ge(logits_done, n + 1)
                nc.scalar.activation(xnT[s][:, :], psT[s][:, :], ACT.Copy).then_inc(xT_copied, 1)

            def exps(n, s):
                a_.wait_ge(diff_chain, 2 * (n + 1))
                a_.wait_ge(pick_chain, NPICK * (n + 1))
                nc.scalar.activation(ex[s][:, :, :], diff[s][:, :, :], ACT.Exp).then_inc(ex_done, 1)

            skewed(a_.Fori, NG, [(exps, 4), (copy_x, 3), (copy_a, 1)])

        @block.vector
        def _(v):
            v.sem_inc(norm_chain, 2 * NST)
            v.sem_inc(apply_done, 2)
            v.sem_inc(pick_chain, 2 * NPICK)
            ch = Count(norm_chain, NST, 2)
            dc = Count(diff_chain, 2)
            pc = Count(pick_chain, NPICK, 2)
            v.wait_ge(setup, 5)

            def residual(n, s):
                ch.start(n)
                v.wait_ge(in_loaded[s], 32 * uses(n, s))
                v.wait_ge(out_done, n + 3)
                v.wait_ge(stored[s], 32 * uses(n, s))
                ch.inc(nc.vector.tensor_tensor(x1[s][:, :, :], x_in[s][:, :, :],
                                               psO[s][:, :].rearrange("p (t c) -> p t c", t=GT), ALU.add))
                ch.wait(v)
                emit_stats(nc, v, ch, x1[s], st[s], mv[s], divider)
                ch.end()
                v.wait_ge(rstd_chain, RSTD_STEPS * (n + 1))
                v.wait_ge(xT_done, n + 1)
                for t in range(GT):
                    last = nc.vector.tensor_scalar(xn[s][:, t, :], x1[s][:, t, :], mv[s][:, t, 0:1],
                                                   rstd[s][:, t:t + 1], ALU.subtract, ALU.mult)
                last.then_inc(apply_done, 1)

            def logits(n, s):
                lg = psR[s][:, 0:GT * NE].rearrange("p (t e) -> p t e", t=GT)
                dc.start(n)
                v.wait_ge(logits_done, n + 3)
                v.wait_ge(ex_done, n - 1) if isinstance(n, int) and n >= 2 else None
                dc.inc(nc.vector.tensor_reduce(top[s][:, :, 0], lg, AX.X, ALU.max))
                dc.wait(v)
                dc.inc(nc.vector.tensor_tensor(diff[s][:, :, :], lg, top[s][:, :, :].to_broadcast([P, GT, NE]),
                                               ALU.subtract))
                dc.end()

            def choose(n, s):
                pc.start(n)
                v.wait_ge(ex_done, n + 1)
                pc.inc(nc.vector.tensor_reduce(tot[s][:, :, 0], ex[s][:, :, :], AX.X, ALU.add))
                pc.inc(nc.vector.scalar_tensor_tensor(out=pick[s][:, :, :], in0=diff[s][:, :, :], scalar=0.0,
                                                      in1=order[:, :, :], op0=ALU.is_ge, op1=ALU.mult))
                pc.wait(v)
                pc.inc(nc.vector.reciprocal(weight_all[:, bass.ds(n * GT, GT)], tot[s][:, :, 0]))
                pc.inc(nc.vector.tensor_reduce(best[s][:, :, 0], pick[s][:, :, :], AX.X, ALU.max))
                pc.wait(v)
                pc.inc(nc.vector.tensor_tensor(onehot_all[:, bass.ds(n * GT, GT), :], pick[s][:, :, :],
                                               best[s][:, :, :].to_broadcast([P, GT, NE]), ALU.is_equal))
                pc.end()

            skewed(v.Fori, NG, [(choose, 5), (logits, 4), (residual, 2)])

        @block.tensor
        def _(t_):
            for q in (aT_done, out_done, xT_done, logits_done):
                t_.sem_inc(q, 2)
            t_.wait_ge(setup, 2)
            t_.wait_ge(weights, 32)

            def turn_a(n, s):
                t_.wait_ge(in_loaded[s], 32 * uses(n, s))
                for t in range(GT):
                    last = nc.tensor.transpose(psA[s][:, t * P:(t + 1) * P], a_in[s][:, t, :], ident[:, :])
                last.then_inc(aT_done, 1)

            def out(n, s):
                t_.wait_ge(aT_copied, n + 1)
                t_.wait_ge(norm_chain, NST * (n + 1))
                for t in range(GT):
                    last = nc.tensor.matmul(psO[s][:, t * D:(t + 1) * D], aT[s][:, t * P:(t + 1) * P], wo[:, :],
                                            start=True, stop=True)
                last.then_inc(out_done, 1)

            def turn_x(n, s):
                t_.wait_ge(apply_done, n + 3)
                for t in range(GT):
                    last = nc.tensor.transpose(psT[s][:, t * P:(t + 1) * P], xn[s][:, t, :], ident[:, :])
                last.then_inc(xT_done, 1)

            def route(n, s):
                t_.wait_ge(xT_copied, n + 1)
                t_.wait_ge(pick_chain, NPICK * (n + 1))
                for t in range(GT):
                    last = nc.tensor.matmul(psR[s][:, t * NE:(t + 1) * NE], xnT[s][:, t * P:(t + 1) * P], gw[:, :],
                                            start=True, stop=True)
                last.then_inc(logits_done, 1)

            skewed(t_.Fori, NG, [(route, 4), (turn_x, 3), (out, 2), (turn_a, 1)])


SORTED_TILES = (T + NE * (P - 1)) // P + 1
SORTED_TILES += SORTED_TILES % 2


def place_phase(nc, sem, onehot_all, place_all, expert_row):
    with Phase(nc, "place") as ph:
        before = ph.sb("before", [P, P])
        ones = ph.sb("ones", [P, P])
        rank = ph.sb("rank", [P, NT, NE])
        total = ph.sb("total", [P, NE * NT])
        cum = ph.sb("cum", [P, NE * NT])
        excl = ph.sb("excl", [P, NE * NT])
        zeros = ph.sb("zeros", [P, NE * NT])
        marks_i, marks = ph.sb("marks_i", [P, NT], I32), ph.sb("marks", [P, NT])
        tiles_i, tiles = ph.sb("tiles_i", [P, SORTED_TILES], I32), ph.sb("tiles", [P, SORTED_TILES])
        count = ph.sb("count", [P, NE, 1])
        over = ph.sb("over", [P, NE, NT])
        blocks, end = ph.sb("blocks", [P, NE]), ph.sb("end", [P, NE])
        adj = ph.sb("adj", [P, NE, 1])
        past = ph.sb("past", [P, SORTED_TILES, NE])
        which = ph.sb("which", [P, SORTED_TILES])
        spot = ph.sb("spot", [P, NT])
        ps_rank, ps_total = ph.ps("ps_rank"), ph.ps("ps_total")
        setup, ready, counted, chain = sem("setup"), sem("ready"), sem("counted"), sem("chain")
        block = ph.block()

        @block.gpsimd
        def _(g):
            g.memset(before[:, :], 1.0).then_inc(setup, 1)
            g.memset(ones[:, :], 1.0)
            g.memset(zeros[:, :], 0.0)
            g.iota(marks_i[:, :], pattern=[[P, NT]], base=0, channel_multiplier=0)
            g.iota(tiles_i[:, :], pattern=[[1, SORTED_TILES]], base=0, channel_multiplier=0).then_inc(setup, 1)
            g.wait_ge(setup, 2)
            g.tensor_copy(marks[:, :], marks_i[:, :])
            g.tensor_copy(tiles[:, :], tiles_i[:, :])
            g.affine_select(out=before[:, :], in_=before[:, :], compare_op=ALU.is_gt, fill=0.0, base=0,
                            pattern=[[1, P]], channel_multiplier=-1).then_inc(ready, 1)

        @block.tensor
        def _(t_):
            t_.wait_ge(ready, 1)
            flat = onehot_all[:, :, :].rearrange("p t e -> p (t e)")
            nc.tensor.matmul(ps_rank[:, :], before[:, :], flat, start=True, stop=True).then_inc(counted, 1)
            nc.tensor.matmul(ps_total[:, :], ones[:, :], flat, start=True, stop=True).then_inc(counted, 1)

        @block.vector
        def _(v):
            c = Count(chain, 0)

            def link(ins):
                c.inc(ins)
                c.wait(v)

            v.wait_ge(counted, 2)
            v.wait_ge(ready, 1)
            link(nc.vector.tensor_copy(total[:, :].rearrange("p (e t) -> p e t", e=NE),
                                       ps_total[:, :].rearrange("p (t e) -> p e t", e=NE)))
            link(nc.vector.tensor_tensor_scan(cum[:, :], total[:, :], zeros[:, :], 0.0, ALU.add, ALU.add))
            link(nc.vector.tensor_tensor(excl[:, :], cum[:, :], total[:, :], ALU.subtract))
            cum3 = cum[:, :].rearrange("p (e t) -> p e t", e=NE)
            excl3 = excl[:, :].rearrange("p (e t) -> p e t", e=NE)
            link(nc.vector.tensor_tensor(count[:, :, :], cum3[:, :, NT - 1:NT], excl3[:, :, 0:1], ALU.subtract))
            link(nc.vector.tensor_tensor(over[:, :, :], count[:, :, :].to_broadcast([P, NE, NT]),
                                         marks[:, :].unsqueeze(1).to_broadcast([P, NE, NT]), ALU.is_gt))
            link(nc.vector.tensor_reduce(blocks[:, :], over[:, :, :], AX.X, ALU.add))
            link(nc.vector.tensor_tensor_scan(end[:, :], blocks[:, :], zeros[:, 0:NE], 0.0, ALU.add, ALU.add))
            link(nc.vector.tensor_tensor(adj[:, :, 0], end[:, :], blocks[:, :], ALU.subtract))
            link(nc.vector.scalar_tensor_tensor(out=adj[:, :, :], in0=adj[:, :, :], scalar=float(P),
                                                in1=excl3[:, :, 0:1], op0=ALU.mult, op1=ALU.subtract))
            link(nc.vector.tensor_tensor(excl3, excl3, adj[:, :, :].to_broadcast([P, NE, NT]), ALU.add))
            link(nc.vector.tensor_tensor(rank[:, :, :], ps_rank[:, :].rearrange("p (t e) -> p t e", e=NE),
                                         excl[:, :].rearrange("p (e t) -> p t e", e=NE), ALU.add))
            link(nc.vector.tensor_tensor(rank[:, :, :], rank[:, :, :], onehot_all[:, :, :], ALU.mult))
            link(nc.vector.tensor_reduce(spot[:, :], rank[:, :, :], AX.X, ALU.add))
            link(nc.vector.tensor_copy(place_all[:, :], spot[:, :]))
            link(nc.vector.tensor_tensor(past[:, :, :], tiles[:, :].unsqueeze(2).to_broadcast([P, SORTED_TILES, NE]),
                                         end[:, :].unsqueeze(1).to_broadcast([P, SORTED_TILES, NE]), ALU.is_ge))
            link(nc.vector.tensor_reduce(which[:, :], past[:, :, :], AX.X, ALU.add))
            link(nc.vector.tensor_scalar(which[:, :], which[:, :], float(NE - 1), None, ALU.min))
            link(nc.vector.tensor_copy(expert_row[:, :], which[:, :]))


def scatter_phase(nc, sem, xn_dram, sorted_dram, place_all):
    with Phase(nc, "scat") as ph:
        rows = [ph.sb(f"rows{s}", [P, GT, D]) for s in range(2)]
        zeros = ph.sb("zeros", [P, 8, D])
        setup, cleared = sem("setup"), sem("cleared")
        loaded = [sem(f"loaded{s}") for s in range(2)]
        sent = [sem(f"sent{s}") for s in range(2)]
        block = ph.block()

        @block.sync
        def _(sp):
            sp.wait_ge(setup, 1)
            for k in range(SORTED_TILES // 8):
                sp.dma_start(sorted_dram[k * 8 * P:(k + 1) * 8 * P, :].rearrange("(t p) c -> p t c", p=P),
                             zeros[:, :, :]).then_inc(cleared, 16)

            for n in range(NG):
                s = n % 2
                if n >= 2:
                    sp.wait_ge(sent[s], 16 * GT * (n // 2))
                sp.dma_start(rows[s][:, :, :], rows_of(xn_dram, n)).then_inc(loaded[s], 16)

        @block.gpsimd
        def _(g):
            g.memset(zeros[:, :, :], 0.0).then_inc(setup, 1)
            g.wait_ge(cleared, 16 * (SORTED_TILES // 8))
            for n in range(NG):
                s = n % 2
                g.wait_ge(loaded[s], 16 * (n // 2 + 1))
                for t in range(GT):
                    g.indirect_dma_start(sorted_dram[:, :], bass.IndirectOffsetOnAxis(
                        ap=place_all[:, n * GT + t:n * GT + t + 1], axis=0), rows[s][:, t, :], None)\
                        .then_inc(sent[s], 16)
            for s in range(2):
                g.wait_ge(sent[s], 16 * GT * (NG // 2))


def experts_phase(nc, sem, sorted_dram, y_dram, w1, b1, w2, b2, expert_row):
    FC = FF // P
    with Phase(nc, "moe") as ph:
        def two(name, shape, dt=F32):
            return [ph.sb(f"{name}{s}", shape, dt) for s in range(2)]
        w1_sb = ph.sb("w1", [P, NE, FF])
        w2_sb = ph.sb("w2", [P, NE, FC * D])
        b1_sb = ph.sb("b1", [P, NE, FF])
        b2_sb = ph.sb("b2", [P, NE, D])
        ident = ph.sb("ident", [P, P])
        x, xT, hb, h = two("x", [P, D]), two("xT", [P, P]), two("hb", [P, FF]), two("h", [P, FF])
        hT, y = two("hT", [P, FF]), two("y", [P, D])
        psX, psH, psT, psY = [[ph.ps(f"{k}{s}") for s in range(2)] for k in "XHTY"]
        setup, weights = sem("setup"), sem("weights")
        loaded = [sem(f"loaded{s}") for s in range(2)]
        stored = [sem(f"stored{s}") for s in range(2)]
        xT_done, xT_copied, up_done, biased, gelu_done = [sem(k) for k in
                                                          ("xT_done", "xT_copied", "up_done", "biased", "gelu_done")]
        hT_done, hT_copied, down_done, y_done = [sem(k) for k in ("hT_done", "hT_copied", "down_done", "y_done")]
        block = ph.block()

        def expert(eng, n):
            return eng.value_load(expert_row[0:1, bass.ds(n, 1)], min_val=0, max_val=NE - 1)

        @block.sync
        def _(sp):
            for s in range(2):
                sp.sem_inc(stored[s], 16)
            sp.dma_start(w1_sb[:, :, :], w1.rearrange("e c f -> c e f")).then_inc(weights, 16)
            sp.dma_start(b1_sb[:, :, :], bass.AP(tensor=b1.tensor, offset=0, ap=[[0, P], [FF, NE], [1, FF]]))\
                .then_inc(weights, 16)
            sp.dma_start(w2_sb[:, :, :].rearrange("p e (m c) -> p e m c", m=FC),
                         w2.rearrange("e (m p) c -> p e m c", p=P)).then_inc(weights, 16)
            sp.dma_start(b2_sb[:, :, :], bass.AP(tensor=b2.tensor, offset=0, ap=[[0, P], [D, NE], [1, D]]))\
                .then_inc(weights, 16)

            def load(n, s):
                sp.wait_ge(xT_done, n + 1)
                sp.dma_start(x[s][:, :], sorted_dram[bass.ds(n * P, P), :]).then_inc(loaded[s], 16)

            def store(n, s):
                sp.wait_ge(y_done, n + 3)
                sp.dma_start(y_dram[bass.ds(n * P, P), :], y[s][:, :]).then_inc(stored[s], 16)

            skewed(sp.Fori, SORTED_TILES, [(store, 5), (load, 0)])
            for s in range(2):
                sp.wait_ge(stored[s], 16 * (SORTED_TILES // 2 + 1))

        @block.gpsimd
        def _(g):
            emit_identity(nc, g, ident, setup)

        @block.scalar
        def _(a_):
            a_.sem_inc(gelu_done, 2)
            a_.sem_inc(xT_copied, 2)

            def copy_x(n, s):
                a_.wait_ge(xT_done, n + 3)
                a_.wait_ge(up_done, n + 1)
                nc.scalar.activation(xT[s][:, :], psX[s][:, 0:P], ACT.Copy).then_inc(xT_copied, 1)

            def gelu(n, s):
                a_.wait_ge(biased, n + 3)
                a_.wait_ge(hT_done, n + 1)
                nc.scalar.activation(h[s][:, :], hb[s][:, :], ACT.Gelu).then_inc(gelu_done, 1)

            skewed(a_.Fori, SORTED_TILES, [(gelu, 4), (copy_x, 1)])

        @block.vector
        def _(v):
            for q in (biased, hT_copied, y_done):
                v.sem_inc(q, 2)
            v.wait_ge(weights, 64)

            def bias_up(n, s):
                e = expert(v, n)
                v.wait_ge(up_done, n + 3)
                v.wait_ge(gelu_done, n + 1)
                nc.vector.tensor_tensor(hb[s][:, :].unsqueeze(1), psH[s][:, :].unsqueeze(1), b1_sb[:, bass.ds(e, 1), :],
                                        ALU.add).then_inc(biased, 1)

            def copy_h(n, s):
                v.wait_ge(hT_done, n + 3)
                v.wait_ge(down_done, n + 1)
                nc.vector.tensor_copy(hT[s][:, :], psT[s][:, :]).then_inc(hT_copied, 1)

            def bias_down(n, s):
                e = expert(v, n)
                v.wait_ge(down_done, n + 3)
                v.wait_ge(stored[s], 16 * uses(n, s))
                nc.vector.tensor_tensor(y[s][:, :].unsqueeze(1), psY[s][:, 0:D].unsqueeze(1), b2_sb[:, bass.ds(e, 1), :],
                                        ALU.add).then_inc(y_done, 1)

            skewed(v.Fori, SORTED_TILES, [(bias_down, 5), (copy_h, 4), (bias_up, 3)])

        @block.tensor
        def _(t_):
            for q in (xT_done, up_done, hT_done, down_done):
                t_.sem_inc(q, 2)
            t_.wait_ge(setup, 2)
            t_.wait_ge(weights, 64)

            def turn_x(n, s):
                t_.wait_ge(loaded[s], 16 * uses(n, s))
                t_.wait_ge(xT_copied, n + 1)
                nc.tensor.transpose(psX[s][:, 0:P], x[s][:, :], ident[:, :]).then_inc(xT_done, 1)

            def up(n, s):
                e = expert(t_, n)
                t_.wait_ge(xT_copied, n + 3)
                t_.wait_ge(biased, n + 1)
                nc.tensor.matmul(psH[s][:, :], xT[s][:, :], w1_sb[:, bass.ds(e, 1), :].rearrange("p a f -> p (a f)"),
                                 start=True, stop=True).then_inc(up_done, 1)

            def turn_h(n, s):
                t_.wait_ge(gelu_done, n + 3)
                t_.wait_ge(hT_copied, n + 1)
                for m in range(FC):
                    last = nc.tensor.transpose(psT[s][:, m * P:(m + 1) * P], h[s][:, m * P:(m + 1) * P], ident[:, :])
                last.then_inc(hT_done, 1)

            def down(n, s):
                e = expert(t_, n)
                t_.wait_ge(hT_copied, n + 3)
                t_.wait_ge(y_done, n + 1)
                for m in range(FC):
                    last = nc.tensor.matmul(psY[s][:, 0:D], hT[s][:, m * P:(m + 1) * P],
                                            w2_sb[:, bass.ds(e, 1), m * D:(m + 1) * D].rearrange("p a f -> p (a f)"),
                                            start=(m == 0), stop=(m == FC - 1))
                last.then_inc(down_done, 1)

            skewed(t_.Fori, SORTED_TILES, [(down, 5), (turn_h, 4), (up, 2), (turn_x, 1)])


def gather_phase(nc, sem, x1_dram, y_dram, place_all, weight_all, x2_dram):
    with Phase(nc, "gath") as ph:
        x1 = [ph.sb(f"x{s}", [P, GT, D]) for s in range(2)]
        y = [ph.sb(f"y{s}", [P, GT, D]) for s in range(2)]
        x2 = [ph.sb(f"o{s}", [P, GT, D]) for s in range(2)]
        loaded = [sem(f"loaded{s}") for s in range(2)]
        gathered = [sem(f"gathered{s}") for s in range(2)]
        stored = [sem(f"stored{s}") for s in range(2)]
        summed = sem("summed")
        block = ph.block()

        @block.sync
        def _(sp):
            for n in range(NG):
                s = n % 2
                if n >= 2:
                    sp.wait_ge(summed, n - 1)
                sp.dma_start(x1[s][:, :, :], rows_of(x1_dram, n)).then_inc(loaded[s], 16)
            for s in range(2):
                sp.wait_ge(stored[s], 16 * (NG // 2))

        @block.gpsimd
        def _(g):
            for n in range(NG):
                s = n % 2
                if n >= 2:
                    g.wait_ge(summed, n - 1)
                for t in range(GT):
                    g.indirect_dma_start(y[s][:, t, :], None, y_dram[:, :], bass.IndirectOffsetOnAxis(
                        ap=place_all[:, n * GT + t:n * GT + t + 1], axis=0)).then_inc(gathered[s], 16)

        @block.vector
        def _(v):
            for n in range(NG):
                s = n % 2
                v.wait_ge(loaded[s], 16 * (n // 2 + 1))
                v.wait_ge(gathered[s], 16 * GT * (n // 2 + 1))
                if n >= 2:
                    v.wait_ge(stored[s], 16 * (n // 2))
                for t in range(GT):
                    last = nc.vector.scalar_tensor_tensor(
                        out=x2[s][:, t, :], in0=y[s][:, t, :], scalar=weight_all[:, n * GT + t:n * GT + t + 1],
                        in1=x1[s][:, t, :], op0=ALU.mult, op1=ALU.add)
                last.then_inc(summed, 1)

        @block.scalar
        def _(a_):
            for n in range(NG):
                s = n % 2
                a_.wait_ge(summed, n + 1)
                a_.dma_start(rows_of(x2_dram, n), x2[s][:, :, :]).then_inc(stored[s], 16)


def bias_phase(nc, sem, offsets, pos_bias, fwd_dram, rev_dram):
    NCH = WINDOW // P
    with Phase(nc, "bias") as ph:
        off_i, off = ph.sb("off_i", [P, NOFF], I32), ph.sb("off", [P, NOFF])
        pb = ph.sb("pb", [P, NOFF, H])
        dist_i, dist = ph.sb("dist_i", [P, 2 * NCH], I32), ph.sb("dist", [P, 2 * NCH])
        off_mask = ph.sb("off_mask", [P, NOFF])
        val = ph.sb("val", [P, H, NOFF])
        top, tot = ph.sb("top", [P, H, 1]), ph.sb("tot", [P, H])
        res = ph.sb("res", [P, H])
        ident = ph.sb("ident", [P, P])
        rows = [ph.sb(f"rows{k}", [H, 2 * WINDOW]) for k in range(2)]
        psT = ph.ps("psT")
        setup, loaded, chain, shifted, exp_done, ln_done, turned, stored = [sem(k) for k in (
            "setup", "loaded", "chain", "shifted", "exp_done", "ln_done", "turned", "stored")]
        block = ph.block()

        @block.sync
        def _(sp):
            sp.dma_start(off_i[:, :], bass.AP(tensor=offsets.tensor, offset=0, ap=[[0, P], [1, NOFF]])).then_inc(loaded, 16)
            sp.dma_start(pb[:, :, :], bass.AP(tensor=pos_bias.tensor, offset=0, ap=[[0, P], [H, NOFF], [1, H]]))\
                .then_inc(loaded, 16)
            sp.wait_ge(chain, 2 + 5 * 2 * NCH)
            sp.dma_start(fwd_dram, rows[0][:, :]).then_inc(stored, 16)
            sp.dma_start(rev_dram, rows[1][:, :]).then_inc(stored, 16)
            sp.wait_ge(stored, 32)

        @block.gpsimd
        def _(g):
            emit_identity(nc, g, ident, setup)
            for k in range(NCH):
                g.iota(dist_i[:, k:k + 1], pattern=[[0, 1]], base=k * P, channel_multiplier=1)
                last = g.iota(dist_i[:, NCH + k:NCH + k + 1], pattern=[[0, 1]], base=WINDOW - 1 - k * P,
                              channel_multiplier=-1)
            last.then_inc(setup, 1)
            for k in range(2):
                last = g.memset(rows[k][:, :], MASKED)
            last.then_inc(setup, 1)

        @block.vector
        def _(v):
            c = Count(chain, 0)

            def link(ins):
                c.inc(ins)
                c.wait(v)

            v.wait_ge(setup, 4)
            v.wait_ge(loaded, 32)
            link(nc.vector.tensor_copy(dist[:, :], dist_i[:, :]))
            link(nc.vector.tensor_copy(off[:, :], off_i[:, :]))
            for k in range(2 * NCH):
                link(nc.vector.tensor_scalar(off_mask[:, :], off[:, :], dist[:, k:k + 1], MASKED, ALU.not_equal, ALU.mult))
                link(nc.vector.tensor_tensor(val[:, :, :], pb[:, :, :].rearrange("p o h -> p h o"),
                                             off_mask[:, :].unsqueeze(1).to_broadcast([P, H, NOFF]), ALU.add))
                link(nc.vector.tensor_reduce(top[:, :, 0], val[:, :, :], AX.X, ALU.max))
                nc.vector.tensor_tensor(val[:, :, :], val[:, :, :], top[:, :, :].to_broadcast([P, H, NOFF]),
                                        ALU.subtract).then_inc(shifted, 1)
                v.wait_ge(exp_done, k + 1)
                nc.vector.tensor_reduce(tot[:, :], val[:, :, :], AX.X, ALU.add).then_inc(shifted, 1)
                v.wait_ge(ln_done, k + 1)
                link(nc.vector.tensor_tensor(res[:, :], tot[:, :], top[:, :, 0], ALU.add))
                v.wait_ge(turned, k + 1)
                at = (P - 1 if k < NCH else P) + (k % NCH) * P
                link(nc.vector.tensor_copy(rows[k // NCH][:, at:at + P], psT[0:H, 0:P]))

        @block.scalar
        def _(a_):
            for k in range(2 * NCH):
                a_.wait_ge(shifted, 2 * k + 1)
                nc.scalar.activation(val[:, :, :], val[:, :, :], ACT.Exp).then_inc(exp_done, 1)
                a_.wait_ge(shifted, 2 * k + 2)
                nc.scalar.activation(tot[:, :], tot[:, :], ACT.Ln).then_inc(ln_done, 1)

        @block.tensor
        def _(t_):
            t_.wait_ge(setup, 2)
            for k in range(2 * NCH):
                t_.wait_ge(chain, 2 + 5 * k + 4)
                nc.tensor.transpose(psT[0:H, 0:P], res[:, :], ident[:, :]).then_inc(turned, 1)


def shifted_rows(bias_dram, h0, n_heads):
    return bass.AP(tensor=bias_dram.tensor, offset=bias_dram.offset + h0 * 2 * WINDOW,
                   ap=[[1, P], [2 * WINDOW, n_heads], [1, WB * P]])


def backwards(t, n_heads):
    whole = t[:, :, :]
    return bass.AP(tensor=whole.tensor, offset=whole.offset + WB * P - 1,
                   ap=[list(whole.ap[0]), [WB * P, n_heads], [-1, WB * P]])


def gated_phase(nc, sem, x_dram, att_dram, w_gate, b_gate, norm1, w_out, sum_dram, xr_dram):
    with Phase(nc, "gate") as ph:
        def two(name, shape, dt=F32):
            return [ph.sb(f"{name}{s}", shape, dt) for s in range(2)]
        x_in = [ph.sb(f"x{s}", [P, GT, D]) for s in range(4)]
        a_in = [ph.sb(f"a{s}", [P, GT, D]) for s in range(4)]
        y, xr, xT, gate, ag = two("y", [P, GT, D]), two("xr", [P, GT, D]), two("xT", [P, GW]), two("gate", [P, GW]), two("ag", [P, GW])
        yy = two("yy", [P, GT, D])
        total, xr2, junk = two("total", [P, GT, D]), two("xr2", [P, GT, D]), two("junk", [P, D])
        st, mv, rstd, rr = two("st", [P, GT, 6]), two("mv", [P, GT, 2]), two("rstd", [P, GT]), two("rr", [P, GT])
        sq, r2 = two("sq", [P, GT]), two("r2", [P, GT])
        wg, wo, bg, n1 = ph.sb("wg", [P, D]), ph.sb("wo", [P, D]), ph.sb("bg", [P, 1]), ph.sb("n1", [P, 1])
        ident, power = ph.sb("ident", [P, P]), ph.sb("power", [P, GT])
        psT, psG, psA, psO = [[ph.ps(f"{k}{s}") for s in range(2)] for k in "TGAO"]
        setup, weights = sem("setup"), sem("weights")
        divider = sem("divider")
        loaded = [sem(f"loaded{s}") for s in range(4)]
        stored = [sem(f"stored{s}") for s in range(2)]
        stats_chain, rstd_chain, y_chain = sem("stats_chain"), sem("rstd_chain"), sem("y_chain")
        turned, xT_copied, gate_done, sig_done = sem("turned"), sem("xT_copied"), sem("gate_done"), sem("sig_done")
        ag_done, out_done, sq_chain, r2_chain, xr2_done = [sem(k) for k in ("ag_done", "out_done", "sq_chain", "r2_chain", "xr2_done")]
        NY, NSQ = 2 * GT, 2 + GT
        block = ph.block()

        @block.sync
        def _(sp):
            for s in range(2):
                sp.sem_inc(stored[s], 32)
            for dst, src in ((wg[:, :], w_gate), (wo[:, :], w_out), (bg[:, :], b_gate.rearrange("(c a) -> c a", a=1)),
                             (n1[:, :], norm1.rearrange("(c a) -> c a", a=1))):
                sp.dma_start(dst, src).then_inc(weights, 16)

            def load(n, q):
                sp.wait_ge(sq_chain, NSQ * (n + 1))
                sp.dma_start(x_in[q][:, :, :], rows_of(x_dram, n)).then_inc(loaded[q], 16)
                sp.dma_start(a_in[q][:, :, :], rows_of(att_dram, n)).then_inc(loaded[q], 16)

            def store(n, q):
                s = q % 2
                sp.wait_ge(xr2_done, n + 3)
                sp.dma_start(rows_of(sum_dram, n), total[s][:, :, :]).then_inc(stored[s], 16)
                sp.dma_start(rows_of(xr_dram, n), xr2[s][:, :, :]).then_inc(stored[s], 16)

            skewed4(sp.Fori, NG, [(store, 4), (load, 0)])
            for s in range(2):
                sp.wait_ge(stored[s], 32 * (NG // 2 + 1))

        @block.gpsimd
        def _(g):
            g.sem_inc(r2_chain, 4)
            emit_identity(nc, g, ident, setup)
            g.memset(power[:, :], -0.5).then_inc(setup, 1)
            g.wait_ge(setup, 3)
            rc = Count(rstd_chain, RMS_STEPS)

            def rstds(n, q):
                s = q % 2
                wait_apart(g, divider, (stats_chain, (n + 1) * STATS_STEPS), (y_chain, (n + 1) * NY))
                rc.start(n)
                emit_rstd(nc, g, rc, mv[s], rstd[s], power, divider, rms=(RMS_EPS, rr[s]))
                rc.end()

            def second(n, q):
                s = q % 2
                wait_apart(g, divider, (sq_chain, (n + 5) * NSQ), (xr2_done, n + 1))
                g.tensor_scalar(r2[s][:, :], sq[s][:, :], 1.0 / D, RMS_EPS, ALU.mult, ALU.add).then_inc(r2_chain, 1)
                g.wait_ge(r2_chain, 2 * n + 5)
                g.tensor_tensor(r2[s][:, :], r2[s][:, :], power[:, :], ALU.pow).then_inc(r2_chain, 1)

            skewed4(g.Fori, NG, [(second, 3), (rstds, 1)])

        @block.vector
        def _(v):
            v.sem_inc(y_chain, 2 * NY)
            v.sem_inc(sq_chain, 4 * NSQ)
            v.sem_inc(xr2_done, 2)
            v.sem_inc(ag_done, 2)
            c1 = Count(stats_chain, STATS_STEPS)
            c2 = Count(y_chain, NY, 2)
            c3 = Count(sq_chain, NSQ, 4)

            def stats(n, q):
                s = q % 2
                c1.start(n)
                v.wait_ge(loaded[q], 32 * uses4(n, q))
                emit_stats(nc, v, c1, x_in[q], st[s], mv[s], divider)
                c1.end()

            def norm(n, q):
                s = q % 2
                c2.start(n)
                v.wait_ge(rstd_chain, (n + 1) * RMS_STEPS)
                v.wait_ge(turned, n + 1)
                emit_apply(nc, c2, x_in[q], y[s], mv[s], rstd[s])
                c2.wait(v)
                for t in range(GT):
                    c2.inc(nc.vector.tensor_scalar(xr[s][:, t, :], y[s][:, t, :], rr[s][:, t:t + 1], None, ALU.mult))
                c2.end()

            def gating(n, q):
                s = q % 2
                v.wait_ge(sig_done, n + 1)
                v.wait_ge(out_done, n + 1)
                nc.vector.tensor_tensor(ag[s][:, :], psA[s][:, :], gate[s][:, :], ALU.mult).then_inc(ag_done, 1)

            def residual(n, q):
                s = q % 2
                c3.start(n)
                v.wait_ge(out_done, n + 3)
                v.wait_ge(stored[s], 32 * uses4(n, s, 2))
                c3.inc(nc.vector.tensor_tensor(yy[s][:, :, :], y[s][:, :, :],
                                               psO[s][:, :].rearrange("p (t c) -> p t c", t=GT), ALU.add))
                c3.wait(v)
                c3.inc(nc.vector.tensor_tensor(total[s][:, :, :], yy[s][:, :, :], x_in[q][:, :, :], ALU.add))
                for t in range(GT):
                    if t >= 2:
                        v.wait_ge(c3.sem, c3.base + c3.c - 1)
                    c3.inc(nc.vector.tensor_tensor_reduce(out=junk[t % 2][:, :], in0=yy[s][:, t, :], in1=yy[s][:, t, :],
                                                          scale=1.0, scalar=0.0, op0=ALU.mult, op1=ALU.add,
                                                          accum_out=sq[s][:, t:t + 1]))
                c3.end()

            def scale(n, q):
                s = q % 2
                v.wait_ge(r2_chain, 2 * n + 6)
                for t in range(GT):
                    last = nc.vector.tensor_scalar(xr2[s][:, t, :], yy[s][:, t, :], r2[s][:, t:t + 1], None, ALU.mult)
                last.then_inc(xr2_done, 1)

            def late(n, q):
                gating(n, q)
                residual(n, q)

            skewed4(v.Fori, NG, [(scale, 4), (late, 3), (norm, 2), (stats, 1)])

        @block.scalar
        def _(a_):
            a_.wait_ge(weights, 64)

            def gates(n, q):
                s = q % 2
                a_.wait_ge(turned, n + 3)
                a_.wait_ge(gate_done, n + 1)
                nc.scalar.activation(xT[s][:, :], psT[s][:, :], ACT.Copy, scale=n1[:, 0:1]).then_inc(xT_copied, 1)
                a_.wait_ge(gate_done, n + 3)
                a_.wait_ge(ag_done, n + 1)
                nc.scalar.activation(gate[s][:, :], psG[s][:, :], ACT.Sigmoid, bias=bg[:, 0:1]).then_inc(sig_done, 1)

            skewed4(a_.Fori, NG, [(gates, 3)])

        @block.tensor
        def _(t_):
            for q in (turned, gate_done, out_done):
                t_.sem_inc(q, 2)
            t_.wait_ge(setup, 2)
            t_.wait_ge(weights, 64)

            def turn(n, q):
                s = q % 2
                t_.wait_ge(ag_done, n + 1)
                t_.wait_ge(loaded[q], 32 * uses4(n, q))
                for t in range(GT):
                    nc.tensor.transpose(psA[s][:, t * P:(t + 1) * P], a_in[q][:, t, :], ident[:, :])
                t_.wait_ge(y_chain, (n + 3) * NY)
                for t in range(GT):
                    last = nc.tensor.transpose(psT[s][:, t * P:(t + 1) * P], xr[s][:, t, :], ident[:, :])
                last.then_inc(turned, 1)

            def rest(n, q):
                s = q % 2
                t_.wait_ge(xT_copied, n + 1)
                nc.tensor.matmul(psG[s][:, :], wg[:, :], xT[s][:, :], start=True, stop=True).then_inc(gate_done, 1)
                t_.wait_ge(ag_done, n + 3)
                t_.wait_ge(sq_chain, NSQ * (n + 3))
                for t in range(GT):
                    last = nc.tensor.matmul(psO[s][:, t * D:(t + 1) * D], ag[s][:, t * P:(t + 1) * P], wo[:, :],
                                            start=True, stop=True)
                last.then_inc(out_done, 1)

            skewed4(t_.Fori, NG, [(rest, 3), (turn, 2)])


def skewed4(fori, count, stages):
    most = max(lag for _, lag in stages)
    first = -(-most // 4) * 4

    def step(quarter, r, fixed):
        for fn, lag in stages:
            q = (r - lag) % 4
            n = 4 * (quarter + (r - lag - q) // 4) + q
            if not fixed or 0 <= n < count:
                fn(n, q)

    for j in range(first):
        step(j // 4, j % 4, True)
    with fori(first // 4, count // 4) as i:
        for r in range(4):
            step(i, r, False)
    for j in range(count, count + most):
        step(j // 4, j % 4, True)


def uses4(n, q, of=4):
    return (n - q) // of + 1


def swiglu_phase(nc, sem, xr_dram, sum_dram, norm2, w_gate, w_up, w_down, x_dram):
    NC = len(F_CHUNKS)
    with Phase(nc, "swi") as ph:
        def two(name, shape, dt=F32):
            return [ph.sb(f"{name}{s}", shape, dt) for s in range(2)]
        xr = two("xr", [P, GT, D])
        res = [ph.sb(f"res{s}", [P, GT, D]) for s in range(4)]
        xT, x3 = two("xT", [P, GW]), two("x3", [P, GT, D])
        sg = two("sg", [P, GW])
        h = [[ph.sb(f"h{s}{c}", [P, GW]) for c in range(NC)] for s in range(2)]
        wg, wu, n2 = ph.sb("wg", [P, FFN1]), ph.sb("wu", [P, FFN1]), ph.sb("n2", [P, 1])
        wd = ph.sb("wd", [P, NC, D])
        ident = ph.sb("ident", [P, P])
        psT, psG, psU, psD = [[ph.ps(f"{k}{s}") for s in range(2)] for k in "TGUD"]
        setup, weights = sem("setup"), sem("weights")
        loaded = [sem(f"loaded{s}") for s in range(4)]
        stored = [sem(f"stored{s}") for s in range(2)]
        turned, xT_copied, up_done, silu_done, h_done, down_done, x3_done = [sem(k) for k in (
            "turned", "xT_copied", "up_done", "silu_done", "h_done", "down_done", "x3_done")]
        block = ph.block()

        @block.sync
        def _(sp):
            for s in range(2):
                sp.sem_inc(stored[s], 16)
            for dst, src in ((wg[:, :], w_gate), (wu[:, :], w_up), (n2[:, :], norm2.rearrange("(c a) -> c a", a=1))):
                sp.dma_start(dst, src).then_inc(weights, 16)
            for c, (f0, fw) in enumerate(F_CHUNKS):
                sp.dma_start(wd[0:fw, c, :], w_down[f0:f0 + fw, :]).then_inc(weights, 16)

            def load(n, q):
                sp.wait_ge(turned, n + 1)
                sp.wait_ge(x3_done, n + 1)
                sp.dma_start(xr[q % 2][:, :, :], rows_of(xr_dram, n)).then_inc(loaded[q], 16)
                sp.dma_start(res[q][:, :, :], rows_of(sum_dram, n)).then_inc(loaded[q], 16)

            def store(n, q):
                sp.wait_ge(x3_done, n + 5)
                sp.dma_start(rows_of(x_dram, n), x3[q % 2][:, :, :]).then_inc(stored[q % 2], 16)

            skewed4(sp.Fori, NG, [(store, 3), (load, 0)])
            for s in range(2):
                sp.wait_ge(stored[s], 16 * (NG // 2 + 1))

        @block.gpsimd
        def _(g):
            emit_identity(nc, g, ident, setup)

        @block.scalar
        def _(a_):
            a_.sem_inc(silu_done, 2)
            a_.sem_inc(xT_copied, 2)
            a_.wait_ge(weights, 96)

            def copy(n, q):
                a_.wait_ge(turned, n + 3)
                a_.wait_ge(up_done, NC * (n + 1))
                nc.scalar.activation(xT[q % 2][:, :], psT[q % 2][:, :], ACT.Copy, scale=n2[:, 0:1]).then_inc(xT_copied, 1)

            def silu(n, q):
                for c, (f0, fw) in enumerate(F_CHUNKS):
                    a_.wait_ge(up_done, NC * (n + 2) + c + 1)
                    a_.wait_ge(h_done, NC * n + c + 1)
                    k = (NC * q + c) % 2
                    nc.scalar.activation(sg[k][0:fw, :], psG[k][0:fw, :], ACT.Silu).then_inc(silu_done, 1)

            skewed4(a_.Fori, NG, [(silu, 2), (copy, 1)])

        @block.vector
        def _(v):
            v.sem_inc(h_done, 2)
            v.sem_inc(x3_done, 4)

            def mult(n, q):
                v.wait_ge(down_done, n + 1)
                for c, (f0, fw) in enumerate(F_CHUNKS):
                    k = (NC * q + c) % 2
                    v.wait_ge(silu_done, NC * n + c + 3)
                    nc.vector.tensor_tensor(h[q % 2][c][0:fw, :], psU[k][0:fw, :], sg[k][0:fw, :], ALU.mult)\
                        .then_inc(h_done, 1)

            def finish(n, q):
                s = q % 2
                v.wait_ge(down_done, n + 3)
                v.wait_ge(loaded[q], 32 * uses4(n, q))
                v.wait_ge(stored[s], 16 * uses4(n, s, 2))
                nc.vector.tensor_tensor(x3[s][:, :, :], res[q][:, :, :],
                                        psD[s][:, :].rearrange("p (t c) -> p t c", t=GT), ALU.add).then_inc(x3_done, 1)

            skewed4(v.Fori, NG, [(finish, 3), (mult, 2)])

        @block.tensor
        def _(t_):
            t_.sem_inc(turned, 2)
            t_.sem_inc(up_done, 2 * NC)
            t_.sem_inc(down_done, 2)
            t_.wait_ge(setup, 2)
            t_.wait_ge(weights, 96)

            def turn(n, q):
                t_.wait_ge(loaded[q], 32 * uses4(n, q))
                t_.wait_ge(xT_copied, n + 1)
                for t in range(GT):
                    last = nc.tensor.transpose(psT[q % 2][:, t * P:(t + 1) * P], xr[q % 2][:, t, :], ident[:, :])
                last.then_inc(turned, 1)

            def up(n, q):
                t_.wait_ge(xT_copied, n + 3)
                for c, (f0, fw) in enumerate(F_CHUNKS):
                    k = (NC * q + c) % 2
                    t_.wait_ge(h_done, NC * n + c + 1)
                    nc.tensor.matmul(psG[k][0:fw, :], wg[:, f0:f0 + fw], xT[q % 2][:, :], start=True, stop=True)
                    nc.tensor.matmul(psU[k][0:fw, :], wu[:, f0:f0 + fw], xT[q % 2][:, :], start=True, stop=True)\
                        .then_inc(up_done, 1)

            def down(n, q):
                t_.wait_ge(h_done, NC * n + NC + 2)
                t_.wait_ge(x3_done, n + 3)
                for t in range(GT):
                    for c, (f0, fw) in enumerate(F_CHUNKS):
                        last = nc.tensor.matmul(psD[q % 2][:, t * D:(t + 1) * D], h[q % 2][c][0:fw, t * P:(t + 1) * P],
                                                wd[0:fw, c, :], start=(c == 0), stop=(c == NC - 1))
                last.then_inc(down_done, 1)

            skewed4(t_.Fori, NG, [(down, 3), (up, 2), (turn, 1)])


LIGHT, HEAVY = D // 2, 4 * D
TOP = 128
FETCH = 9.0 / 8.0 * TOP
DESCENTS = 50


def two_branch_phase(nc, sem, x_dram, token, light, heavy, base_dram, heavy_dram, s_all):
    HC = HEAVY // P
    with Phase(nc, "two") as ph:
        def two(name, shape, dt=F32):
            return [ph.sb(f"{name}{s}", shape, dt) for s in range(2)]
        x_in = [ph.sb(f"x{s}", [P, GT, D]) for s in range(8)]
        y, z, zT = two("y", [P, GT, D]), two("z", [P, GT, D]), two("zT", [P, GW])
        hl, hh = two("hl", [LIGHT, GW]), two("hh", [P, HC, GW])
        base, hv, junk = two("base", [P, GT, D]), two("hv", [P, GT, D]), two("junk", [P, D])
        st, mv, rstd, rr = two("st", [P, GT, 6]), two("mv", [P, GT, 2]), two("rstd", [P, GT]), two("rr", [P, GT])
        w1l, w1h = ph.sb("w1l", [P, LIGHT]), ph.sb("w1h", [P, HEAVY])
        w2l, w2h = ph.sb("w2l", [LIGHT, D]), ph.sb("w2h", [P, HC, D])
        gl, gh = ph.sb("gl", [P, 1]), ph.sb("gh", [P, 1])
        b1l, b1h = ph.sb("b1l", [LIGHT, 1]), ph.sb("b1h", [P, HC])
        b2l, b2h, tok = ph.sb("b2l", [P, 1, D]), ph.sb("b2h", [P, 1, D]), ph.sb("tok", [P, D])
        ident, power = ph.sb("ident", [P, P]), ph.sb("power", [P, GT])
        psT = [ph.ps("psT0")]
        psL = [ph.ps("psL0")]
        psH = [ph.ps(f"psH{s}") for s in range(2)]
        psDL, psDH = [[ph.ps(f"{k}{s}") for s in range(2)] for k in ("DL", "DH")]
        setup, weights, scaled = sem("setup"), sem("weights"), sem("scaled")
        divider = sem("divider")
        loaded = [sem(f"loaded{s}") for s in range(8)]
        stored = [sem(f"stored{s}") for s in range(2)]
        stats_chain, rstd_chain, y_chain, turned, zT_copied = [sem(k) for k in (
            "stats_chain", "rstd_chain", "y_chain", "turned", "zT_copied")]
        up_done, gelu_done, down_done, out_done = [sem(k) for k in ("up_done", "gelu_done", "down_done", "out_done")]
        base_step = sem("base_step")
        NY = 3 * GT
        UP = HC + 1
        block = ph.block()
        one = lambda a: a.rearrange("(c a) -> c a", a=1)
        loads = [(w1l[:, :], light[1]), (w1h[:, :], heavy[1]), (w2l[:, :], light[3]),
                 (w2h[:, :, :], heavy[3].rearrange("(m p) c -> p m c", p=P)), (gl[:, :], one(light[0])),
                 (gh[:, :], one(heavy[0])), (b1l[:, :], one(light[2])), (b2l[:, 0, :], bc_rows(light[4], D)),
                 (b2h[:, 0, :], bc_rows(heavy[4], D)), (tok[:, :], bc_rows(token, D))]
        loads += [(b1h[:, m:m + 1], one(heavy[2][m * P:(m + 1) * P])) for m in range(HC)]
        NW = 16 * len(loads)

        @block.sync
        def _(sp):
            for s in range(2):
                sp.sem_inc(stored[s], 32)
            for dst, src in loads:
                sp.dma_start(dst, src).then_inc(weights, 16)

            def load(n, q):
                sp.wait_ge(out_done, n + 1)
                sp.dma_start(x_in[q][:, :, :], rows_of(x_dram, n)).then_inc(loaded[q], 16)

            def store(n, q):
                s = q % 2
                sp.wait_ge(out_done, n + 9)
                sp.dma_start(rows_of(base_dram, n), base[s][:, :, :]).then_inc(stored[s], 16)
                sp.dma_start(rows_of(heavy_dram, n), hv[s][:, :, :]).then_inc(stored[s], 16)

            skewed8(sp.Fori, NG, [(store, 5), (load, 0)])
            for s in range(2):
                sp.wait_ge(stored[s], 32 * (NG // 2 + 1))

        @block.gpsimd
        def _(g):
            emit_identity(nc, g, ident, setup)
            g.memset(power[:, :], -0.5).then_inc(setup, 1)
            g.wait_ge(setup, 3)
            rc = Count(rstd_chain, RMS_STEPS)

            def rstds(n, q):
                s = q % 2
                wait_apart(g, divider, (stats_chain, (n + 1) * STATS_STEPS), (y_chain, (n + 1) * NY))
                rc.start(n)
                emit_rstd(nc, g, rc, mv[s], rstd[s], power, divider, rms=(None, rr[s]))
                rc.end()

            skewed8(g.Fori, NG, [(rstds, 1)])

        @block.vector
        def _(v):
            v.sem_inc(y_chain, 2 * NY)
            v.sem_inc(out_done, 8)
            c1 = Count(stats_chain, STATS_STEPS)
            c2 = Count(y_chain, NY, 2)
            v.wait_ge(weights, NW)
            nc.vector.tensor_scalar(w1l[:, :], w1l[:, :], gl[:, 0:1], None, ALU.mult).then_inc(scaled, 1)
            nc.vector.tensor_scalar(w1h[:, :], w1h[:, :], gh[:, 0:1], None, ALU.mult).then_inc(scaled, 1)

            def stats(n, q):
                s = q % 2
                c1.start(n)
                v.wait_ge(loaded[q], 16 * uses4(n, q, 8))
                emit_stats(nc, v, c1, x_in[q], st[s], mv[s], divider)
                c1.end()

            def norm(n, q):
                s = q % 2
                c2.start(n)
                v.wait_ge(rstd_chain, (n + 1) * RMS_STEPS)
                v.wait_ge(turned, n + 1)
                emit_apply(nc, c2, x_in[q], y[s], mv[s], rstd[s])
                c2.wait(v)
                for t in range(GT):
                    c2.inc(nc.vector.tensor_scalar(z[s][:, t, :], y[s][:, t, :], rr[s][:, t:t + 1], None, ALU.mult))
                for t in range(GT):
                    if t >= 2:
                        v.wait_ge(c2.sem, c2.base + c2.c - 1)
                    c2.inc(nc.vector.tensor_tensor_reduce(out=junk[t % 2][:, :], in0=y[s][:, t, :], in1=tok[:, :],
                                                          scale=1.0, scalar=0.0, op0=ALU.mult, op1=ALU.add,
                                                          accum_out=s_all[:, bass.ds(n * GT + t, 1)]))
                c2.end()

            def finish(n, q):
                s = q % 2
                v.wait_ge(down_done, n + 3)
                v.wait_ge(stored[s], 32 * uses4(n, s, 2))
                nc.vector.tensor_tensor(base[s][:, :, :], x_in[q][:, :, :],
                                        psDL[s][:, :].rearrange("p (t c) -> p t c", t=GT), ALU.add).then_inc(base_step, 1)
                nc.vector.tensor_tensor(hv[s][:, :, :], psDH[s][:, :].rearrange("p (t c) -> p t c", t=GT),
                                        b2h[:, :, :].to_broadcast([P, GT, D]), ALU.add)
                v.wait_ge(base_step, n + 1)
                nc.vector.tensor_tensor(base[s][:, :, :], base[s][:, :, :], b2l[:, :, :].to_broadcast([P, GT, D]),
                                        ALU.add).then_inc(out_done, 1)

            skewed8(v.Fori, NG, [(finish, 5), (norm, 2), (stats, 1)])

        @block.scalar
        def _(a_):
            a_.sem_inc(gelu_done, 2 * UP)
            a_.wait_ge(weights, NW)

            def gelus(n, q):
                s = q % 2
                a_.wait_ge(down_done, n + 1)
                for c in range(UP):
                    a_.wait_ge(up_done, UP * n + c + 1)
                    if c == 0:
                        ins = nc.scalar.activation(hl[s][:, :], psL[0][0:LIGHT, :], ACT.Gelu, bias=b1l[:, 0:1])
                    else:
                        ins = nc.scalar.activation(hh[s][:, c - 1, :], psH[c % 2][:, :], ACT.Gelu, bias=b1h[:, c - 1:c])
                    ins.then_inc(gelu_done, 1)

            def copy(n, q):
                a_.wait_ge(turned, n + 3)
                a_.wait_ge(up_done, UP * (n - 1)) if isinstance(n, int) and n >= 2 else (
                    a_.wait_ge(up_done, UP * (n - 1)) if not isinstance(n, int) else None)
                nc.scalar.activation(zT[q % 2][:, :], psT[0][:, :], ACT.Copy).then_inc(zT_copied, 1)

            skewed8(a_.Fori, NG, [(gelus, 4), (copy, 3)])

        @block.tensor
        def _(t_):
            t_.sem_inc(turned, 2)
            t_.sem_inc(down_done, 2)
            t_.wait_ge(setup, 2)
            t_.wait_ge(scaled, 2)

            def turn(n, q):
                t_.wait_ge(y_chain, (n + 3) * NY)
                if not (isinstance(n, int) and n == 0):
                    t_.wait_ge(zT_copied, n)
                for t in range(GT):
                    last = nc.tensor.transpose(psT[0][:, t * P:(t + 1) * P], z[q % 2][:, t, :], ident[:, :])
                last.then_inc(turned, 1)

            def up(n, q):
                t_.wait_ge(zT_copied, n + 1)
                for c in range(UP):
                    if c == 0:
                        t_.wait_ge(gelu_done, UP * (n + 1) + 1)
                        ins = nc.tensor.matmul(psL[0][0:LIGHT, :], w1l[:, :], zT[q % 2][:, :], start=True, stop=True)
                    else:
                        t_.wait_ge(gelu_done, UP * (n + 1) + c + 2 if c <= 2 else UP * (n + 2) + c - 1)
                        ins = nc.tensor.matmul(psH[c % 2][:, :], w1h[:, (c - 1) * P:c * P], zT[q % 2][:, :],
                                               start=True, stop=True)
                    ins.then_inc(up_done, 1)

            def down(n, q):
                s = q % 2
                t_.wait_ge(gelu_done, UP * (n + 3))
                t_.wait_ge(out_done, n + 7)
                for t in range(GT):
                    nc.tensor.matmul(psDL[s][:, t * D:(t + 1) * D], hl[s][:, t * P:(t + 1) * P], w2l[:, :],
                                     start=True, stop=True)
                for t in range(GT):
                    for m in range(HC):
                        last = nc.tensor.matmul(psDH[s][:, t * D:(t + 1) * D], hh[s][:, m, t * P:(t + 1) * P],
                                                w2h[:, m, :], start=(m == 0), stop=(m == HC - 1))
                last.then_inc(down_done, 1)

            skewed8(t_.Fori, NG, [(down, 5), (up, 4), (turn, 3)])


def skewed8(fori, count, stages):
    most = max(lag for _, lag in stages)
    assert most <= 8

    def step(eighth, r, fixed):
        for fn, lag in stages:
            q = (r - lag) % 8
            n = 8 * (eighth + (r - lag - q) // 8) + q
            if not fixed or 0 <= n < count:
                fn(n, q)

    for j in range(8):
        step(0, j, True)
    if count > 16:
        with fori(1, count // 8) as i:
            for r in range(8):
                step(i, r, False)
    else:
        for r in range(8):
            step(1, r, True)
    for j in range(count, count + most):
        step(j // 8, j % 8, True)


def descent_phase(nc, sem, s_all, coef_all):
    ROWS = NT
    LOGK = math.log(FETCH)
    with Phase(nc, "desc") as ph:
        s64, t64, e64 = ph.sb("s64", [ROWS, P]), ph.sb("t64", [ROWS, P]), ph.sb("e64", [ROWS, P])
        s8, key8, work = ph.sb("s8", [B, S]), ph.sb("key8", [B, S]), [ph.sb(f"work{k}", [B, S]) for k in range(2)]
        sc8, gt8, eq8, cum8, zeros = [ph.sb(k, [B, S]) for k in ("sc8", "gt8", "eq8", "cum8", "zeros")]
        key64 = ph.sb("key64", [ROWS, P])
        coef64 = ph.sb("coef64", [ROWS, P])
        top8 = ph.sb("top8", [B, 8])
        smax8, smax, nega, M, lnz, acc = [ph.sb(k, [ROWS, 1]) for k in ("smax8", "smax", "nega", "M", "lnz", "acc")]
        need = ph.sb("need", [B, 1])
        spread, same, ident = ph.sb("spread", [B, B, 8]), ph.sb("same", [ROWS, B, 8]), ph.sb("ident", [P, P])
        psA, psB = ph.ps("psA"), ph.ps("psB")
        divider = sem("divider")
        setup, turned, chain, moved, zed, expd, lnd, dd = [sem(k) for k in (
            "setup", "turned", "chain", "moved", "zed", "expd", "lnd", "dd")]
        block = ph.block()

        @block.gpsimd
        def _(g):
            emit_identity(nc, g, ident, setup)
            g.memset(spread[:, :, :], 0.0)
            g.memset(same[:, :, :], 1.0)
            g.memset(zeros[:, :], 0.0).then_inc(setup, 1)
            g.wait_ge(setup, 3)
            g.affine_select(out=spread[:, :, :], in_=spread[:, :, :], compare_op=ALU.not_equal, fill=1.0, base=0,
                            pattern=[[-1, B], [0, 8]], channel_multiplier=1)
            g.affine_select(out=same[:, :, :], in_=same[:, :, :], compare_op=ALU.is_ge, fill=0.0, base=0,
                            pattern=[[-8, B], [0, 8]], channel_multiplier=1).then_inc(setup, 1)
            g.wait_ge(setup, 4)
            g.affine_select(out=same[:, :, :], in_=same[:, :, :], compare_op=ALU.is_ge, fill=0.0, base=7,
                            pattern=[[8, B], [0, 8]], channel_multiplier=-1).then_inc(setup, 1)

        @block.tensor
        def _(t_):
            t_.wait_ge(setup, 5)
            nc.tensor.transpose(psA[0:ROWS, 0:P], s_all[:, :], ident[:, :]).then_inc(turned, 1)
            t_.wait_ge(chain, 2)
            nc.tensor.matmul(psB[0:ROWS, 0:1], spread[:, :, :].rearrange("b c j -> b (c j)"), smax8[0:B, :],
                             start=True, stop=True).then_inc(turned, 1)
            with t_.Fori(0, DESCENTS - 1) as i:
                wait_apart(t_, divider, (expd, i + 1))
                nc.tensor.matmul(psA[0:ROWS, 256:257], same[:, :, :].rearrange("b c j -> b (c j)"), acc[:, :],
                                 start=True, stop=True).then_inc(zed, 1)
            t_.wait_ge(moved, 48)
            nc.tensor.transpose(psB[:, 128:128 + ROWS], coef64[:, :], ident[0:ROWS, 0:ROWS]).then_inc(turned, 1)

        @block.scalar
        def _(a_):
            with a_.Fori(0, DESCENTS - 1) as i:
                a_.wait_ge(dd, 3 * i + 3)
                nc.scalar.activation(e64[:, :], t64[:, :], ACT.Exp, accum_out=acc[:, :]).then_inc(expd, 1)
                a_.wait_ge(zed, i + 1)
                nc.scalar.activation(lnz[:, :], psA[0:ROWS, 256:257], ACT.Ln).then_inc(lnd, 1)
            a_.wait_ge(moved, 32)
            nc.scalar.activation(sc8[:, :], key8[:, :], ACT.Exp).then_inc(expd, 1)

        @block.sync
        def _(sp):
            sp.wait_ge(chain, 1)
            sp.dma_start(s8[:, :], s64[:, :]).then_inc(moved, 16)
            sp.wait_ge(chain, 5)
            sp.dma_start(key8[:, :], key64[:, :]).then_inc(moved, 16)
            sp.wait_ge(lnd, DESCENTS)
            sp.dma_start(coef64[:, :], gt8[:, :]).then_inc(moved, 16)

        @block.vector
        def _(v):
            c = Count(chain, 0)

            def link(ins):
                c.inc(ins)
                c.wait(v)

            v.wait_ge(turned, 1)
            link(nc.vector.tensor_copy(s64[:, :], psA[0:ROWS, 0:P]))
            v.wait_ge(moved, 16)
            link(nc.vector.tensor_reduce(smax8[0:B, :], s8[:, :], AX.X, ALU.max))
            v.wait_ge(turned, 2)
            link(nc.vector.tensor_copy(smax[:, :], psB[0:ROWS, 0:1]))
            nc.vector.memset(nega[:, :], math.log(S) - LOGK).then_inc(dd, 1)
            with v.Fori(0, DESCENTS - 1) as i:
                v.wait_ge(dd, 3 * i + 1)
                nc.vector.tensor_tensor(M[:, :], smax[:, :], nega[:, :], ALU.min).then_inc(dd, 1)
                v.wait_ge(dd, 3 * i + 2)
                nc.vector.tensor_scalar(t64[:, :], s64[:, :], nega[:, 0:1], M[:, 0:1], ALU.min, ALU.subtract)\
                    .then_inc(dd, 1)
                v.wait_ge(lnd, i + 1)
                nc.vector.scalar_tensor_tensor(out=nega[:, :], in0=lnz[:, :], scalar=-LOGK, in1=M[:, :],
                                               op0=ALU.add, op1=ALU.add).then_inc(dd, 1)
            v.wait_ge(dd, 3 * (DESCENTS - 1) + 1)
            link(nc.vector.tensor_scalar(key64[:, :], s64[:, :], nega[:, 0:1], 0.0, ALU.subtract, ALU.min))
            link(nc.vector.tensor_scalar(key64[:, :], key64[:, :], -104.0, None, ALU.max))
            v.wait_ge(moved, 32)
            cur = key8
            for r in range(TOP // 8):
                link(nc.vector.max(top8[:, :], cur[:, :]))
                if r < TOP // 8 - 1:
                    link(nc.vector.match_replace(work[r % 2][:, :], top8[:, :], cur[:, :], -1.0e30))
                    cur = work[r % 2]
            bar = top8[:, 7:8]
            link(nc.vector.tensor_scalar(gt8[:, :], key8[:, :], bar, None, ALU.is_gt))
            link(nc.vector.tensor_scalar(eq8[:, :], key8[:, :], bar, None, ALU.is_equal))
            link(nc.vector.tensor_reduce(need[:, :], gt8[:, :], AX.X, ALU.add))
            link(nc.vector.tensor_scalar(need[:, :], need[:, :], -1.0, float(TOP), ALU.mult, ALU.add))
            link(nc.vector.tensor_tensor_scan(cum8[:, :], eq8[:, :], zeros[:, :], 0.0, ALU.add, ALU.add))
            link(nc.vector.scalar_tensor_tensor(out=eq8[:, :], in0=cum8[:, :], scalar=need[:, 0:1], in1=eq8[:, :],
                                                op0=ALU.is_le, op1=ALU.mult))
            link(nc.vector.tensor_tensor(gt8[:, :], gt8[:, :], eq8[:, :], ALU.add))
            v.wait_ge(expd, DESCENTS)
            link(nc.vector.tensor_scalar(eq8[:, :], sc8[:, :], -1.0, 1.0, ALU.mult, ALU.add))
            link(nc.vector.tensor_tensor(eq8[:, :], eq8[:, :], sc8[:, :], ALU.add))
            nc.vector.tensor_tensor(gt8[:, :], gt8[:, :], eq8[:, :], ALU.mult).then_inc(lnd, 1)
            v.wait_ge(turned, 3)
            nc.vector.tensor_copy(coef_all[:, :], psB[:, 128:128 + ROWS]).then_inc(dd, 1)


def last_phase(nc, sem, base_dram, heavy_dram, coef_all, out_dram):
    with Phase(nc, "last") as ph:
        base = [ph.sb(f"b{s}", [P, GT, D]) for s in range(2)]
        hv = [ph.sb(f"h{s}", [P, GT, D]) for s in range(2)]
        out = [ph.sb(f"o{s}", [P, GT, D]) for s in range(2)]
        loaded = [sem(f"loaded{s}") for s in range(2)]
        stored = [sem(f"stored{s}") for s in range(2)]
        summed = sem("summed")
        block = ph.block()

        @block.sync
        def _(sp):
            def load(n, s):
                sp.wait_ge(summed, n + 1)
                sp.dma_start(base[s][:, :, :], rows_of(base_dram, n)).then_inc(loaded[s], 16)
                sp.dma_start(hv[s][:, :, :], rows_of(heavy_dram, n)).then_inc(loaded[s], 16)

            skewed(sp.Fori, NG, [(load, 0)])

        @block.vector
        def _(v):
            v.sem_inc(summed, 2)

            def total(n, s):
                v.wait_ge(loaded[s], 32 * uses4(n, s, 2))
                v.wait_ge(stored[s], 16 * uses4(n, s, 2))
                for t in range(GT):
                    last = nc.vector.scalar_tensor_tensor(
                        out=out[s][:, t, :], in0=hv[s][:, t, :], scalar=coef_all[:, bass.ds(n * GT + t, 1)],
                        in1=base[s][:, t, :], op0=ALU.mult, op1=ALU.add)
                last.then_inc(summed, 1)

            skewed(v.Fori, NG, [(total, 0)])

        @block.scalar
        def _(a_):
            for s in range(2):
                a_.sem_inc(stored[s], 16)

            def store(n, s):
                a_.wait_ge(summed, n + 3)
                a_.dma_start(rows_of(out_dram, n), out[s][:, :, :]).then_inc(stored[s], 16)

            skewed(a_.Fori, NG, [(store, 0)])
            for s in range(2):
                a_.wait_ge(stored[s], 16 * (NG // 2 + 1))


def program(nc, x, i, out):
    U32 = mybir.dt.uint32
    phase_name, used = [""], []

    def sem(name):
        used.append(nc.alloc_semaphore(name=f"{phase_name[0]}_{name}"))
        return used[-1]

    def give_back():
        nc.clear_and_free_semaphores(used)
        nc.all_engine_barrier()
        used.clear()

    if True:

        def dram(name, shape, dt=F32):
            return nc.dram_tensor(name, shape, dt, kind="Internal").ap()

        qd, kd = [dram(k, [H, SPLIT_ROWS, T], BF16) for k in ("q_parts", "k_parts")]
        vd, att = dram("values", [T, D]), dram("attention", [T, D])
        x1, xn, x2, x3 = dram("x1", [T, D]), dram("xn", [T, D]), dram("x2", [T, D]), dram("x3", [T, D])
        xsorted, ysorted = dram("x_sorted", [SORTED_TILES * P, D]), dram("y_sorted", [SORTED_TILES * P, D])
        fwd, rev = dram("bias_fwd", [H, 2 * WINDOW]), dram("bias_rev", [H, 2 * WINDOW])

        phase_name[0] = "qkv0"
        qkv_phase(nc, sem, "qkv0", x, i["L0_attn_w_qkv"], HD ** -0.5, qd, kd, vd)
        phase_name[0] = "att0"
        attention_phase(nc, sem, "att0", qd, kd, vd, att, True)
        with ExitStack() as moe:
            def keep(name, shape, dt=F32):
                return moe.enter_context(nc.sbuf_tensor(name, shape, dt))
            onehot, weight = keep("onehot", [P, NT, NE]), keep("weight", [P, NT])
            place, expert_row = keep("place", [P, NT], U32), keep("expert_row", [P, SORTED_TILES], I32)
            phase_name[0] = "mix"
            mix_phase(nc, sem, x, att, i["L0_attn_w_out"], i["L0_ffn_gate_w"], x1, xn, onehot, weight)
            phase_name[0] = "place"
            place_phase(nc, sem, onehot, place, expert_row)
            phase_name[0] = "scatter"
            scatter_phase(nc, sem, xn, xsorted, place)
            phase_name[0] = "experts"
            experts_phase(nc, sem, xsorted, ysorted, i["L0_ffn_w1"], i["L0_ffn_b1"], i["L0_ffn_w2"], i["L0_ffn_b2"],
                          expert_row)
            phase_name[0] = "gather"
            gather_phase(nc, sem, x1, ysorted, place, weight, x2)
        give_back()
        phase_name[0] = "bias"
        bias_phase(nc, sem, i["L1_attn_offsets"], i["L1_attn_pos_bias"], fwd, rev)
        phase_name[0] = "qkv1"
        qkv_phase(nc, sem, "qkv1", x2, i["L1_attn_w_qkv"], HD ** -0.5, qd, kd, vd, i["L1_attn_norm1_scale"])
        phase_name[0] = "att1"
        attention_phase(nc, sem, "att1", qd, kd, vd, att, False, rev, fwd)
        phase_name[0] = "gated"
        gated_phase(nc, sem, x2, att, i["L1_attn_w_gate"], i["L1_attn_b_gate"], i["L1_attn_norm1_scale"],
                    i["L1_attn_w_out"], x1, xn)
        phase_name[0] = "swiglu"
        swiglu_phase(nc, sem, xn, x1, i["L1_attn_norm2_scale"], i["L1_attn_w_ffn_gate"], i["L1_attn_w_ffn_up"],
                     i["L1_attn_w_ffn_down"], x3)
        with ExitStack() as route:
            s_all = route.enter_context(nc.sbuf_tensor("s_all", [P, NT], F32))
            coef = route.enter_context(nc.sbuf_tensor("coef", [P, NT], F32))
            phase_name[0] = "two"
            two_branch_phase(nc, sem, x3, i["L1_ffn_routing_token"],
                             [i[f"L1_ffn_light_{k}"] for k in ("gamma", "w1", "b1", "w2", "b2")],
                             [i[f"L1_ffn_heavy_{k}"] for k in ("gamma", "w1", "b1", "w2", "b2")], x1, x2, s_all)
            phase_name[0] = "descent"
            descent_phase(nc, sem, s_all, coef)
            phase_name[0] = "last"
            last_phase(nc, sem, x1, x2, coef, out)


def kernel(**inputs):
    import numpy as np
    import concourse.bacc as bacc
    from concourse.bass_utils import run_bass_kernel_spmd

    nc = bacc.Bacc("TRN2", target_bir_lowering=False, num_devices=1)
    arrays, given = {}, {}
    for name, a in inputs.items():
        a = np.ascontiguousarray(a)
        if name == "L0_attn_x":
            a = a.reshape(T, D)
        arrays[f"in_{name}"] = a
        given[name] = nc.dram_tensor(f"in_{name}", a.shape, mybir.dt.from_np(a.dtype), kind="ExternalInput").ap()
    out = nc.dram_tensor("out", (T, D), F32, kind="ExternalOutput").ap()
    program(nc, given["L0_attn_x"], given, out)
    r = run_bass_kernel_spmd(nc, [arrays], core_ids=[0])
    return r.results[0]["out"].reshape(B, S, D)
```

```python
from contextlib import ExitStack
import math

import concourse.bass as bass
from concourse import mybir

F32 = mybir.dt.float32
BF16 = mybir.dt.bfloat16
I32 = mybir.dt.int32
ACT = mybir.ActivationFunctionType
ALU = mybir.AluOpType
AX = mybir.AxisListType

P = 128
B, S, D = 8, 1024, 128
T = B * S
H, HD = 16, 8
TB = S // P
NT = T // P
GT = 4
GW = GT * P
NG = T // GW
HG = 4
NHG = H // HG
SPLIT_ROWS = 6 * HD
PAD_ROWS = 96
ALL_ROWS = PAD_ROWS + 3
Q_RUNS = ((0, 2), (0, 1), (0, 0))
K_RUNS = ((0, 0), (0, 0), (0, 0), (1, 1), (1, 1), (2, 2))
MASKED = -1.0e30
NE, FF = 8, 512
NOFF = 38
WINDOW = 256
WB = WINDOW // P + 1
FFN1 = 352
F_CHUNKS = ((0, 128), (128, 128), (256, 96))
LN_EPS, RMS_EPS = 1e-5, 1e-6
TINY = 1e-24 / D


class Count:

    def __init__(self, sem, per, credits=0):
        self.sem, self.per, self.credits, self.base, self.c = sem, per, credits, 0, 0

    def start(self, n):
        self.base, self.c = (n + self.credits) * self.per, 0

    def inc(self, ins, k=1):
        ins.then_inc(self.sem, k)
        self.c += k

    def wait(self, eng):
        eng.wait_ge(self.sem, self.base + self.c)

    def wait_apart(self, eng, divider):
        wait_apart(eng, divider, (self.sem, self.base + self.c))

    def end(self):
        assert self.c == self.per, (self.c, self.per)


class Phase:

    def __init__(self, nc, name):
        self.nc, self.name, self.ctx = nc, name, ExitStack()

    def __enter__(self):
        self.ctx.__enter__()
        return self

    def __exit__(self, *a):
        return self.ctx.__exit__(*a)

    def sb(self, name, shape, dt=F32):
        return self.ctx.enter_context(self.nc.sbuf_tensor(f"{self.name}_{name}", shape, dt))

    def ps(self, name, shape=(P, 512), dt=F32):
        return self.ctx.enter_context(self.nc.psum_tensor(f"{self.name}_{name}", list(shape), dt))

    def block(self):
        return self.ctx.enter_context(self.nc.Block())


def wait_apart(eng, divider, *waits):
    for sem, value in waits:
        eng.wait_ge(sem, value)
    eng.sem_inc(divider, 1)


def rows_of(dram, n):
    return dram[bass.ds(n * GW, GW), :].rearrange("(t p) c -> p t c", p=P)


def bc_rows(vec, width):
    return bass.AP(tensor=vec.tensor, offset=vec.offset, ap=[[0, P], [1, width]])


def emit_identity(nc, eng, ident, sem):
    eng.memset(ident[:, :], 0.0).then_inc(sem, 1)
    eng.wait_ge(sem, 1)
    eng.affine_select(out=ident[:, :], in_=ident[:, :], compare_op=ALU.not_equal, fill=1.0, base=0,
                      pattern=[[-1, P]], channel_multiplier=1).then_inc(sem, 1)


def emit_stats(nc, v, ch, x, st, mv, divider):
    for t in range(GT):
        ch.inc(nc.vector.bn_stats(st[:, t, :], x[:, t, :]))
    ch.wait_apart(v, divider)
    for t in range(GT):
        ch.inc(nc.vector.bn_aggr(mv[:, t, :], st[:, t, :]))


def emit_rstd(nc, g, ch, mv, rstd, power, divider, eps=LN_EPS, rms=None):
    ch.inc(nc.gpsimd.tensor_scalar(rstd[:, :], mv[:, :, 1], eps, None, ALU.add))
    ch.wait(g)
    ch.inc(nc.gpsimd.tensor_tensor(rstd[:, :], rstd[:, :], power[:, :], ALU.pow))
    if rms is not None:
        rms_eps, r = rms
        ch.wait(g)
        ch.inc(nc.gpsimd.tensor_tensor(r[:, :], mv[:, :, 1], rstd[:, :], ALU.mult))
        ch.wait(g)
        ch.inc(nc.gpsimd.tensor_tensor(r[:, :], r[:, :], rstd[:, :], ALU.mult))
        ch.wait_apart(g, divider)
        if rms_eps is None:
            ch.inc(nc.gpsimd.tensor_scalar(r[:, :], r[:, :], TINY, None, ALU.max))
        else:
            ch.inc(nc.gpsimd.tensor_scalar(r[:, :], r[:, :], rms_eps, None, ALU.add))
        ch.wait(g)
        ch.inc(nc.gpsimd.tensor_tensor(r[:, :], r[:, :], power[:, :], ALU.pow))


RSTD_STEPS, RMS_STEPS = 2, 6


def emit_apply(nc, ch, x, y, mv, rstd):
    for t in range(GT):
        ch.inc(nc.vector.tensor_scalar(y[:, t, :], x[:, t, :], mv[:, t, 0:1], rstd[:, t:t + 1],
                                       ALU.subtract, ALU.mult))


STATS_STEPS = 2 * GT


def qkv_phase(nc, sem, name, x_dram, w_qkv, q_scale, qd, kd, vd, norm_scale=None):
    rms = norm_scale is not None
    with Phase(nc, name) as ph:
        x_in = [ph.sb(f"x{s}", [P, GT, D]) for s in range(4)]
        xn = [ph.sb(f"xn{s}", [P, GT, D]) for s in range(2)]
        xr = [ph.sb(f"xr{s}", [P, GT, D]) for s in range(2)] if rms else xn
        xnT = [ph.sb(f"xnT{s}", [P, GW]) for s in range(2)]
        st = [ph.sb(f"st{s}", [P, GT, 6]) for s in range(2)]
        mv = [ph.sb(f"mv{s}", [P, GT, 2]) for s in range(2)]
        rstd = [ph.sb(f"rstd{s}", [P, GT]) for s in range(2)]
        rr = [ph.sb(f"rr{s}", [P, GT]) for s in range(2)]
        power = ph.sb("power", [P, GT])
        w = ph.sb("w", [P, 3 * D])
        ident = ph.sb("ident", [P, P])
        nscale = ph.sb("nscale", [P, 1])
        parts = [[ph.sb(f"part{s}{a}", [P, 3, GW], BF16) for a in range(2)] for s in range(2)]
        rest = [[ph.sb(f"rest{s}{a}", [P, GW]) for a in range(2)] for s in range(2)]
        v_out = [ph.sb(f"v{s}", [P, GT, D]) for s in range(2)]
        ps_t = [ph.ps(f"pst{s}") for s in range(2)]
        ps_q = [[ph.ps(f"psq{s}{a}") for a in range(2)] for s in range(2)]
        ps_v = [ph.ps(f"psv{s}") for s in range(2)]

        setup, divider = sem("setup"), sem("divider")
        w_ready = sem("w_ready")
        w_scaled = sem("w_scaled")
        x_loaded = [sem(f"x_loaded{s}") for s in range(4)]
        norm_chain = sem("norm_chain")
        t_done = sem("t_done")
        xnT_ready = sem("xnT_ready")
        qk_done = sem("qk_done")
        v_done = sem("v_done")
        high_ready = sem("high_ready")
        v_copied = sem("v_copied")
        split_chain = sem("split_chain")
        parts_stored = [sem(f"parts_stored{s}") for s in range(2)]
        v_stored = [sem(f"v_stored{s}") for s in range(2)]
        n_consts = 32 if rms else 16
        NSTORE = 16 * 6
        KN = 2 * GT if rms else GT
        KR = RMS_STEPS if rms else RSTD_STEPS
        rstd_chain = sem("rstd_chain")
        stats_chain = sem("stats_chain")
        SPLIT_STEPS = 5

        block = ph.block()

        @block.gpsimd
        def _(g):
            emit_identity(nc, g, ident, setup)
            g.memset(power[:, :], -0.5).then_inc(setup, 1)
            g.wait_ge(setup, 3)
            rc = Count(rstd_chain, KR)

            def rstds(n, quarter):
                s = quarter % 2
                wait_apart(g, divider, (stats_chain, (n + 1) * STATS_STEPS), (norm_chain, (n + 3) * KN))
                rc.start(n)
                emit_rstd(nc, g, rc, mv[s], rstd[s], power, divider, rms=(RMS_EPS, rr[s]) if rms else None)
                rc.end()

            skewed4(g.Fori, NG, [(rstds, 1)])

        @block.sync
        def _(sp):
            sp.dma_start(w[:, :], w_qkv).then_inc(w_ready, 16)
            if rms:
                sp.dma_start(nscale[:, :], norm_scale.rearrange("(c a) -> c a", a=1)).then_inc(w_ready, 16)

            def load(n, quarter):
                sp.wait_ge(norm_chain, (n + 1) * KN)
                sp.dma_start(x_in[quarter][:, :, :], rows_of(x_dram, n)).then_inc(x_loaded[quarter], 16)

            def store(n, quarter):
                s = quarter % 2
                sp.wait_ge(split_chain, (n + 1) * SPLIT_STEPS)
                for a, dst in enumerate((qd, kd)):
                    for part in range(3):
                        sp.dma_start(dst[:, part * HD:(part + 1) * HD, bass.ds(n * GW, GW)],
                                     parts[s][a][:, part, :]).then_inc(parts_stored[s], 16)

            skewed4(sp.Fori, NG, [(store, 4), (load, 0)])
            for s in range(2):
                sp.wait_ge(parts_stored[s], NSTORE * (NG // 2 + 1))

        @block.vector
        def _(v):
            v.sem_inc(norm_chain, 4 * KN)
            sc0 = Count(stats_chain, STATS_STEPS)
            ch = Count(norm_chain, KN, 4)
            sc = Count(split_chain, SPLIT_STEPS)
            v.wait_ge(w_ready, n_consts)
            nc.vector.tensor_scalar(w[:, 0:D], w[:, 0:D], q_scale, None, ALU.mult).then_inc(w_scaled, 1)

            def stats(n, quarter):
                s = quarter % 2
                sc0.start(n)
                v.wait_ge(x_loaded[quarter], 16 * uses4(n, quarter))
                emit_stats(nc, v, sc0, x_in[quarter], st[s], mv[s], divider)
                sc0.end()

            def norm(n, quarter):
                s = quarter % 2
                ch.start(n)
                v.wait_ge(rstd_chain, (n + 1) * KR)
                v.wait_ge(t_done, n + 1)
                emit_apply(nc, ch, x_in[quarter], xn[s], mv[s], rstd[s])
                if rms:
                    ch.wait(v)
                    for t in range(GT):
                        ins = nc.vector.tensor_scalar(xr[s][:, t, :], xn[s][:, t, :], rr[s][:, t:t + 1], None, ALU.mult)
                        ch.inc(ins)
                ch.end()

            def split(n, quarter):
                s = quarter % 2
                sc.start(n)
                v.wait_ge(high_ready, 2 * n + 2)
                v.wait_ge(parts_stored[s], NSTORE * uses4(n, s, 2))
                for a in range(2):
                    sc.inc(nc.vector.tensor_tensor(rest[s][a][:, :], ps_q[s][a][:, :], parts[s][a][:, 0, :],
                                                   ALU.subtract))
                sc.wait(v)
                for a in range(2):
                    sc.inc(nc.vector.tensor_copy(parts[s][a][:, 1, :], rest[s][a][:, :]))
                sc.wait(v)
                nc.vector.tensor_tensor(parts[s][0][:, 2, :], rest[s][0][:, :], parts[s][0][:, 1, :], ALU.subtract)
                sc.inc(nc.vector.tensor_tensor(parts[s][1][:, 2, :], rest[s][1][:, :], parts[s][1][:, 1, :],
                                               ALU.subtract))
                sc.end()

            skewed4(v.Fori, NG, [(split, 4), (norm, 2), (stats, 1)])

        @block.scalar
        def _(a_):
            a_.wait_ge(w_ready, n_consts)

            a_.sem_inc(xnT_ready, 2)
            a_.sem_inc(v_copied, 2)

            def copies(n, quarter):
                s = quarter % 2
                a_.wait_ge(t_done, n + 3)
                a_.wait_ge(v_done, n + 1)
                if rms:
                    nc.scalar.activation(xnT[s][:, :], ps_t[s][:, :], ACT.Copy, scale=nscale[:, 0:1])\
                        .then_inc(xnT_ready, 1)
                else:
                    nc.scalar.activation(xnT[s][:, :], ps_t[s][:, :], ACT.Copy).then_inc(xnT_ready, 1)
                a_.wait_ge(parts_stored[s], NSTORE * uses4(n, s, 2))
                for a in range(2):
                    a_.wait_ge(qk_done, 2 * n + a + 1)
                    nc.scalar.activation(parts[s][a][:, 0, :], ps_q[s][a][:, :], ACT.Copy).then_inc(high_ready, 1)
                a_.wait_ge(v_done, n + 3)
                a_.wait_ge(v_stored[s], 16 * uses4(n, s, 2))
                nc.scalar.activation(v_out[s][:, :, :], ps_v[s][:, :].rearrange("p (t c) -> p t c", t=GT),
                                     ACT.Copy).then_inc(v_copied, 1)
                a_.wait_ge(v_copied, n + 3)
                a_.dma_start(rows_of(vd, n), v_out[s][:, :, :]).then_inc(v_stored[s], 16)

            skewed4(a_.Fori, NG, [(copies, 3)])
            for s in range(2):
                a_.wait_ge(v_stored[s], 16 * (NG // 2 + 1))

        @block.tensor
        def _(t_):
            t_.sem_inc(t_done, 2)
            t_.sem_inc(v_done, 2)
            for s in range(2):
                t_.sem_inc(v_stored[s], 16)
                t_.sem_inc(parts_stored[s], NSTORE)
            t_.wait_ge(setup, 2)
            t_.wait_ge(w_scaled, 1)

            def transposes(n, quarter):
                s = quarter % 2
                t_.wait_ge(norm_chain, (n + 5) * KN)
                t_.wait_ge(xnT_ready, n + 1)
                for t in range(GT):
                    last = nc.tensor.transpose(ps_t[s][:, t * P:(t + 1) * P], xr[s][:, t, :], ident[:, :])
                last.then_inc(t_done, 1)

            def products(n, quarter):
                s = quarter % 2
                t_.wait_ge(xnT_ready, n + 3)
                t_.wait_ge(parts_stored[s], NSTORE * uses4(n, s, 2))
                for a in range(2):
                    nc.tensor.matmul(ps_q[s][a][:, :], w[:, a * D:(a + 1) * D], xnT[s][:, :], start=True, stop=True)\
                        .then_inc(qk_done, 1)
                t_.wait_ge(v_copied, n + 1)
                for t in range(GT):
                    last = nc.tensor.matmul(ps_v[s][:, t * D:(t + 1) * D], xnT[s][:, t * P:(t + 1) * P],
                                            w[:, 2 * D:3 * D], start=True, stop=True)
                last.then_inc(v_done, 1)

            skewed4(t_.Fori, NG, [(products, 3), (transposes, 2)])


class Attention:

    def __init__(self, causal):
        self.causal = causal
        self.tiles = []
        for qb in range(TB):
            if not causal:
                k0 = max(0, qb - WB + 1)
                self.tiles += [(h, qb, k0 * P, (qb + 1 - k0) * P, True) for h in range(HG)]
            elif qb < 4:
                self.tiles += [(h, qb, 0, (qb + 1) * P, True) for h in range(HG)]
            else:
                self.tiles += [(h, qb, 0, 4 * P, False) for h in range(HG)]
                self.tiles += [(h, qb, 4 * P, (qb - 3) * P, True) for h in range(HG)]
        self.slots = []
        if causal:
            for half in range(2):
                for kb in range(4 * half + 4):
                    q0 = max(512 * half, P * kb)
                    for pair in range(2):
                        self.slots.append((kb, pair, q0, 512 * (half + 1) - q0))
        else:
            for kb in range(TB):
                q0 = kb * P
                for pair in range(2):
                    self.slots.append((kb, pair, q0, min(WB * P, S - q0)))
        self.masked = [k for k, (kb, _, q0, _) in enumerate(self.slots) if causal and q0 == kb * P]
        self.bank_end = [max(k for k, sl in enumerate(self.slots) if self.banks(sl)[b]) for b in range(2)]
        self.bank_start = [min(k for k, sl in enumerate(self.slots) if self.banks(sl)[b]) for b in range(2)]
        self.n_tiles, self.n_slots = len(self.tiles), len(self.slots)
        assert self.n_tiles % 2 == 0 and self.n_slots % 4 == 0
        self.last = self.n_slots - (10 if causal else 4)
        self.turn = self.last + (3 if causal else 1)
        starts = [sum(sl[3] for sl in self.slots[:k]) for k in range(self.n_slots + 1)]
        first, whole = starts[self.turn], starts[-1]
        room = whole - (first - starts[self.last + 1])
        total = sum(t[3] for t in self.tiles)
        self.late, self.early = [[[] for _ in self.slots] for _ in range(2)]
        done = 0
        for j, t in enumerate(self.tiles):
            at = first + room * done / total
            which, at = (self.late, at) if at < whole else (self.early, at - whole)
            which[max(k for k in range(self.n_slots) if starts[k] <= at)].append(j)
            done += t[3]

    @staticmethod
    def banks(slot):
        _, _, q0, n = slot
        out = []
        for b in range(2):
            lo, hi = max(q0, 512 * b), min(q0 + n, 512 * (b + 1))
            out.append((lo, hi) if lo < hi else None)
        return out


TABLE_PARTS = tuple((src, half) for src in range(2) for half in range(2))


def attention_phase(nc, sem, name, qd, kd, vd, att_dram, causal, bias_k=None, bias_q=None):
    plan = Attention(causal)
    pv_lag, p_bufs = (5, 8) if causal else (3, 4)
    NTL, NSL = plan.n_tiles, plan.n_slots
    TILES = NTL + 2
    NMASK = len(plan.masked)
    NGR = B * NHG
    ML = 4
    with Phase(nc, name) as ph:
        Q = [ph.sb(f"Q{g}", [P, HG, S], BF16) for g in range(NHG)]
        K = [ph.sb(f"K{g}", [P, HG, S], BF16) for g in range(NHG)]
        v_in = ph.sb("v", [P, TB, D])
        V = [ph.sb(f"V{s}", [P, TB, HG, 32]) for s in range(2)]
        probs = [ph.sb(f"probs{s}", [P, 2, 512]) for s in range(p_bufs)]
        O = [ph.sb(f"O{b}", [P, 512]) for b in range(2)]
        att = ph.sb("att", [P, TB, D])
        rec = [ph.sb(f"rec{b}", [P, GT, HG, 1]) for b in range(2)]
        part_max = ph.sb("part_max", [P, HG])
        mx = ph.sb("mx", [P, HG, TB])
        mrest = ph.sb("mrest", [P, HG * TB])
        mparts = ph.sb("mparts", [P, 3, HG * TB], BF16)
        mT = ph.sb("mT", [3 * HG * TB, P], BF16)
        ident = ph.sb("ident", [P, P])
        identb = ph.sb("identb", [P, P], BF16)
        if causal:
            mask = ph.sb("mask", [P, 512])
        else:
            tab_k = ph.sb("tab_k", [P, H, WB * P])
            tab_q = ph.sb("tab_q", [P, H, WB * P])
            raw = [ph.sb(f"raw{s}", [P, H // 2, WB * P]) for s in range(2)]
            raw_loaded = [sem(f"raw_loaded{s}") for s in range(2)]
        ps1 = [ph.ps(f"ps1{s}") for s in range(2)]
        ps2 = [ph.ps(f"ps2{s}", [P, 2, 512]) for s in range(2)]
        psO = [ph.ps(f"psO{b}") for b in range(2)]
        psT = ps1[0][:, 0:P // 2].bitcast(BF16)

        setup, divider = sem("setup"), sem("divider")
        pads = [sem(f"pads{g}") for g in range(NHG)]
        identb_ready = sem("identb_ready")
        tabs = sem("tabs")
        qk_loaded = [sem(f"qk_loaded{g}") for g in range(NHG)]
        v_loaded = sem("v_loaded")
        v_spread = sem("v_spread")
        t1_done = sem("t1_done")
        t1_read = sem("t1_read")
        m_chain = sem("m_chain")
        m_sent = [sem(f"m_sent{g}") for g in range(NHG)]
        s2_done = sem("s2_done")
        s2_read = sem("s2_read")
        exp_done = sem("exp_done")
        masked = sem("masked")
        pv_done = sem("pv_done")
        o_copied = sem("o_copied")
        oT_done = sem("oT_done")
        o_chain = sem("o_chain")
        att_stored = sem("att_stored")
        NSET = 4
        block = ph.block()

        def pad(eng, g):
            fills = [(t[g][part, :, :], 0.0) for part in (slice(32, 64), slice(64, 96)) for t in (Q, K)]
            for i, (dst, value) in enumerate(fills + [(K[g][PAD_ROWS:P, :, :], 1.0)]):
                eng.memset(dst, value).then_inc(pads[g], 1)
                eng.wait_ge(pads[g], i + 1)

        @block.sync
        def _(sp):
            sp.sem_inc(att_stored, 16)
            sp.wait_ge(setup, NSET)
            if not causal:
                for i, (src, half) in enumerate(TABLE_PARTS):
                    if i >= 2:
                        sp.wait_ge(tabs, i - 1)
                    sp.dma_start(raw[half][:, :, :], shifted_rows((bias_k, bias_q)[src], half * H // 2, H // 2))\
                        .then_inc(raw_loaded[half], 16)

            def load(n, b, g):
                sp.wait_ge(pv_done, NSL * (n + 1))
                sp.wait_ge(pads[g], 5)
                for dst, src, runs in ((Q[g], qd, Q_RUNS), (K[g], kd, K_RUNS)):
                    row = 0
                    for first, last in runs:
                        rows = (last + 1 - first) * HD
                        sp.dma_start(dst[row:row + rows, :, :],
                                     src[g * HG:(g + 1) * HG, first * HD:(last + 1) * HD, bass.ds(b * S, S)]
                                     .rearrange("h r t -> r h t")).then_inc(qk_loaded[g], 16)
                        row += rows

            def load_v(b):
                sp.wait_ge(v_spread, NHG * (b + 1))
                sp.dma_start(v_in[:, :, :], vd[bass.ds(b * S, S), :].rearrange("(t p) c -> p t c", p=P))\
                    .then_inc(v_loaded, 16)

            def store(b):
                sp.wait_ge(o_chain, 4 * (NHG * b + NHG) + 4)
                sp.dma_start(att_dram[bass.ds(b * S, S), :].rearrange("(t p) c -> p t c", p=P), att[:, :, :])\
                    .then_inc(att_stored, 16)

            def body(b, first=False, last=False):
                for g in range(NHG):
                    n = NHG * b + g
                    sp.wait_ge(t1_read, (n + 1) * TILES + 2)
                    for part in range(3):
                        sp.dma_start(Q[g][PAD_ROWS + part:PAD_ROWS + part + 1, :, :].rearrange("r h t -> r (h t)"),
                                     mT[part * HG * TB:(part + 1) * HG * TB, :]).then_inc(m_sent[g], 16)
                    if g == NHG - 1 and not last:
                        load_v(b + 1)
                    if not (last and g >= 1):
                        load(n + 3, b + (g + 3) // NHG, (g + 3) % NHG)
                    if g == 0 and not first:
                        store(b - 1)

            load(0, 0, 0)
            load_v(0)
            load(1, 0, 1)
            load(2, 0, 2)
            body(0, first=True)
            with sp.Fori(1, B - 1) as b:
                body(b)
            body(B - 1, last=True)
            store(B - 1)
            sp.wait_ge(att_stored, 16 * (B + 1))

        @block.gpsimd
        def _(g_):
            g_.sem_inc(v_spread, NHG)
            emit_identity(nc, g_, ident, setup)
            g_.memset(V[0][:, :, :, :], 0.0)
            g_.memset(V[1][:, :, :, :], 0.0).then_inc(setup, 1)
            g_.wait_ge(setup, 3)
            g_.memset(V[0][:, :, :, HD:HD + 1], 1.0)
            g_.memset(V[1][:, :, :, HD:HD + 1], 1.0).then_inc(setup, 1)
            if causal:
                g_.memset(mask[:, :], 0.0).then_inc(tabs, 1)
                g_.wait_ge(tabs, 1)
                g_.affine_select(out=mask[:, 512 - P:512], in_=mask[:, 512 - P:512], compare_op=ALU.is_ge,
                                 fill=MASKED, base=0, pattern=[[-1, P]], channel_multiplier=1).then_inc(tabs, 1)
            g_.wait_ge(setup, NSET)
            if causal:
                g_.wait_ge(tabs, 2)
            for g in range(1, NHG):
                pad(nc.gpsimd, g)
            with g_.Fori(0, B) as b:
                g_.wait_ge(v_loaded, 16 * (b + 1))
                for g in range(NHG):
                    n = NHG * b + g
                    wait_apart(g_, divider, (pv_done, NSL * (n + 3)))
                    nc.gpsimd.tensor_copy(V[g % 2][:, :, :, 0:HD],
                                          v_in[:, :, g * HG * HD:(g + 1) * HG * HD]
                                          .rearrange("p t (h d) -> p t h d", d=HD)).then_inc(v_spread, 1)
                    for k in plan.masked:
                        wait_apart(g_, divider, (exp_done, n * NSL + k + 3))
                        pt = probs[k % p_bufs]
                        nc.gpsimd.affine_select(out=pt[:, :, 0:P], in_=pt[:, :, 0:P], compare_op=ALU.is_ge,
                                                fill=0.0, base=0, pattern=[[0, 2], [1, P]],
                                                channel_multiplier=-1).then_inc(masked, 1)

        @block.scalar
        def _(a_):
            a_.sem_inc(exp_done, 2)
            if not causal:
                for i, (src, half) in enumerate(TABLE_PARTS):
                    a_.wait_ge(raw_loaded[half], 16 * (i // 2 + 1))
                    nc.scalar.activation((tab_k, tab_q)[src][:, half * H // 2:(half + 1) * H // 2, :],
                                         backwards(raw[half], H // 2), ACT.Copy).then_inc(tabs, 1)

            def copy_o(n, bank):
                a_.wait_ge(pv_done, NSL * (n + 4) + plan.bank_end[bank] + 1)
                a_.wait_ge(oT_done, 2 * n + bank + 1)
                nc.scalar.activation(O[bank][:, :], psO[bank][:, :], ACT.Copy).then_inc(o_copied, 1)

            def group(n, first=False):
                for k, (kb, pair, q0, w) in enumerate(plan.slots):
                    if causal:
                        a_.wait_ge(s2_done, n * NSL + k + 1)
                    else:
                        a_.wait_ge(s2_read, n * NSL + k + 3)
                    a_.wait_ge(pv_done, NSL * (n + 4) + k - p_bufs + 1)
                    pt = probs[k % p_bufs]
                    src = ps2[k % 2] if causal else pt
                    nc.scalar.activation(pt[:, :, 0:w], src[:, :, 0:w], ACT.Exp).then_inc(exp_done, 1)
                    if k == pv_lag and not first:
                        copy_o(n - 1, 1)
                    if k == plan.bank_end[0] + pv_lag:
                        copy_o(n, 0)

            group(0, first=True)
            with a_.Fori(0, B - 1) as b:
                for g in range(1, NHG + 1):
                    group(NHG * b + g)
            for g in range(1, NHG):
                group(NHG * (B - 1) + g)
            copy_o(NGR - 1, 1)

        @block.vector
        def _(v):
            v.sem_inc(t1_read, 2)
            v.sem_inc(s2_read, 2)
            v.sem_inc(o_chain, 4)
            pad(nc.vector, 0)
            v.wait_ge(setup, NSET)
            nc.vector.tensor_copy(identb[:, :], ident[:, :]).then_inc(identb_ready, 1)
            v.wait_ge(tabs, 2 if causal else len(TABLE_PARTS))
            mc = Count(m_chain, ML)

            def tile(n, g, j):
                h, qb, k0, w, with_mask = plan.tiles[j]
                wait_apart(v, divider, (t1_done, n * TILES + j + 1))
                src = ps1[j % 2]
                if not with_mask:
                    nc.vector.tensor_reduce(part_max[:, h:h + 1], src[:, 0:w], AX.X, ALU.max).then_inc(t1_read, 1)
                    return
                start = part_max[:, h:h + 1] if causal and k0 else 3 * MASKED
                table = mask[:, 512 - w:512] if causal else tab_q[:, g * HG + h, WB * P - w:WB * P]
                nc.vector.tensor_tensor_reduce(out=src[:, 0:w], in0=src[:, 0:w], in1=table, scale=1.0, scalar=start,
                                               op0=ALU.add, op1=ALU.max, accum_out=mx[:, h, qb:qb + 1])\
                    .then_inc(t1_read, 1)

            def maxima(n):
                mc.start(n)
                v.wait_ge(t1_read, n * TILES + NTL + 2)
                m2 = mx[:, :, :].rearrange("p h t -> p (h t)")
                mc.inc(nc.vector.tensor_scalar(mparts[:, 0, :], m2, -1.0, None, ALU.mult))
                mc.wait(v)
                mc.inc(nc.vector.scalar_tensor_tensor(out=mrest[:, :], in0=m2, scalar=-1.0, in1=mparts[:, 0, :],
                                                      op0=ALU.mult, op1=ALU.subtract))
                mc.wait(v)
                mc.inc(nc.vector.tensor_copy(mparts[:, 1, :], mrest[:, :]))
                mc.wait(v)
                mc.inc(nc.vector.tensor_tensor(mparts[:, 2, :], mrest[:, :], mparts[:, 1, :], ALU.subtract))
                mc.end()

            def copy_maxima(n, b, g):
                v.wait_ge(t1_done, n * TILES + NTL + 2)
                if g > 0:
                    v.wait_ge(m_sent[g - 1], 48 * (b + 1))
                elif not (isinstance(b, int) and b == 0):
                    v.wait_ge(m_sent[NHG - 1], 48 * b)
                nc.vector.tensor_copy(mT[:, :], psT[0:3 * HG * TB, :]).then_inc(t1_read, 2)

            def add_bias(n, g, k):
                kb, pair, q0, w = plan.slots[k]
                v.wait_ge(s2_done, n * NSL + k + 1)
                v.wait_ge(pv_done, NSL * (n + 4) + k - p_bufs + 1)
                h = g * HG + 2 * pair
                nc.vector.tensor_tensor(probs[k % p_bufs][:, :, 0:w], ps2[k % 2][:, :, 0:w], tab_k[:, h:h + 2, 0:w],
                                        ALU.add).then_inc(s2_read, 1)

            def norm(n, b, g, bank):
                v.wait_ge(oT_done, 2 * n + bank + 3)
                if g == 0 and bank == 0:
                    v.wait_ge(att_stored, 16 * (b + 1))
                src = psO[bank][:, :].rearrange("p (t h e) -> p t h e", t=GT, h=HG)
                nc.vector.reciprocal(rec[bank][:, :, :, :], src[:, :, :, HD:HD + 1]).then_inc(o_chain, 1)
                v.wait_ge(o_chain, 4 * (n + 1) + 2 * bank + 1)
                nc.vector.tensor_tensor(att[:, GT * bank:GT * (bank + 1), g * HG * HD:(g + 1) * HG * HD]
                                        .rearrange("p t (h d) -> p t h d", d=HD),
                                        src[:, :, :, 0:HD], rec[bank][:, :, :, :].to_broadcast([P, GT, HG, HD]),
                                        ALU.mult).then_inc(o_chain, 1)

            def group(this, nxt, later, prev):
                for k in range(NSL):
                    if not causal:
                        add_bias(this[0], this[2], k)
                    if nxt and k == plan.turn:
                        copy_maxima(*nxt)
                    for whose, tiles in ((nxt, plan.early[k]), (later, plan.late[k])):
                        for j in tiles if whose else ():
                            tile(whose[0], whose[2], j)
                    if nxt and k == plan.last:
                        maxima(nxt[0])
                    if prev and k == pv_lag + 2:
                        norm(*prev, 1)
                    if k == plan.bank_end[0] + pv_lag + 3:
                        norm(*this, 0)

            def before():
                for j in range(NTL):
                    tile(0, 0, j)
                maxima(0)
                copy_maxima(0, 0, 0)
                for j in range(sum(map(len, plan.late))):
                    tile(1, 1, j)

            walk(plan, B, group, before, after=lambda: norm(NGR - 1, B - 1, NHG - 1, 1), fori=v.Fori)

        @block.tensor
        def _(t_):
            t_.sem_inc(pv_done, 4 * NSL)
            t_.sem_inc(oT_done, 2)
            t_.wait_ge(setup, NSET)
            t_.wait_ge(identb_ready, 1)

            def tile(n, b, g, j):
                h, qb, k0, w, _ = plan.tiles[j]
                if j == 0:
                    t_.wait_ge(qk_loaded[g], 16 * (len(Q_RUNS) + len(K_RUNS)) * (b + 1))
                t_.wait_ge(t1_read, n * TILES + j + 1)
                nc.tensor.matmul(ps1[j % 2][:, 0:w], Q[g][0:PAD_ROWS, h, qb * P:(qb + 1) * P],
                                 K[g][0:PAD_ROWS, h, k0:k0 + w], start=True, stop=True).then_inc(t1_done, 1)

            def turn_maxima(n):
                t_.wait_ge(m_chain, ML * (n + 1))
                t_.wait_ge(t1_read, n * TILES + NTL + 1)
                nc.tensor.transpose(psT[0:3 * HG * TB, :], mparts[:, :, :].rearrange("p a b -> p (a b)"),
                                    identb[:, :]).then_inc(t1_done, 2)

            def score(n, b, g, k, hh):
                kb, pair, q0, w = plan.slots[k]
                if k == 0 and hh == 0:
                    t_.wait_ge(m_sent[g], 48 * (b + 1))
                if hh == 0:
                    t_.wait_ge(exp_done if causal else s2_read, n * NSL + k + 1)
                h = 2 * pair + hh
                last = nc.tensor.matmul(ps2[k % 2][:, hh, 0:w], K[g][0:ALL_ROWS, h, kb * P:(kb + 1) * P],
                                        Q[g][0:ALL_ROWS, h, q0:q0 + w], start=True, stop=True)
                if hh == 1:
                    last.then_inc(s2_done, 1)

            def values(n, g, k):
                kb, _, q0, w = plan.slots[k]
                if k in plan.masked:
                    t_.wait_ge(masked, n * NMASK + plan.masked.index(k) + 2)
                else:
                    t_.wait_ge(exp_done, n * NSL + k + 4)
                if k == 0:
                    t_.wait_ge(v_spread, n + NHG + 1)
                for bank in range(2):
                    if k == plan.bank_start[bank]:
                        t_.wait_ge(o_chain, 4 * n + 2 * (bank + 1))
                for bank, part in enumerate(plan.banks(plan.slots[k])):
                    if part is None:
                        continue
                    for h in range(HG):
                        last = nc.tensor.matmul(psO[bank][32 * h:32 * h + 32, part[0] - 512 * bank:part[1] - 512 * bank],
                                                V[g % 2][:, kb, h, :],
                                                probs[(k + h // 2) % p_bufs][:, h % 2, part[0] - q0:part[1] - q0],
                                                start=(k == plan.bank_start[bank]),
                                                stop=(k == plan.bank_end[bank] - 1), skip_group_check=True)
                last.then_inc(pv_done, 2)

            def turn_outputs(n, bank):
                t_.wait_ge(o_copied, 2 * n + bank + 1)
                for t in range(GT):
                    last = nc.tensor.transpose(psO[bank][:, t * P:(t + 1) * P], O[bank][:, t * P:(t + 1) * P],
                                               ident[:, :])
                last.then_inc(oT_done, 1)

            def group(this, nxt, later, prev):
                n, b, g = this
                for k in range(NSL):
                    tiles = [(nxt, j) for j in plan.early[k]] if nxt else []
                    tiles += [(later, j) for j in plan.late[k]] if later else []
                    parts = 3 if k % 2 else 2
                    if causal and nxt and k == plan.turn:
                        turn_maxima(nxt[0])
                    for i in range(parts):
                        if i < 2:
                            score(n, b, g, k, i)
                        elif k >= pv_lag:
                            values(n, g, k - pv_lag)
                        elif prev:
                            values(prev[0], prev[2], NSL + k - pv_lag)
                        if not causal and nxt and k == plan.turn and i == 1:
                            turn_maxima(nxt[0])
                        if causal:
                            first, end = i * len(tiles) // parts, (i + 1) * len(tiles) // parts
                        else:
                            first, end = (0, len(tiles)) if i == parts - 1 else (0, 0)
                        for whose, j in tiles[first:end]:
                            tile(*whose, j)
                    if prev and k == pv_lag + 1:
                        turn_outputs(prev[0], 1)
                    if k == plan.bank_end[0] + pv_lag + 2:
                        turn_outputs(n, 0)

            def before():
                for j in range(NTL):
                    tile(0, 0, 0, j)
                turn_maxima(0)
                for j in range(sum(map(len, plan.late))):
                    tile(1, 0, 1, j)

            def finish():
                for k in range(NSL + 1 - pv_lag, NSL, 2):
                    values(NGR - 1, NHG - 1, k)
                turn_outputs(NGR - 1, 1)

            walk(plan, B, group, before, after=finish, fori=t_.Fori)


def walk(plan, n_seq, group, before, after, fori):
    def at(b, g):
        if g < 0:
            return (NHG * b + g, b - 1, NHG + g)
        return (NHG * b + g, b + g // NHG, g % NHG)

    def step(b, g, end=None, first=False):
        nxt, later = [at(b, g + i) if end is None or g + i < end else None for i in (1, 2)]
        group(at(b, g), nxt, later, None if first else at(b, g - 1))

    before()
    step(0, 0, first=True)
    with fori(0, n_seq - 1) as b:
        for g in range(1, NHG + 1):
            step(b, g)
    for g in range(1, NHG):
        step(n_seq - 1, g, end=NHG)
    after()


def skewed(fori, count, stages):
    most = max(lag for _, lag in stages)
    first = most + most % 2

    def step(half, r, fixed):
        for fn, lag in stages:
            s = (r - lag) % 2
            n = 2 * (half + (r - lag - s) // 2) + s
            if not fixed or 0 <= n < count:
                fn(n, s)

    for j in range(first):
        step(j // 2, j % 2, True)
    with fori(first // 2, count // 2) as i:
        for r in range(2):
            step(i, r, False)
    for j in range(count, count + most):
        step(j // 2, j % 2, True)


def uses(n, s):
    return (n - s) // 2 + 1 if isinstance(n, int) else (n + (2 - s)) // 2


def mix_phase(nc, sem, x_dram, att_dram, w_out, gate_w, x1_dram, xn_dram, onehot_all, weight_all):
    with Phase(nc, "mix") as ph:
        def two(name, shape, dt=F32):
            return [ph.sb(f"{name}{s}", shape, dt) for s in range(2)]
        x_in, a_in = two("x", [P, GT, D]), two("a", [P, GT, D])
        aT, x1, xn, xnT = two("aT", [P, GW]), two("x1", [P, GT, D]), two("xn", [P, GT, D]), two("xnT", [P, GW])
        st, mv, rstd = two("st", [P, GT, 6]), two("mv", [P, GT, 2]), two("rstd", [P, GT])
        top, diff, ex = two("top", [P, GT, 1]), two("diff", [P, GT, NE]), two("ex", [P, GT, NE])
        tot, pick, best = two("tot", [P, GT, 1]), two("pick", [P, GT, NE]), two("best", [P, GT, 1])
        wo, gw = ph.sb("wo", [P, D]), ph.sb("gw", [P, NE])
        ident, power = ph.sb("ident", [P, P]), ph.sb("power", [P, GT])
        order_i, order = ph.sb("order_i", [P, GT, NE], I32), ph.sb("order", [P, GT, NE])
        psA, psO, psT, psR = [[ph.ps(f"{k}{s}") for s in range(2)] for k in "AOTR"]

        setup, weights = sem("setup"), sem("weights")
        divider = sem("divider")
        in_loaded = [sem(f"in_loaded{s}") for s in range(2)]
        aT_done, aT_copied, out_done = sem("aT_done"), sem("aT_copied"), sem("out_done")
        norm_chain, rstd_chain, apply_done = sem("norm_chain"), sem("rstd_chain"), sem("apply_done")
        xT_done, xT_copied, logits_done = sem("xT_done"), sem("xT_copied"), sem("logits_done")
        diff_chain, ex_done, pick_chain = sem("diff_chain"), sem("ex_done"), sem("pick_chain")
        stored = [sem(f"stored{s}") for s in range(2)]
        NST = 1 + STATS_STEPS
        NPICK = 5
        block = ph.block()

        @block.sync
        def _(sp):
            for s in range(2):
                sp.sem_inc(stored[s], 32)
            sp.dma_start(wo[:, :], w_out).then_inc(weights, 16)
            sp.dma_start(gw[:, :], gate_w).then_inc(weights, 16)

            def load(n, s):
                sp.wait_ge(norm_chain, (n + 1) * NST)
                sp.wait_ge(aT_done, n + 1)
                sp.dma_start(x_in[s][:, :, :], rows_of(x_dram, n)).then_inc(in_loaded[s], 16)
                sp.dma_start(a_in[s][:, :, :], rows_of(att_dram, n)).then_inc(in_loaded[s], 16)

            def store(n, s):
                sp.wait_ge(apply_done, n + 3)
                sp.dma_start(rows_of(x1_dram, n), x1[s][:, :, :]).then_inc(stored[s], 16)
                sp.dma_start(rows_of(xn_dram, n), xn[s][:, :, :]).then_inc(stored[s], 16)

            skewed(sp.Fori, NG, [(store, 2), (load, 0)])
            for s in range(2):
                sp.wait_ge(stored[s], 32 * (NG // 2 + 1))

        @block.gpsimd
        def _(g):
            emit_identity(nc, g, ident, setup)
            g.memset(power[:, :], -0.5).then_inc(setup, 1)
            g.iota(order_i[:, :, :], pattern=[[0, GT], [-1, NE]], base=NE, channel_multiplier=0).then_inc(setup, 1)
            g.wait_ge(setup, 4)
            g.tensor_copy(order[:, :, :], order_i[:, :, :]).then_inc(setup, 1)
            rc = Count(rstd_chain, RSTD_STEPS)

            def rstds(n, s):
                wait_apart(g, divider, (norm_chain, (n + 3) * NST), (apply_done, n + 1))
                rc.start(n)
                emit_rstd(nc, g, rc, mv[s], rstd[s], power, divider)
                rc.end()

            skewed(g.Fori, NG, [(rstds, 2)])

        @block.scalar
        def _(a_):
            def copy_a(n, s):
                a_.wait_ge(aT_done, n + 3)
                a_.wait_ge(out_done, n + 1)
                nc.scalar.activation(aT[s][:, :], psA[s][:, :], ACT.Copy).then_inc(aT_copied, 1)

            def copy_x(n, s):
                a_.wait_ge(xT_done, n + 3)
                a_.wait_ge(logits_done, n + 1)
                nc.scalar.activation(xnT[s][:, :], psT[s][:, :], ACT.Copy).then_inc(xT_copied, 1)

            def exps(n, s):
                a_.wait_ge(diff_chain, 2 * (n + 1))
                a_.wait_ge(pick_chain, NPICK * (n + 1))
                nc.scalar.activation(ex[s][:, :, :], diff[s][:, :, :], ACT.Exp).then_inc(ex_done, 1)

            skewed(a_.Fori, NG, [(exps, 4), (copy_x, 3), (copy_a, 1)])

        @block.vector
        def _(v):
            v.sem_inc(norm_chain, 2 * NST)
            v.sem_inc(apply_done, 2)
            v.sem_inc(pick_chain, 2 * NPICK)
            ch = Count(norm_chain, NST, 2)
            dc = Count(diff_chain, 2)
            pc = Count(pick_chain, NPICK, 2)
            v.wait_ge(setup, 5)

            def residual(n, s):
                ch.start(n)
                v.wait_ge(in_loaded[s], 32 * uses(n, s))
                v.wait_ge(out_done, n + 3)
                v.wait_ge(stored[s], 32 * uses(n, s))
                ch.inc(nc.vector.tensor_tensor(x1[s][:, :, :], x_in[s][:, :, :],
                                               psO[s][:, :].rearrange("p (t c) -> p t c", t=GT), ALU.add))
                ch.wait(v)
                emit_stats(nc, v, ch, x1[s], st[s], mv[s], divider)
                ch.end()
                v.wait_ge(rstd_chain, RSTD_STEPS * (n + 1))
                v.wait_ge(xT_done, n + 1)
                for t in range(GT):
                    last = nc.vector.tensor_scalar(xn[s][:, t, :], x1[s][:, t, :], mv[s][:, t, 0:1],
                                                   rstd[s][:, t:t + 1], ALU.subtract, ALU.mult)
                last.then_inc(apply_done, 1)

            def logits(n, s):
                lg = psR[s][:, 0:GT * NE].rearrange("p (t e) -> p t e", t=GT)
                dc.start(n)
                v.wait_ge(logits_done, n + 3)
                v.wait_ge(ex_done, n - 1) if isinstance(n, int) and n >= 2 else None
                dc.inc(nc.vector.tensor_reduce(top[s][:, :, 0], lg, AX.X, ALU.max))
                dc.wait(v)
                dc.inc(nc.vector.tensor_tensor(diff[s][:, :, :], lg, top[s][:, :, :].to_broadcast([P, GT, NE]),
                                               ALU.subtract))
                dc.end()

            def choose(n, s):
                pc.start(n)
                v.wait_ge(ex_done, n + 1)
                pc.inc(nc.vector.tensor_reduce(tot[s][:, :, 0], ex[s][:, :, :], AX.X, ALU.add))
                pc.inc(nc.vector.scalar_tensor_tensor(out=pick[s][:, :, :], in0=diff[s][:, :, :], scalar=0.0,
                                                      in1=order[:, :, :], op0=ALU.is_ge, op1=ALU.mult))
                pc.wait(v)
                pc.inc(nc.vector.reciprocal(weight_all[:, bass.ds(n * GT, GT)], tot[s][:, :, 0]))
                pc.inc(nc.vector.tensor_reduce(best[s][:, :, 0], pick[s][:, :, :], AX.X, ALU.max))
                pc.wait(v)
                pc.inc(nc.vector.tensor_tensor(onehot_all[:, bass.ds(n * GT, GT), :], pick[s][:, :, :],
                                               best[s][:, :, :].to_broadcast([P, GT, NE]), ALU.is_equal))
                pc.end()

            skewed(v.Fori, NG, [(choose, 5), (logits, 4), (residual, 2)])

        @block.tensor
        def _(t_):
            for q in (aT_done, out_done, xT_done, logits_done):
                t_.sem_inc(q, 2)
            t_.wait_ge(setup, 2)
            t_.wait_ge(weights, 32)

            def turn_a(n, s):
                t_.wait_ge(in_loaded[s], 32 * uses(n, s))
                for t in range(GT):
                    last = nc.tensor.transpose(psA[s][:, t * P:(t + 1) * P], a_in[s][:, t, :], ident[:, :])
                last.then_inc(aT_done, 1)

            def out(n, s):
                t_.wait_ge(aT_copied, n + 1)
                t_.wait_ge(norm_chain, NST * (n + 1))
                for t in range(GT):
                    last = nc.tensor.matmul(psO[s][:, t * D:(t + 1) * D], aT[s][:, t * P:(t + 1) * P], wo[:, :],
                                            start=True, stop=True)
                last.then_inc(out_done, 1)

            def turn_x(n, s):
                t_.wait_ge(apply_done, n + 3)
                for t in range(GT):
                    last = nc.tensor.transpose(psT[s][:, t * P:(t + 1) * P], xn[s][:, t, :], ident[:, :])
                last.then_inc(xT_done, 1)

            def route(n, s):
                t_.wait_ge(xT_copied, n + 1)
                t_.wait_ge(pick_chain, NPICK * (n + 1))
                for t in range(GT):
                    last = nc.tensor.matmul(psR[s][:, t * NE:(t + 1) * NE], xnT[s][:, t * P:(t + 1) * P], gw[:, :],
                                            start=True, stop=True)
                last.then_inc(logits_done, 1)

            skewed(t_.Fori, NG, [(route, 4), (turn_x, 3), (out, 2), (turn_a, 1)])


SORTED_TILES = (T + NE * (P - 1)) // P + 1
SORTED_TILES += SORTED_TILES % 2


def place_phase(nc, sem, onehot_all, place_all, expert_row):
    with Phase(nc, "place") as ph:
        before = ph.sb("before", [P, P])
        ones = ph.sb("ones", [P, P])
        rank = ph.sb("rank", [P, NT, NE])
        total = ph.sb("total", [P, NE * NT])
        cum = ph.sb("cum", [P, NE * NT])
        excl = ph.sb("excl", [P, NE * NT])
        zeros = ph.sb("zeros", [P, NE * NT])
        marks_i, marks = ph.sb("marks_i", [P, NT], I32), ph.sb("marks", [P, NT])
        tiles_i, tiles = ph.sb("tiles_i", [P, SORTED_TILES], I32), ph.sb("tiles", [P, SORTED_TILES])
        count = ph.sb("count", [P, NE, 1])
        over = ph.sb("over", [P, NE, NT])
        blocks, end = ph.sb("blocks", [P, NE]), ph.sb("end", [P, NE])
        adj = ph.sb("adj", [P, NE, 1])
        past = ph.sb("past", [P, SORTED_TILES, NE])
        which = ph.sb("which", [P, SORTED_TILES])
        spot = ph.sb("spot", [P, NT])
        ps_rank, ps_total = ph.ps("ps_rank"), ph.ps("ps_total")
        setup, ready, counted, chain = sem("setup"), sem("ready"), sem("counted"), sem("chain")
        block = ph.block()

        @block.gpsimd
        def _(g):
            g.memset(before[:, :], 1.0).then_inc(setup, 1)
            g.memset(ones[:, :], 1.0)
            g.memset(zeros[:, :], 0.0)
            g.iota(marks_i[:, :], pattern=[[P, NT]], base=0, channel_multiplier=0)
            g.iota(tiles_i[:, :], pattern=[[1, SORTED_TILES]], base=0, channel_multiplier=0).then_inc(setup, 1)
            g.wait_ge(setup, 2)
            g.tensor_copy(marks[:, :], marks_i[:, :])
            g.tensor_copy(tiles[:, :], tiles_i[:, :])
            g.affine_select(out=before[:, :], in_=before[:, :], compare_op=ALU.is_gt, fill=0.0, base=0,
                            pattern=[[1, P]], channel_multiplier=-1).then_inc(ready, 1)

        @block.tensor
        def _(t_):
            t_.wait_ge(ready, 1)
            flat = onehot_all[:, :, :].rearrange("p t e -> p (t e)")
            nc.tensor.matmul(ps_rank[:, :], before[:, :], flat, start=True, stop=True).then_inc(counted, 1)
            nc.tensor.matmul(ps_total[:, :], ones[:, :], flat, start=True, stop=True).then_inc(counted, 1)

        @block.vector
        def _(v):
            c = Count(chain, 0)

            def link(ins):
                c.inc(ins)
                c.wait(v)

            v.wait_ge(counted, 2)
            v.wait_ge(ready, 1)
            link(nc.vector.tensor_copy(total[:, :].rearrange("p (e t) -> p e t", e=NE),
                                       ps_total[:, :].rearrange("p (t e) -> p e t", e=NE)))
            link(nc.vector.tensor_tensor_scan(cum[:, :], total[:, :], zeros[:, :], 0.0, ALU.add, ALU.add))
            link(nc.vector.tensor_tensor(excl[:, :], cum[:, :], total[:, :], ALU.subtract))
            cum3 = cum[:, :].rearrange("p (e t) -> p e t", e=NE)
            excl3 = excl[:, :].rearrange("p (e t) -> p e t", e=NE)
            link(nc.vector.tensor_tensor(count[:, :, :], cum3[:, :, NT - 1:NT], excl3[:, :, 0:1], ALU.subtract))
            link(nc.vector.tensor_tensor(over[:, :, :], count[:, :, :].to_broadcast([P, NE, NT]),
                                         marks[:, :].unsqueeze(1).to_broadcast([P, NE, NT]), ALU.is_gt))
            link(nc.vector.tensor_reduce(blocks[:, :], over[:, :, :], AX.X, ALU.add))
            link(nc.vector.tensor_tensor_scan(end[:, :], blocks[:, :], zeros[:, 0:NE], 0.0, ALU.add, ALU.add))
            link(nc.vector.tensor_tensor(adj[:, :, 0], end[:, :], blocks[:, :], ALU.subtract))
            link(nc.vector.scalar_tensor_tensor(out=adj[:, :, :], in0=adj[:, :, :], scalar=float(P),
                                                in1=excl3[:, :, 0:1], op0=ALU.mult, op1=ALU.subtract))
            link(nc.vector.tensor_tensor(excl3, excl3, adj[:, :, :].to_broadcast([P, NE, NT]), ALU.add))
            link(nc.vector.tensor_tensor(rank[:, :, :], ps_rank[:, :].rearrange("p (t e) -> p t e", e=NE),
                                         excl[:, :].rearrange("p (e t) -> p t e", e=NE), ALU.add))
            link(nc.vector.tensor_tensor(rank[:, :, :], rank[:, :, :], onehot_all[:, :, :], ALU.mult))
            link(nc.vector.tensor_reduce(spot[:, :], rank[:, :, :], AX.X, ALU.add))
            link(nc.vector.tensor_copy(place_all[:, :], spot[:, :]))
            link(nc.vector.tensor_tensor(past[:, :, :], tiles[:, :].unsqueeze(2).to_broadcast([P, SORTED_TILES, NE]),
                                         end[:, :].unsqueeze(1).to_broadcast([P, SORTED_TILES, NE]), ALU.is_ge))
            link(nc.vector.tensor_reduce(which[:, :], past[:, :, :], AX.X, ALU.add))
            link(nc.vector.tensor_scalar(which[:, :], which[:, :], float(NE - 1), None, ALU.min))
            link(nc.vector.tensor_copy(expert_row[:, :], which[:, :]))


def scatter_phase(nc, sem, xn_dram, sorted_dram, place_all):
    with Phase(nc, "scat") as ph:
        rows = [ph.sb(f"rows{s}", [P, GT, D]) for s in range(2)]
        zeros = ph.sb("zeros", [P, 8, D])
        setup, cleared = sem("setup"), sem("cleared")
        loaded = [sem(f"loaded{s}") for s in range(2)]
        sent = [sem(f"sent{s}") for s in range(2)]
        block = ph.block()

        @block.sync
        def _(sp):
            sp.wait_ge(setup, 1)
            for k in range(SORTED_TILES // 8):
                sp.dma_start(sorted_dram[k * 8 * P:(k + 1) * 8 * P, :].rearrange("(t p) c -> p t c", p=P),
                             zeros[:, :, :]).then_inc(cleared, 16)

            for n in range(NG):
                s = n % 2
                if n >= 2:
                    sp.wait_ge(sent[s], 16 * GT * (n // 2))
                sp.dma_start(rows[s][:, :, :], rows_of(xn_dram, n)).then_inc(loaded[s], 16)

        @block.gpsimd
        def _(g):
            g.memset(zeros[:, :, :], 0.0).then_inc(setup, 1)
            g.wait_ge(cleared, 16 * (SORTED_TILES // 8))
            for n in range(NG):
                s = n % 2
                g.wait_ge(loaded[s], 16 * (n // 2 + 1))
                for t in range(GT):
                    g.indirect_dma_start(sorted_dram[:, :], bass.IndirectOffsetOnAxis(
                        ap=place_all[:, n * GT + t:n * GT + t + 1], axis=0), rows[s][:, t, :], None)\
                        .then_inc(sent[s], 16)
            for s in range(2):
                g.wait_ge(sent[s], 16 * GT * (NG // 2))


def experts_phase(nc, sem, sorted_dram, y_dram, w1, b1, w2, b2, expert_row):
    FC = FF // P
    with Phase(nc, "moe") as ph:
        def two(name, shape, dt=F32):
            return [ph.sb(f"{name}{s}", shape, dt) for s in range(2)]
        w1_sb = ph.sb("w1", [P, NE, FF])
        w2_sb = ph.sb("w2", [P, NE, FC * D])
        b1_sb = ph.sb("b1", [P, NE, FF])
        b2_sb = ph.sb("b2", [P, NE, D])
        ident = ph.sb("ident", [P, P])
        x = [ph.sb(f"x{s}", [P, D]) for s in range(4)]
        xT, hb, h = two("xT", [P, P]), two("hb", [P, FF]), two("h", [P, FF])
        hT, y = two("hT", [P, FF]), two("y", [P, D])
        psX, psH, psT, psY = [[ph.ps(f"{k}{s}") for s in range(2)] for k in "XHTY"]
        setup, weights = sem("setup"), sem("weights")
        loaded = [sem(f"loaded{s}") for s in range(4)]
        stored = [sem(f"stored{s}") for s in range(2)]
        xT_done, xT_copied, up_done, biased, gelu_done = [sem(k) for k in
                                                          ("xT_done", "xT_copied", "up_done", "biased", "gelu_done")]
        hT_done, hT_copied, down_done, y_done = [sem(k) for k in ("hT_done", "hT_copied", "down_done", "y_done")]
        block = ph.block()

        def expert(eng, n):
            return eng.value_load(expert_row[0:1, bass.ds(n, 1)], min_val=0, max_val=NE - 1)

        @block.sync
        def _(sp):
            for s in range(2):
                sp.sem_inc(stored[s], 16)
            sp.dma_start(w1_sb[:, :, :], w1.rearrange("e c f -> c e f")).then_inc(weights, 16)
            sp.dma_start(b1_sb[:, :, :], bass.AP(tensor=b1.tensor, offset=0, ap=[[0, P], [FF, NE], [1, FF]]))\
                .then_inc(weights, 16)
            sp.dma_start(w2_sb[:, :, :].rearrange("p e (m c) -> p e m c", m=FC),
                         w2.rearrange("e (m p) c -> p e m c", p=P)).then_inc(weights, 16)
            sp.dma_start(b2_sb[:, :, :], bass.AP(tensor=b2.tensor, offset=0, ap=[[0, P], [D, NE], [1, D]]))\
                .then_inc(weights, 16)

            def load(n, q):
                if not (isinstance(n, int) and n < 4):
                    sp.wait_ge(xT_done, n - 1)
                sp.dma_start(x[q][:, :], sorted_dram[bass.ds(n * P, P), :]).then_inc(loaded[q], 16)

            def store(n, q):
                s = q % 2
                sp.wait_ge(y_done, n + 3)
                sp.dma_start(y_dram[bass.ds(n * P, P), :], y[s][:, :]).then_inc(stored[s], 16)

            skewed4(sp.Fori, SORTED_TILES, [(store, 11), (load, 0)])
            for s in range(2):
                sp.wait_ge(stored[s], 16 * (SORTED_TILES // 2 + 1))

        @block.gpsimd
        def _(g):
            emit_identity(nc, g, ident, setup)

        @block.scalar
        def _(a_):
            a_.sem_inc(gelu_done, 2)
            a_.sem_inc(xT_copied, 2)

            def copy_x(n, q):
                s = q % 2
                a_.wait_ge(xT_done, n + 3)
                a_.wait_ge(up_done, n + 1)
                nc.scalar.activation(xT[s][:, :], psX[s][:, 0:P], ACT.Copy).then_inc(xT_copied, 1)

            def gelu(n, q):
                s = q % 2
                a_.wait_ge(biased, n + 3)
                a_.wait_ge(hT_done, n + 1)
                nc.scalar.activation(h[s][:, :], hb[s][:, :], ACT.Gelu).then_inc(gelu_done, 1)

            skewed4(a_.Fori, SORTED_TILES, [(gelu, 6), (copy_x, 3)])

        @block.vector
        def _(v):
            for q in (biased, hT_copied, y_done):
                v.sem_inc(q, 2)
            v.wait_ge(weights, 64)

            def bias_up(n, q):
                s = q % 2
                e = expert(v, n)
                v.wait_ge(up_done, n + 3)
                v.wait_ge(gelu_done, n + 1)
                nc.vector.tensor_tensor(hb[s][:, :].unsqueeze(1), psH[s][:, :].unsqueeze(1), b1_sb[:, bass.ds(e, 1), :],
                                        ALU.add).then_inc(biased, 1)

            def copy_h(n, q):
                s = q % 2
                v.wait_ge(hT_done, n + 3)
                v.wait_ge(down_done, n + 1)
                nc.vector.tensor_copy(hT[s][:, :], psT[s][:, :]).then_inc(hT_copied, 1)

            def bias_down(n, q):
                s = q % 2
                e = expert(v, n)
                v.wait_ge(down_done, n + 3)
                v.wait_ge(stored[s], 16 * uses4(n, s, 2))
                nc.vector.tensor_tensor(y[s][:, :].unsqueeze(1), psY[s][:, 0:D].unsqueeze(1), b2_sb[:, bass.ds(e, 1), :],
                                        ALU.add).then_inc(y_done, 1)

            skewed4(v.Fori, SORTED_TILES, [(bias_down, 10), (copy_h, 8), (bias_up, 5)])

        @block.tensor
        def _(t_):
            for q in (xT_done, up_done, hT_done, down_done):
                t_.sem_inc(q, 2)
            t_.wait_ge(setup, 2)
            t_.wait_ge(weights, 64)

            def turn_x(n, q):
                s = q % 2
                t_.wait_ge(loaded[q], 16 * uses4(n, q))
                t_.wait_ge(xT_copied, n + 1)
                nc.tensor.transpose(psX[s][:, 0:P], x[q][:, :], ident[:, :]).then_inc(xT_done, 1)

            def up(n, q):
                s = q % 2
                e = expert(t_, n)
                t_.wait_ge(xT_copied, n + 3)
                t_.wait_ge(biased, n + 1)
                nc.tensor.matmul(psH[s][:, :], xT[s][:, :], w1_sb[:, bass.ds(e, 1), :].rearrange("p a f -> p (a f)"),
                                 start=True, stop=True).then_inc(up_done, 1)

            def turn_h(n, q):
                s = q % 2
                t_.wait_ge(gelu_done, n + 3)
                t_.wait_ge(hT_copied, n + 1)
                for m in range(FC):
                    last = nc.tensor.transpose(psT[s][:, m * P:(m + 1) * P], h[s][:, m * P:(m + 1) * P], ident[:, :])
                last.then_inc(hT_done, 1)

            def down(n, q):
                s = q % 2
                e = expert(t_, n)
                t_.wait_ge(hT_copied, n + 3)
                t_.wait_ge(y_done, n + 1)
                for m in range(FC):
                    last = nc.tensor.matmul(psY[s][:, 0:D], hT[s][:, m * P:(m + 1) * P],
                                            w2_sb[:, bass.ds(e, 1), m * D:(m + 1) * D].rearrange("p a f -> p (a f)"),
                                            start=(m == 0), stop=(m == FC - 1))
                last.then_inc(down_done, 1)

            skewed4(t_.Fori, SORTED_TILES, [(down, 9), (turn_h, 7), (up, 4), (turn_x, 2)])


def gather_phase(nc, sem, x1_dram, y_dram, place_all, weight_all, x2_dram):
    with Phase(nc, "gath") as ph:
        x1 = [ph.sb(f"x{s}", [P, GT, D]) for s in range(2)]
        y = [ph.sb(f"y{s}", [P, GT, D]) for s in range(2)]
        x2 = [ph.sb(f"o{s}", [P, GT, D]) for s in range(2)]
        loaded = [sem(f"loaded{s}") for s in range(2)]
        gathered = [sem(f"gathered{s}") for s in range(2)]
        stored = [sem(f"stored{s}") for s in range(2)]
        summed = sem("summed")
        block = ph.block()

        @block.sync
        def _(sp):
            for n in range(NG):
                s = n % 2
                if n >= 2:
                    sp.wait_ge(summed, n - 1)
                sp.dma_start(x1[s][:, :, :], rows_of(x1_dram, n)).then_inc(loaded[s], 16)
            for s in range(2):
                sp.wait_ge(stored[s], 16 * (NG // 2))

        @block.gpsimd
        def _(g):
            for n in range(NG):
                s = n % 2
                if n >= 2:
                    g.wait_ge(summed, n - 1)
                for t in range(GT):
                    g.indirect_dma_start(y[s][:, t, :], None, y_dram[:, :], bass.IndirectOffsetOnAxis(
                        ap=place_all[:, n * GT + t:n * GT + t + 1], axis=0)).then_inc(gathered[s], 16)

        @block.vector
        def _(v):
            for n in range(NG):
                s = n % 2
                v.wait_ge(loaded[s], 16 * (n // 2 + 1))
                v.wait_ge(gathered[s], 16 * GT * (n // 2 + 1))
                if n >= 2:
                    v.wait_ge(stored[s], 16 * (n // 2))
                for t in range(GT):
                    last = nc.vector.scalar_tensor_tensor(
                        out=x2[s][:, t, :], in0=y[s][:, t, :], scalar=weight_all[:, n * GT + t:n * GT + t + 1],
                        in1=x1[s][:, t, :], op0=ALU.mult, op1=ALU.add)
                last.then_inc(summed, 1)

        @block.scalar
        def _(a_):
            for n in range(NG):
                s = n % 2
                a_.wait_ge(summed, n + 1)
                a_.dma_start(rows_of(x2_dram, n), x2[s][:, :, :]).then_inc(stored[s], 16)


def bias_phase(nc, sem, offsets, pos_bias, fwd_dram, rev_dram):
    NCH = WINDOW // P
    with Phase(nc, "bias") as ph:
        off_i, off = ph.sb("off_i", [P, NOFF], I32), ph.sb("off", [P, NOFF])
        pb = ph.sb("pb", [P, NOFF, H])
        dist_i, dist = ph.sb("dist_i", [P, 2 * NCH], I32), ph.sb("dist", [P, 2 * NCH])
        off_mask = ph.sb("off_mask", [P, NOFF])
        val = ph.sb("val", [P, H, NOFF])
        top, tot = ph.sb("top", [P, H, 1]), ph.sb("tot", [P, H])
        res = ph.sb("res", [P, H])
        ident = ph.sb("ident", [P, P])
        rows = [ph.sb(f"rows{k}", [H, 2 * WINDOW]) for k in range(2)]
        psT = ph.ps("psT")
        setup, loaded, chain, shifted, exp_done, ln_done, turned, stored = [sem(k) for k in (
            "setup", "loaded", "chain", "shifted", "exp_done", "ln_done", "turned", "stored")]
        block = ph.block()

        @block.sync
        def _(sp):
            sp.dma_start(off_i[:, :], bass.AP(tensor=offsets.tensor, offset=0, ap=[[0, P], [1, NOFF]])).then_inc(loaded, 16)
            sp.dma_start(pb[:, :, :], bass.AP(tensor=pos_bias.tensor, offset=0, ap=[[0, P], [H, NOFF], [1, H]]))\
                .then_inc(loaded, 16)
            sp.wait_ge(chain, 2 + 5 * 2 * NCH)
            sp.dma_start(fwd_dram, rows[0][:, :]).then_inc(stored, 16)
            sp.dma_start(rev_dram, rows[1][:, :]).then_inc(stored, 16)
            sp.wait_ge(stored, 32)

        @block.gpsimd
        def _(g):
            emit_identity(nc, g, ident, setup)
            for k in range(NCH):
                g.iota(dist_i[:, k:k + 1], pattern=[[0, 1]], base=k * P, channel_multiplier=1)
                last = g.iota(dist_i[:, NCH + k:NCH + k + 1], pattern=[[0, 1]], base=WINDOW - 1 - k * P,
                              channel_multiplier=-1)
            last.then_inc(setup, 1)
            for k in range(2):
                last = g.memset(rows[k][:, :], MASKED)
            last.then_inc(setup, 1)

        @block.vector
        def _(v):
            c = Count(chain, 0)

            def link(ins):
                c.inc(ins)
                c.wait(v)

            v.wait_ge(setup, 4)
            v.wait_ge(loaded, 32)
            link(nc.vector.tensor_copy(dist[:, :], dist_i[:, :]))
            link(nc.vector.tensor_copy(off[:, :], off_i[:, :]))
            for k in range(2 * NCH):
                link(nc.vector.tensor_scalar(off_mask[:, :], off[:, :], dist[:, k:k + 1], MASKED, ALU.not_equal, ALU.mult))
                link(nc.vector.tensor_tensor(val[:, :, :], pb[:, :, :].rearrange("p o h -> p h o"),
                                             off_mask[:, :].unsqueeze(1).to_broadcast([P, H, NOFF]), ALU.add))
                link(nc.vector.tensor_reduce(top[:, :, 0], val[:, :, :], AX.X, ALU.max))
                nc.vector.tensor_tensor(val[:, :, :], val[:, :, :], top[:, :, :].to_broadcast([P, H, NOFF]),
                                        ALU.subtract).then_inc(shifted, 1)
                v.wait_ge(exp_done, k + 1)
                nc.vector.tensor_reduce(tot[:, :], val[:, :, :], AX.X, ALU.add).then_inc(shifted, 1)
                v.wait_ge(ln_done, k + 1)
                link(nc.vector.tensor_tensor(res[:, :], tot[:, :], top[:, :, 0], ALU.add))
                v.wait_ge(turned, k + 1)
                at = (P - 1 if k < NCH else P) + (k % NCH) * P
                link(nc.vector.tensor_copy(rows[k // NCH][:, at:at + P], psT[0:H, 0:P]))

        @block.scalar
        def _(a_):
            for k in range(2 * NCH):
                a_.wait_ge(shifted, 2 * k + 1)
                nc.scalar.activation(val[:, :, :], val[:, :, :], ACT.Exp).then_inc(exp_done, 1)
                a_.wait_ge(shifted, 2 * k + 2)
                nc.scalar.activation(tot[:, :], tot[:, :], ACT.Ln).then_inc(ln_done, 1)

        @block.tensor
        def _(t_):
            t_.wait_ge(setup, 2)
            for k in range(2 * NCH):
                t_.wait_ge(chain, 2 + 5 * k + 4)
                nc.tensor.transpose(psT[0:H, 0:P], res[:, :], ident[:, :]).then_inc(turned, 1)


def shifted_rows(bias_dram, h0, n_heads):
    return bass.AP(tensor=bias_dram.tensor, offset=bias_dram.offset + h0 * 2 * WINDOW,
                   ap=[[1, P], [2 * WINDOW, n_heads], [1, WB * P]])


def backwards(t, n_heads):
    whole = t[:, :, :]
    return bass.AP(tensor=whole.tensor, offset=whole.offset + WB * P - 1,
                   ap=[list(whole.ap[0]), [WB * P, n_heads], [-1, WB * P]])


def gated_phase(nc, sem, x_dram, att_dram, w_gate, b_gate, norm1, w_out, sum_dram, xr_dram):
    with Phase(nc, "gate") as ph:
        def two(name, shape, dt=F32):
            return [ph.sb(f"{name}{s}", shape, dt) for s in range(2)]
        x_in = [ph.sb(f"x{s}", [P, GT, D]) for s in range(4)]
        a_in = [ph.sb(f"a{s}", [P, GT, D]) for s in range(4)]
        y, xr, xT, gate, ag = two("y", [P, GT, D]), two("xr", [P, GT, D]), two("xT", [P, GW]), two("gate", [P, GW]), two("ag", [P, GW])
        yy = two("yy", [P, GT, D])
        total, xr2, junk = two("total", [P, GT, D]), two("xr2", [P, GT, D]), two("junk", [P, D])
        st, mv, rstd, rr = two("st", [P, GT, 6]), two("mv", [P, GT, 2]), two("rstd", [P, GT]), two("rr", [P, GT])
        sq, r2 = two("sq", [P, GT]), two("r2", [P, GT])
        wg, wo, bg, n1 = ph.sb("wg", [P, D]), ph.sb("wo", [P, D]), ph.sb("bg", [P, 1]), ph.sb("n1", [P, 1])
        ident, power = ph.sb("ident", [P, P]), ph.sb("power", [P, GT])
        psT, psG, psA, psO = [[ph.ps(f"{k}{s}") for s in range(2)] for k in "TGAO"]
        setup, weights = sem("setup"), sem("weights")
        divider = sem("divider")
        loaded = [sem(f"loaded{s}") for s in range(4)]
        stored = [sem(f"stored{s}") for s in range(2)]
        stats_chain, rstd_chain, y_chain = sem("stats_chain"), sem("rstd_chain"), sem("y_chain")
        turned, xT_copied, gate_done, sig_done = sem("turned"), sem("xT_copied"), sem("gate_done"), sem("sig_done")
        ag_done, out_done, sq_chain, r2_chain, xr2_done = [sem(k) for k in ("ag_done", "out_done", "sq_chain", "r2_chain", "xr2_done")]
        NY, NSQ = 2 * GT, 2 + GT
        block = ph.block()

        @block.sync
        def _(sp):
            for s in range(2):
                sp.sem_inc(stored[s], 32)
            for dst, src in ((wg[:, :], w_gate), (wo[:, :], w_out), (bg[:, :], b_gate.rearrange("(c a) -> c a", a=1)),
                             (n1[:, :], norm1.rearrange("(c a) -> c a", a=1))):
                sp.dma_start(dst, src).then_inc(weights, 16)

            def load(n, q):
                sp.wait_ge(sq_chain, NSQ * (n + 1))
                sp.dma_start(x_in[q][:, :, :], rows_of(x_dram, n)).then_inc(loaded[q], 16)
                sp.dma_start(a_in[q][:, :, :], rows_of(att_dram, n)).then_inc(loaded[q], 16)

            def store(n, q):
                s = q % 2
                sp.wait_ge(xr2_done, n + 3)
                sp.dma_start(rows_of(sum_dram, n), total[s][:, :, :]).then_inc(stored[s], 16)
                sp.dma_start(rows_of(xr_dram, n), xr2[s][:, :, :]).then_inc(stored[s], 16)

            skewed4(sp.Fori, NG, [(store, 4), (load, 0)])
            for s in range(2):
                sp.wait_ge(stored[s], 32 * (NG // 2 + 1))

        @block.gpsimd
        def _(g):
            g.sem_inc(r2_chain, 4)
            emit_identity(nc, g, ident, setup)
            g.memset(power[:, :], -0.5).then_inc(setup, 1)
            g.wait_ge(setup, 3)
            rc = Count(rstd_chain, RMS_STEPS)

            def rstds(n, q):
                s = q % 2
                wait_apart(g, divider, (stats_chain, (n + 1) * STATS_STEPS), (y_chain, (n + 1) * NY))
                rc.start(n)
                emit_rstd(nc, g, rc, mv[s], rstd[s], power, divider, rms=(RMS_EPS, rr[s]))
                rc.end()

            def second(n, q):
                s = q % 2
                wait_apart(g, divider, (sq_chain, (n + 5) * NSQ), (xr2_done, n + 1))
                g.tensor_scalar(r2[s][:, :], sq[s][:, :], 1.0 / D, RMS_EPS, ALU.mult, ALU.add).then_inc(r2_chain, 1)
                g.wait_ge(r2_chain, 2 * n + 5)
                g.tensor_tensor(r2[s][:, :], r2[s][:, :], power[:, :], ALU.pow).then_inc(r2_chain, 1)

            skewed4(g.Fori, NG, [(second, 3), (rstds, 1)])

        @block.vector
        def _(v):
            v.sem_inc(y_chain, 2 * NY)
            v.sem_inc(sq_chain, 4 * NSQ)
            v.sem_inc(xr2_done, 2)
            v.sem_inc(ag_done, 2)
            c1 = Count(stats_chain, STATS_STEPS)
            c2 = Count(y_chain, NY, 2)
            c3 = Count(sq_chain, NSQ, 4)

            def stats(n, q):
                s = q % 2
                c1.start(n)
                v.wait_ge(loaded[q], 32 * uses4(n, q))
                emit_stats(nc, v, c1, x_in[q], st[s], mv[s], divider)
                c1.end()

            def norm(n, q):
                s = q % 2
                c2.start(n)
                v.wait_ge(rstd_chain, (n + 1) * RMS_STEPS)
                v.wait_ge(turned, n + 1)
                emit_apply(nc, c2, x_in[q], y[s], mv[s], rstd[s])
                c2.wait(v)
                for t in range(GT):
                    c2.inc(nc.vector.tensor_scalar(xr[s][:, t, :], y[s][:, t, :], rr[s][:, t:t + 1], None, ALU.mult))
                c2.end()

            def gating(n, q):
                s = q % 2
                v.wait_ge(sig_done, n + 1)
                v.wait_ge(out_done, n + 1)
                nc.vector.tensor_tensor(ag[s][:, :], psA[s][:, :], gate[s][:, :], ALU.mult).then_inc(ag_done, 1)

            def residual(n, q):
                s = q % 2
                c3.start(n)
                v.wait_ge(out_done, n + 3)
                v.wait_ge(stored[s], 32 * uses4(n, s, 2))
                c3.inc(nc.vector.tensor_tensor(yy[s][:, :, :], y[s][:, :, :],
                                               psO[s][:, :].rearrange("p (t c) -> p t c", t=GT), ALU.add))
                c3.wait(v)
                c3.inc(nc.vector.tensor_tensor(total[s][:, :, :], yy[s][:, :, :], x_in[q][:, :, :], ALU.add))
                for t in range(GT):
                    if t >= 2:
                        v.wait_ge(c3.sem, c3.base + c3.c - 1)
                    c3.inc(nc.vector.tensor_tensor_reduce(out=junk[t % 2][:, :], in0=yy[s][:, t, :], in1=yy[s][:, t, :],
                                                          scale=1.0, scalar=0.0, op0=ALU.mult, op1=ALU.add,
                                                          accum_out=sq[s][:, t:t + 1]))
                c3.end()

            def scale(n, q):
                s = q % 2
                v.wait_ge(r2_chain, 2 * n + 6)
                for t in range(GT):
                    last = nc.vector.tensor_scalar(xr2[s][:, t, :], yy[s][:, t, :], r2[s][:, t:t + 1], None, ALU.mult)
                last.then_inc(xr2_done, 1)

            def late(n, q):
                gating(n, q)
                residual(n, q)

            skewed4(v.Fori, NG, [(scale, 4), (late, 3), (norm, 2), (stats, 1)])

        @block.scalar
        def _(a_):
            a_.wait_ge(weights, 64)

            def gates(n, q):
                s = q % 2
                a_.wait_ge(turned, n + 3)
                a_.wait_ge(gate_done, n + 1)
                nc.scalar.activation(xT[s][:, :], psT[s][:, :], ACT.Copy, scale=n1[:, 0:1]).then_inc(xT_copied, 1)
                a_.wait_ge(gate_done, n + 3)
                a_.wait_ge(ag_done, n + 1)
                nc.scalar.activation(gate[s][:, :], psG[s][:, :], ACT.Sigmoid, bias=bg[:, 0:1]).then_inc(sig_done, 1)

            skewed4(a_.Fori, NG, [(gates, 3)])

        @block.tensor
        def _(t_):
            for q in (turned, gate_done, out_done):
                t_.sem_inc(q, 2)
            t_.wait_ge(setup, 2)
            t_.wait_ge(weights, 64)

            def turn(n, q):
                s = q % 2
                t_.wait_ge(ag_done, n + 1)
                t_.wait_ge(loaded[q], 32 * uses4(n, q))
                for t in range(GT):
                    nc.tensor.transpose(psA[s][:, t * P:(t + 1) * P], a_in[q][:, t, :], ident[:, :])
                t_.wait_ge(y_chain, (n + 3) * NY)
                for t in range(GT):
                    last = nc.tensor.transpose(psT[s][:, t * P:(t + 1) * P], xr[s][:, t, :], ident[:, :])
                last.then_inc(turned, 1)

            def rest(n, q):
                s = q % 2
                t_.wait_ge(xT_copied, n + 1)
                nc.tensor.matmul(psG[s][:, :], wg[:, :], xT[s][:, :], start=True, stop=True).then_inc(gate_done, 1)
                t_.wait_ge(ag_done, n + 3)
                t_.wait_ge(sq_chain, NSQ * (n + 3))
                for t in range(GT):
                    last = nc.tensor.matmul(psO[s][:, t * D:(t + 1) * D], ag[s][:, t * P:(t + 1) * P], wo[:, :],
                                            start=True, stop=True)
                last.then_inc(out_done, 1)

            skewed4(t_.Fori, NG, [(rest, 3), (turn, 2)])


def skewed4(fori, count, stages):
    most = max(lag for _, lag in stages)
    first = -(-most // 4) * 4

    def step(quarter, r, fixed):
        for fn, lag in stages:
            q = (r - lag) % 4
            n = 4 * (quarter + (r - lag - q) // 4) + q
            if not fixed or 0 <= n < count:
                fn(n, q)

    for j in range(first):
        step(j // 4, j % 4, True)
    with fori(first // 4, count // 4) as i:
        for r in range(4):
            step(i, r, False)
    for j in range(count, count + most):
        step(j // 4, j % 4, True)


def uses4(n, q, of=4):
    return (n - q) // of + 1


def swiglu_phase(nc, sem, xr_dram, sum_dram, norm2, w_gate, w_up, w_down, x_dram):
    NC = len(F_CHUNKS)
    with Phase(nc, "swi") as ph:
        def two(name, shape, dt=F32):
            return [ph.sb(f"{name}{s}", shape, dt) for s in range(2)]
        xr = two("xr", [P, GT, D])
        res = [ph.sb(f"res{s}", [P, GT, D]) for s in range(4)]
        xT, x3 = two("xT", [P, GW]), two("x3", [P, GT, D])
        sg = two("sg", [P, GW])
        h = [[ph.sb(f"h{s}{c}", [P, GW]) for c in range(NC)] for s in range(2)]
        wg, wu, n2 = ph.sb("wg", [P, FFN1]), ph.sb("wu", [P, FFN1]), ph.sb("n2", [P, 1])
        wd = ph.sb("wd", [P, NC, D])
        ident = ph.sb("ident", [P, P])
        psT, psG, psU, psD = [[ph.ps(f"{k}{s}") for s in range(2)] for k in "TGUD"]
        setup, weights = sem("setup"), sem("weights")
        loaded = [sem(f"loaded{s}") for s in range(4)]
        stored = [sem(f"stored{s}") for s in range(2)]
        turned, xT_copied, up_done, silu_done, h_done, down_done, x3_done = [sem(k) for k in (
            "turned", "xT_copied", "up_done", "silu_done", "h_done", "down_done", "x3_done")]
        block = ph.block()

        @block.sync
        def _(sp):
            for s in range(2):
                sp.sem_inc(stored[s], 16)
            for dst, src in ((wg[:, :], w_gate), (wu[:, :], w_up), (n2[:, :], norm2.rearrange("(c a) -> c a", a=1))):
                sp.dma_start(dst, src).then_inc(weights, 16)
            for c, (f0, fw) in enumerate(F_CHUNKS):
                sp.dma_start(wd[0:fw, c, :], w_down[f0:f0 + fw, :]).then_inc(weights, 16)

            def load(n, q):
                sp.wait_ge(turned, n + 1)
                sp.wait_ge(x3_done, n + 1)
                sp.dma_start(xr[q % 2][:, :, :], rows_of(xr_dram, n)).then_inc(loaded[q], 16)
                sp.dma_start(res[q][:, :, :], rows_of(sum_dram, n)).then_inc(loaded[q], 16)

            def store(n, q):
                sp.wait_ge(x3_done, n + 5)
                sp.dma_start(rows_of(x_dram, n), x3[q % 2][:, :, :]).then_inc(stored[q % 2], 16)

            skewed4(sp.Fori, NG, [(store, 3), (load, 0)])
            for s in range(2):
                sp.wait_ge(stored[s], 16 * (NG // 2 + 1))

        @block.gpsimd
        def _(g):
            emit_identity(nc, g, ident, setup)

        @block.scalar
        def _(a_):
            a_.sem_inc(silu_done, 2)
            a_.sem_inc(xT_copied, 2)
            a_.wait_ge(weights, 96)

            def copy(n, q):
                a_.wait_ge(turned, n + 3)
                a_.wait_ge(up_done, NC * (n + 1))
                nc.scalar.activation(xT[q % 2][:, :], psT[q % 2][:, :], ACT.Copy, scale=n2[:, 0:1]).then_inc(xT_copied, 1)

            def silu(n, q):
                for c, (f0, fw) in enumerate(F_CHUNKS):
                    a_.wait_ge(up_done, NC * (n + 2) + c + 1)
                    a_.wait_ge(h_done, NC * n + c + 1)
                    k = (NC * q + c) % 2
                    nc.scalar.activation(sg[k][0:fw, :], psG[k][0:fw, :], ACT.Silu).then_inc(silu_done, 1)

            skewed4(a_.Fori, NG, [(silu, 2), (copy, 1)])

        @block.vector
        def _(v):
            v.sem_inc(h_done, 2)
            v.sem_inc(x3_done, 4)

            def mult(n, q):
                v.wait_ge(down_done, n + 1)
                for c, (f0, fw) in enumerate(F_CHUNKS):
                    k = (NC * q + c) % 2
                    v.wait_ge(silu_done, NC * n + c + 3)
                    nc.vector.tensor_tensor(h[q % 2][c][0:fw, :], psU[k][0:fw, :], sg[k][0:fw, :], ALU.mult)\
                        .then_inc(h_done, 1)

            def finish(n, q):
                s = q % 2
                v.wait_ge(down_done, n + 3)
                v.wait_ge(loaded[q], 32 * uses4(n, q))
                v.wait_ge(stored[s], 16 * uses4(n, s, 2))
                nc.vector.tensor_tensor(x3[s][:, :, :], res[q][:, :, :],
                                        psD[s][:, :].rearrange("p (t c) -> p t c", t=GT), ALU.add).then_inc(x3_done, 1)

            skewed4(v.Fori, NG, [(finish, 3), (mult, 2)])

        @block.tensor
        def _(t_):
            t_.sem_inc(turned, 2)
            t_.sem_inc(up_done, 2 * NC)
            t_.sem_inc(down_done, 2)
            t_.wait_ge(setup, 2)
            t_.wait_ge(weights, 96)

            def turn(n, q):
                t_.wait_ge(loaded[q], 32 * uses4(n, q))
                t_.wait_ge(xT_copied, n + 1)
                for t in range(GT):
                    last = nc.tensor.transpose(psT[q % 2][:, t * P:(t + 1) * P], xr[q % 2][:, t, :], ident[:, :])
                last.then_inc(turned, 1)

            def up(n, q):
                t_.wait_ge(xT_copied, n + 3)
                for c, (f0, fw) in enumerate(F_CHUNKS):
                    k = (NC * q + c) % 2
                    t_.wait_ge(h_done, NC * n + c + 1)
                    nc.tensor.matmul(psG[k][0:fw, :], wg[:, f0:f0 + fw], xT[q % 2][:, :], start=True, stop=True)
                    nc.tensor.matmul(psU[k][0:fw, :], wu[:, f0:f0 + fw], xT[q % 2][:, :], start=True, stop=True)\
                        .then_inc(up_done, 1)

            def down(n, q):
                t_.wait_ge(h_done, NC * n + NC + 2)
                t_.wait_ge(x3_done, n + 3)
                for t in range(GT):
                    for c, (f0, fw) in enumerate(F_CHUNKS):
                        last = nc.tensor.matmul(psD[q % 2][:, t * D:(t + 1) * D], h[q % 2][c][0:fw, t * P:(t + 1) * P],
                                                wd[0:fw, c, :], start=(c == 0), stop=(c == NC - 1))
                last.then_inc(down_done, 1)

            skewed4(t_.Fori, NG, [(down, 3), (up, 2), (turn, 1)])


LIGHT, HEAVY = D // 2, 4 * D
E_CAP = 20.0
TOP = 128
FETCH = 9.0 / 8.0 * TOP
DESCENTS = 50
STEPS = 7
ROUNDS = (DESCENTS - 1) // STEPS


def two_branch_phase(nc, sem, x_dram, token, light, heavy, base_dram, heavy_dram, s_all):
    HC = HEAVY // P
    with Phase(nc, "two") as ph:
        def two(name, shape, dt=F32):
            return [ph.sb(f"{name}{s}", shape, dt) for s in range(2)]
        x_in = [ph.sb(f"x{s}", [P, GT, D]) for s in range(8)]
        y, z, zT = two("y", [P, GT, D]), two("z", [P, GT, D]), two("zT", [P, GW])
        hl, hh = two("hl", [LIGHT, GW]), two("hh", [P, HC, GW])
        base, hv, junk = two("base", [P, GT, D]), two("hv", [P, GT, D]), two("junk", [P, D])
        st, mv, rstd, rr = two("st", [P, GT, 6]), two("mv", [P, GT, 2]), two("rstd", [P, GT]), two("rr", [P, GT])
        w1l, w1h = ph.sb("w1l", [P, LIGHT]), ph.sb("w1h", [P, HEAVY])
        w2l, w2h = ph.sb("w2l", [LIGHT, D]), ph.sb("w2h", [P, HC, D])
        gl, gh = ph.sb("gl", [P, 1]), ph.sb("gh", [P, 1])
        b1l, b1h = ph.sb("b1l", [LIGHT, 1]), ph.sb("b1h", [P, HC])
        b2l, b2h, tok = ph.sb("b2l", [P, 1, D]), ph.sb("b2h", [P, 1, D]), ph.sb("tok", [P, D])
        ident, power = ph.sb("ident", [P, P]), ph.sb("power", [P, GT])
        psT = [ph.ps("psT0")]
        psL = [ph.ps("psL0")]
        psH = [ph.ps(f"psH{s}") for s in range(2)]
        psDL, psDH = [[ph.ps(f"{k}{s}") for s in range(2)] for k in ("DL", "DH")]
        setup, weights, scaled = sem("setup"), sem("weights"), sem("scaled")
        divider = sem("divider")
        loaded = [sem(f"loaded{s}") for s in range(8)]
        stored = [sem(f"stored{s}") for s in range(2)]
        stats_chain, rstd_chain, y_chain, turned, zT_copied = [sem(k) for k in (
            "stats_chain", "rstd_chain", "y_chain", "turned", "zT_copied")]
        up_done, gelu_done, down_done, out_done = [sem(k) for k in ("up_done", "gelu_done", "down_done", "out_done")]
        base_step = sem("base_step")
        NY = 3 * GT
        UP = HC + 1
        block = ph.block()
        one = lambda a: a.rearrange("(c a) -> c a", a=1)
        loads = [(w1l[:, :], light[1]), (w1h[:, :], heavy[1]), (w2l[:, :], light[3]),
                 (w2h[:, :, :], heavy[3].rearrange("(m p) c -> p m c", p=P)), (gl[:, :], one(light[0])),
                 (gh[:, :], one(heavy[0])), (b1l[:, :], one(light[2])), (b2l[:, 0, :], bc_rows(light[4], D)),
                 (b2h[:, 0, :], bc_rows(heavy[4], D)), (tok[:, :], bc_rows(token, D))]
        loads += [(b1h[:, m:m + 1], one(heavy[2][m * P:(m + 1) * P])) for m in range(HC)]
        NW = 16 * len(loads)

        @block.sync
        def _(sp):
            for s in range(2):
                sp.sem_inc(stored[s], 32)
            for dst, src in loads:
                sp.dma_start(dst, src).then_inc(weights, 16)

            def load(n, q):
                sp.wait_ge(out_done, n + 1)
                sp.dma_start(x_in[q][:, :, :], rows_of(x_dram, n)).then_inc(loaded[q], 16)

            def store(n, q):
                s = q % 2
                sp.wait_ge(out_done, n + 9)
                sp.dma_start(rows_of(base_dram, n), base[s][:, :, :]).then_inc(stored[s], 16)
                sp.dma_start(rows_of(heavy_dram, n), hv[s][:, :, :]).then_inc(stored[s], 16)

            skewed8(sp.Fori, NG, [(store, 5), (load, 0)])
            for s in range(2):
                sp.wait_ge(stored[s], 32 * (NG // 2 + 1))

        @block.gpsimd
        def _(g):
            emit_identity(nc, g, ident, setup)
            g.memset(power[:, :], -0.5).then_inc(setup, 1)
            g.wait_ge(setup, 3)
            rc = Count(rstd_chain, RMS_STEPS)

            def rstds(n, q):
                s = q % 2
                wait_apart(g, divider, (stats_chain, (n + 1) * STATS_STEPS), (y_chain, (n + 1) * NY))
                rc.start(n)
                emit_rstd(nc, g, rc, mv[s], rstd[s], power, divider, rms=(None, rr[s]))
                rc.end()

            skewed8(g.Fori, NG, [(rstds, 1)])

        @block.vector
        def _(v):
            v.sem_inc(y_chain, 2 * NY)
            v.sem_inc(out_done, 8)
            c1 = Count(stats_chain, STATS_STEPS)
            c2 = Count(y_chain, NY, 2)
            v.wait_ge(weights, NW)
            nc.vector.tensor_scalar(w1l[:, :], w1l[:, :], gl[:, 0:1], None, ALU.mult).then_inc(scaled, 1)
            nc.vector.tensor_scalar(w1h[:, :], w1h[:, :], gh[:, 0:1], None, ALU.mult).then_inc(scaled, 1)

            def stats(n, q):
                s = q % 2
                c1.start(n)
                v.wait_ge(loaded[q], 16 * uses4(n, q, 8))
                emit_stats(nc, v, c1, x_in[q], st[s], mv[s], divider)
                c1.end()

            def norm(n, q):
                s = q % 2
                c2.start(n)
                v.wait_ge(rstd_chain, (n + 1) * RMS_STEPS)
                v.wait_ge(turned, n + 1)
                emit_apply(nc, c2, x_in[q], y[s], mv[s], rstd[s])
                c2.wait(v)
                for t in range(GT):
                    c2.inc(nc.vector.tensor_scalar(z[s][:, t, :], y[s][:, t, :], rr[s][:, t:t + 1], None, ALU.mult))
                for t in range(GT):
                    if t >= 2:
                        v.wait_ge(c2.sem, c2.base + c2.c - 1)
                    c2.inc(nc.vector.tensor_tensor_reduce(out=junk[t % 2][:, :], in0=y[s][:, t, :], in1=tok[:, :],
                                                          scale=1.0, scalar=0.0, op0=ALU.mult, op1=ALU.add,
                                                          accum_out=s_all[:, bass.ds(n * GT + t, 1)]))
                c2.end()

            def finish(n, q):
                s = q % 2
                v.wait_ge(down_done, n + 3)
                v.wait_ge(stored[s], 32 * uses4(n, s, 2))
                nc.vector.tensor_tensor(base[s][:, :, :], x_in[q][:, :, :],
                                        psDL[s][:, :].rearrange("p (t c) -> p t c", t=GT), ALU.add).then_inc(base_step, 1)
                nc.vector.tensor_tensor(hv[s][:, :, :], psDH[s][:, :].rearrange("p (t c) -> p t c", t=GT),
                                        b2h[:, :, :].to_broadcast([P, GT, D]), ALU.add)
                v.wait_ge(base_step, n + 1)
                nc.vector.tensor_tensor(base[s][:, :, :], base[s][:, :, :], b2l[:, :, :].to_broadcast([P, GT, D]),
                                        ALU.add).then_inc(out_done, 1)

            skewed8(v.Fori, NG, [(finish, 5), (norm, 2), (stats, 1)])

        @block.scalar
        def _(a_):
            a_.sem_inc(gelu_done, 2 * UP)
            a_.wait_ge(weights, NW)

            def gelus(n, q):
                s = q % 2
                a_.wait_ge(down_done, n + 1)
                for c in range(UP):
                    a_.wait_ge(up_done, UP * n + c + 1)
                    if c == 0:
                        ins = nc.scalar.activation(hl[s][:, :], psL[0][0:LIGHT, :], ACT.Gelu, bias=b1l[:, 0:1])
                    else:
                        ins = nc.scalar.activation(hh[s][:, c - 1, :], psH[c % 2][:, :], ACT.Gelu, bias=b1h[:, c - 1:c])
                    ins.then_inc(gelu_done, 1)

            def copy(n, q):
                a_.wait_ge(turned, n + 3)
                a_.wait_ge(up_done, UP * (n - 1)) if isinstance(n, int) and n >= 2 else (
                    a_.wait_ge(up_done, UP * (n - 1)) if not isinstance(n, int) else None)
                nc.scalar.activation(zT[q % 2][:, :], psT[0][:, :], ACT.Copy).then_inc(zT_copied, 1)

            skewed8(a_.Fori, NG, [(gelus, 4), (copy, 3)])

        @block.tensor
        def _(t_):
            t_.sem_inc(turned, 2)
            t_.sem_inc(down_done, 2)
            t_.wait_ge(setup, 2)
            t_.wait_ge(scaled, 2)

            def turn(n, q):
                t_.wait_ge(y_chain, (n + 3) * NY)
                if not (isinstance(n, int) and n == 0):
                    t_.wait_ge(zT_copied, n)
                for t in range(GT):
                    last = nc.tensor.transpose(psT[0][:, t * P:(t + 1) * P], z[q % 2][:, t, :], ident[:, :])
                last.then_inc(turned, 1)

            def up(n, q):
                t_.wait_ge(zT_copied, n + 1)
                for c in range(UP):
                    if c == 0:
                        t_.wait_ge(gelu_done, UP * (n + 1) + 1)
                        ins = nc.tensor.matmul(psL[0][0:LIGHT, :], w1l[:, :], zT[q % 2][:, :], start=True, stop=True)
                    else:
                        t_.wait_ge(gelu_done, UP * (n + 1) + c + 2 if c <= 2 else UP * (n + 2) + c - 1)
                        ins = nc.tensor.matmul(psH[c % 2][:, :], w1h[:, (c - 1) * P:c * P], zT[q % 2][:, :],
                                               start=True, stop=True)
                    ins.then_inc(up_done, 1)

            def down(n, q):
                s = q % 2
                t_.wait_ge(gelu_done, UP * (n + 3))
                t_.wait_ge(out_done, n + 7)
                for t in range(GT):
                    nc.tensor.matmul(psDL[s][:, t * D:(t + 1) * D], hl[s][:, t * P:(t + 1) * P], w2l[:, :],
                                     start=True, stop=True)
                for t in range(GT):
                    for m in range(HC):
                        last = nc.tensor.matmul(psDH[s][:, t * D:(t + 1) * D], hh[s][:, m, t * P:(t + 1) * P],
                                                w2h[:, m, :], start=(m == 0), stop=(m == HC - 1))
                last.then_inc(down_done, 1)

            skewed8(t_.Fori, NG, [(down, 5), (up, 4), (turn, 3)])


def skewed8(fori, count, stages):
    most = max(lag for _, lag in stages)
    assert most <= 8

    def step(eighth, r, fixed):
        for fn, lag in stages:
            q = (r - lag) % 8
            n = 8 * (eighth + (r - lag - q) // 8) + q
            if not fixed or 0 <= n < count:
                fn(n, q)

    for j in range(8):
        step(0, j, True)
    if count > 16:
        with fori(1, count // 8) as i:
            for r in range(8):
                step(i, r, False)
    else:
        for r in range(8):
            step(1, r, True)
    for j in range(count, count + most):
        step(j // 8, j % 8, True)


def descent_phase(nc, sem, s_all, coef_all):
    assert DESCENTS - 1 == ROUNDS * STEPS and STEPS * math.log(S / FETCH) < E_CAP
    assert STEPS * math.log(FETCH) < 40.0
    ROWS = NT
    LOGK = math.log(FETCH)
    with Phase(nc, "desc") as ph:
        s64, t64, e64 = ph.sb("s64", [ROWS, P]), ph.sb("t64", [ROWS, P]), ph.sb("e64", [ROWS, P])
        s8, key8, work = ph.sb("s8", [B, S]), ph.sb("key8", [B, S]), [ph.sb(f"work{k}", [B, S]) for k in range(2)]
        sc8, gt8, eq8, cum8, zeros = [ph.sb(k, [B, S]) for k in ("sc8", "gt8", "eq8", "cum8", "zeros")]
        key64, low64 = ph.sb("key64", [ROWS, P]), ph.sb("low64", [ROWS, P])
        coef64 = ph.sb("coef64", [ROWS, P])
        top8 = ph.sb("top8", [B, 8])
        smax8, smax, nega, M, lnz, acc = [ph.sb(k, [ROWS, 1]) for k in ("smax8", "smax", "nega", "M", "lnz", "acc")]
        need = ph.sb("need", [B, 1])
        spread, same, ident = ph.sb("spread", [B, B, 8]), ph.sb("same", [ROWS, B, 8]), ph.sb("ident", [P, P])
        psA, psB = ph.ps("psA"), ph.ps("psB")
        divider, summed = sem("divider"), sem("summed")
        setup, turned, chain, moved, zed, expd, lnd, dd = [sem(k) for k in (
            "setup", "turned", "chain", "moved", "zed", "expd", "lnd", "dd")]
        block = ph.block()

        @block.gpsimd
        def _(g):
            emit_identity(nc, g, ident, setup)
            g.memset(spread[:, :, :], 0.0)
            g.memset(same[:, :, :], 1.0 / FETCH)
            g.memset(zeros[:, :], 0.0).then_inc(setup, 1)
            g.wait_ge(setup, 3)
            g.affine_select(out=spread[:, :, :], in_=spread[:, :, :], compare_op=ALU.not_equal, fill=1.0, base=0,
                            pattern=[[-1, B], [0, 8]], channel_multiplier=1)
            g.affine_select(out=same[:, :, :], in_=same[:, :, :], compare_op=ALU.is_ge, fill=0.0, base=0,
                            pattern=[[-8, B], [0, 8]], channel_multiplier=1).then_inc(setup, 1)
            g.wait_ge(setup, 4)
            g.affine_select(out=same[:, :, :], in_=same[:, :, :], compare_op=ALU.is_ge, fill=0.0, base=7,
                            pattern=[[8, B], [0, 8]], channel_multiplier=-1).then_inc(setup, 1)

        @block.tensor
        def _(t_):
            t_.wait_ge(setup, 5)
            nc.tensor.transpose(psA[0:ROWS, 0:P], s_all[:, :], ident[:, :]).then_inc(turned, 1)
            t_.wait_ge(chain, 2)
            nc.tensor.matmul(psB[0:ROWS, 0:1], spread[:, :, :].rearrange("b c j -> b (c j)"), smax8[0:B, :],
                             start=True, stop=True).then_inc(turned, 1)
            with t_.Fori(0, ROUNDS) as r:
                for j in range(STEPS):
                    wait_apart(t_, divider, (summed, STEPS * r + j + 1))
                    nc.tensor.matmul(psA[0:ROWS, 256:257], same[:, :, :].rearrange("b c j -> b (c j)"), acc[:, :],
                                     start=True, stop=True).then_inc(zed, 1)
            t_.wait_ge(moved, 48)
            nc.tensor.transpose(psB[:, 128:128 + ROWS], coef64[:, :], ident[0:ROWS, 0:ROWS]).then_inc(turned, 1)

        @block.scalar
        def _(a_):
            with a_.Fori(0, ROUNDS) as r:
                a_.wait_ge(dd, 3 * r + 3)
                nc.scalar.activation(e64[:, :], t64[:, :], ACT.Exp).then_inc(expd, 1)
                a_.wait_ge(zed, STEPS * r + STEPS)
                nc.scalar.activation(lnz[:, :], psA[0:ROWS, 256:257], ACT.Ln).then_inc(lnd, 1)
            a_.wait_ge(moved, 32)
            nc.scalar.activation(sc8[:, :], key8[:, :], ACT.Exp).then_inc(expd, 1)

        @block.sync
        def _(sp):
            sp.wait_ge(chain, 1)
            sp.dma_start(s8[:, :], s64[:, :]).then_inc(moved, 16)
            sp.wait_ge(chain, 5)
            sp.dma_start(key8[:, :], key64[:, :]).then_inc(moved, 16)
            sp.wait_ge(lnd, ROUNDS + 1)
            sp.dma_start(coef64[:, :], gt8[:, :]).then_inc(moved, 16)

        @block.vector
        def _(v):
            c = Count(chain, 0)

            def link(ins):
                c.inc(ins)
                c.wait(v)

            v.wait_ge(turned, 1)
            link(nc.vector.tensor_copy(s64[:, :], psA[0:ROWS, 0:P]))
            v.wait_ge(moved, 16)
            link(nc.vector.tensor_reduce(smax8[0:B, :], s8[:, :], AX.X, ALU.max))
            v.wait_ge(turned, 2)
            link(nc.vector.tensor_copy(smax[:, :], psB[0:ROWS, 0:1]))
            nc.vector.memset(nega[:, :], math.log(S) - LOGK).then_inc(dd, 1)
            with v.Fori(0, ROUNDS) as r:
                v.wait_ge(dd, 3 * r + 1)
                nc.vector.tensor_tensor(M[:, :], smax[:, :], nega[:, :], ALU.min).then_inc(dd, 1)
                v.wait_ge(dd, 3 * r + 2)
                nc.vector.tensor_scalar(t64[:, :], s64[:, :], M[:, 0:1], E_CAP, ALU.subtract, ALU.min).then_inc(dd, 1)
                for j in range(STEPS):
                    if j == 0:
                        v.wait_ge(expd, r + 1)
                    else:
                        v.wait_ge(zed, STEPS * r + j)
                    nc.vector.tensor_scalar(low64[:, :], e64[:, :], psA[0:ROWS, 256:257] if j else 1.0, 0.0, ALU.min,
                                            ALU.add, accum_out=acc[:, :]).then_inc(summed, 1)
                v.wait_ge(lnd, r + 1)
                nc.vector.tensor_tensor(nega[:, :], lnz[:, :], M[:, :], ALU.add).then_inc(dd, 1)
            v.wait_ge(dd, 3 * ROUNDS + 1)
            link(nc.vector.tensor_scalar(key64[:, :], s64[:, :], nega[:, 0:1], 0.0, ALU.subtract, ALU.min))
            link(nc.vector.tensor_scalar(key64[:, :], key64[:, :], -104.0, None, ALU.max))
            v.wait_ge(moved, 32)
            cur = key8
            for r in range(TOP // 8):
                link(nc.vector.max(top8[:, :], cur[:, :]))
                if r < TOP // 8 - 1:
                    link(nc.vector.match_replace(work[r % 2][:, :], top8[:, :], cur[:, :], -1.0e30))
                    cur = work[r % 2]
            bar = top8[:, 7:8]
            link(nc.vector.tensor_scalar(gt8[:, :], key8[:, :], bar, None, ALU.is_gt))
            link(nc.vector.tensor_scalar(eq8[:, :], key8[:, :], bar, None, ALU.is_equal))
            link(nc.vector.tensor_reduce(need[:, :], gt8[:, :], AX.X, ALU.add))
            link(nc.vector.tensor_scalar(need[:, :], need[:, :], -1.0, float(TOP), ALU.mult, ALU.add))
            link(nc.vector.tensor_tensor_scan(cum8[:, :], eq8[:, :], zeros[:, :], 0.0, ALU.add, ALU.add))
            link(nc.vector.scalar_tensor_tensor(out=eq8[:, :], in0=cum8[:, :], scalar=need[:, 0:1], in1=eq8[:, :],
                                                op0=ALU.is_le, op1=ALU.mult))
            link(nc.vector.tensor_tensor(gt8[:, :], gt8[:, :], eq8[:, :], ALU.add))
            v.wait_ge(expd, ROUNDS + 1)
            link(nc.vector.tensor_scalar(eq8[:, :], sc8[:, :], -1.0, 1.0, ALU.mult, ALU.add))
            link(nc.vector.tensor_tensor(eq8[:, :], eq8[:, :], sc8[:, :], ALU.add))
            nc.vector.tensor_tensor(gt8[:, :], gt8[:, :], eq8[:, :], ALU.mult).then_inc(lnd, 1)
            v.wait_ge(turned, 3)
            nc.vector.tensor_copy(coef_all[:, :], psB[:, 128:128 + ROWS]).then_inc(dd, 1)


def last_phase(nc, sem, base_dram, heavy_dram, coef_all, out_dram):
    with Phase(nc, "last") as ph:
        base = [ph.sb(f"b{s}", [P, GT, D]) for s in range(2)]
        hv = [ph.sb(f"h{s}", [P, GT, D]) for s in range(2)]
        out = [ph.sb(f"o{s}", [P, GT, D]) for s in range(2)]
        loaded = [sem(f"loaded{s}") for s in range(2)]
        stored = [sem(f"stored{s}") for s in range(2)]
        summed = sem("summed")
        block = ph.block()

        @block.sync
        def _(sp):
            def load(n, s):
                sp.wait_ge(summed, n + 1)
                sp.dma_start(base[s][:, :, :], rows_of(base_dram, n)).then_inc(loaded[s], 16)
                sp.dma_start(hv[s][:, :, :], rows_of(heavy_dram, n)).then_inc(loaded[s], 16)

            skewed(sp.Fori, NG, [(load, 0)])

        @block.vector
        def _(v):
            v.sem_inc(summed, 2)

            def total(n, s):
                v.wait_ge(loaded[s], 32 * uses4(n, s, 2))
                v.wait_ge(stored[s], 16 * uses4(n, s, 2))
                for t in range(GT):
                    last = nc.vector.scalar_tensor_tensor(
                        out=out[s][:, t, :], in0=hv[s][:, t, :], scalar=coef_all[:, bass.ds(n * GT + t, 1)],
                        in1=base[s][:, t, :], op0=ALU.mult, op1=ALU.add)
                last.then_inc(summed, 1)

            skewed(v.Fori, NG, [(total, 0)])

        @block.scalar
        def _(a_):
            for s in range(2):
                a_.sem_inc(stored[s], 16)

            def store(n, s):
                a_.wait_ge(summed, n + 3)
                a_.dma_start(rows_of(out_dram, n), out[s][:, :, :]).then_inc(stored[s], 16)

            skewed(a_.Fori, NG, [(store, 0)])
            for s in range(2):
                a_.wait_ge(stored[s], 16 * (NG // 2 + 1))


def program(nc, x, i, out):
    U32 = mybir.dt.uint32
    phase_name, used = [""], []

    def sem(name):
        used.append(nc.alloc_semaphore(name=f"{phase_name[0]}_{name}"))
        return used[-1]

    def give_back():
        nc.clear_and_free_semaphores(used)
        nc.all_engine_barrier()
        used.clear()

    if True:

        def dram(name, shape, dt=F32):
            return nc.dram_tensor(name, shape, dt, kind="Internal").ap()

        qd, kd = [dram(k, [H, 3 * HD, T], BF16) for k in ("q_parts", "k_parts")]
        vd, att = dram("values", [T, D]), dram("attention", [T, D])
        x1, xn, x2, x3 = dram("x1", [T, D]), dram("xn", [T, D]), dram("x2", [T, D]), dram("x3", [T, D])
        xsorted, ysorted = dram("x_sorted", [SORTED_TILES * P, D]), dram("y_sorted", [SORTED_TILES * P, D])
        fwd, rev = dram("bias_fwd", [H, 2 * WINDOW]), dram("bias_rev", [H, 2 * WINDOW])

        phase_name[0] = "qkv0"
        qkv_phase(nc, sem, "qkv0", x, i["L0_attn_w_qkv"], HD ** -0.5, qd, kd, vd)
        phase_name[0] = "att0"
        attention_phase(nc, sem, "att0", qd, kd, vd, att, True)
        with ExitStack() as moe:
            def keep(name, shape, dt=F32):
                return moe.enter_context(nc.sbuf_tensor(name, shape, dt))
            onehot, weight = keep("onehot", [P, NT, NE]), keep("weight", [P, NT])
            place, expert_row = keep("place", [P, NT], U32), keep("expert_row", [P, SORTED_TILES], I32)
            phase_name[0] = "mix"
            mix_phase(nc, sem, x, att, i["L0_attn_w_out"], i["L0_ffn_gate_w"], x1, xn, onehot, weight)
            phase_name[0] = "place"
            place_phase(nc, sem, onehot, place, expert_row)
            phase_name[0] = "scatter"
            scatter_phase(nc, sem, xn, xsorted, place)
            phase_name[0] = "experts"
            experts_phase(nc, sem, xsorted, ysorted, i["L0_ffn_w1"], i["L0_ffn_b1"], i["L0_ffn_w2"], i["L0_ffn_b2"],
                          expert_row)
            phase_name[0] = "gather"
            gather_phase(nc, sem, x1, ysorted, place, weight, x2)
        give_back()
        phase_name[0] = "bias"
        bias_phase(nc, sem, i["L1_attn_offsets"], i["L1_attn_pos_bias"], fwd, rev)
        phase_name[0] = "qkv1"
        qkv_phase(nc, sem, "qkv1", x2, i["L1_attn_w_qkv"], HD ** -0.5, qd, kd, vd, i["L1_attn_norm1_scale"])
        phase_name[0] = "att1"
        attention_phase(nc, sem, "att1", qd, kd, vd, att, False, rev, fwd)
        phase_name[0] = "gated"
        gated_phase(nc, sem, x2, att, i["L1_attn_w_gate"], i["L1_attn_b_gate"], i["L1_attn_norm1_scale"],
                    i["L1_attn_w_out"], x1, xn)
        phase_name[0] = "swiglu"
        swiglu_phase(nc, sem, xn, x1, i["L1_attn_norm2_scale"], i["L1_attn_w_ffn_gate"], i["L1_attn_w_ffn_up"],
                     i["L1_attn_w_ffn_down"], x3)
        with ExitStack() as route:
            s_all = route.enter_context(nc.sbuf_tensor("s_all", [P, NT], F32))
            coef = route.enter_context(nc.sbuf_tensor("coef", [P, NT], F32))
            phase_name[0] = "two"
            two_branch_phase(nc, sem, x3, i["L1_ffn_routing_token"],
                             [i[f"L1_ffn_light_{k}"] for k in ("gamma", "w1", "b1", "w2", "b2")],
                             [i[f"L1_ffn_heavy_{k}"] for k in ("gamma", "w1", "b1", "w2", "b2")], x1, x2, s_all)
            phase_name[0] = "descent"
            descent_phase(nc, sem, s_all, coef)
            phase_name[0] = "last"
            last_phase(nc, sem, x1, x2, coef, out)


def kernel(**inputs):
    import numpy as np
    import concourse.bacc as bacc
    from concourse.bass_utils import run_bass_kernel_spmd

    nc = bacc.Bacc("TRN2", target_bir_lowering=False, num_devices=1)
    arrays, given = {}, {}
    for name, a in inputs.items():
        a = np.ascontiguousarray(a)
        if name == "L0_attn_x":
            a = a.reshape(T, D)
        arrays[f"in_{name}"] = a
        given[name] = nc.dram_tensor(f"in_{name}", a.shape, mybir.dt.from_np(a.dtype), kind="ExternalInput").ap()
    out = nc.dram_tensor("out", (T, D), F32, kind="ExternalOutput").ap()
    program(nc, given["L0_attn_x"], given, out)
    r = run_bass_kernel_spmd(nc, [arrays], core_ids=[0])
    return r.results[0]["out"].reshape(B, S, D)
```

```python
from contextlib import ExitStack
import math

import concourse.bass as bass
from concourse import mybir

F32 = mybir.dt.float32
BF16 = mybir.dt.bfloat16
I32 = mybir.dt.int32
ACT = mybir.ActivationFunctionType
ALU = mybir.AluOpType
AX = mybir.AxisListType

P = 128
B, S, D = 8, 1024, 128
T = B * S
H, HD = 16, 8
TB = S // P
NT = T // P
GT = 4
GW = GT * P
NG = T // GW
HG = 4
NHG = H // HG
SPLIT_ROWS = 6 * HD
PAD_ROWS = 96
ALL_ROWS = PAD_ROWS + 3
Q_RUNS = ((0, 2), (0, 1), (0, 0))
K_RUNS = ((0, 0), (0, 0), (0, 0), (1, 1), (1, 1), (2, 2))
MASKED = -1.0e30
NE, FF = 8, 512
NOFF = 38
WINDOW = 256
WB = WINDOW // P + 1
FFN1 = 352
F_CHUNKS = ((0, 128), (128, 128), (256, 96))
LN_EPS, RMS_EPS = 1e-5, 1e-6
TINY = 1e-24 / D


class Count:

    def __init__(self, sem, per, credits=0):
        self.sem, self.per, self.credits, self.base, self.c = sem, per, credits, 0, 0

    def start(self, n):
        self.base, self.c = (n + self.credits) * self.per, 0

    def inc(self, ins, k=1):
        ins.then_inc(self.sem, k)
        self.c += k

    def wait(self, eng):
        eng.wait_ge(self.sem, self.base + self.c)

    def wait_apart(self, eng, divider):
        wait_apart(eng, divider, (self.sem, self.base + self.c))

    def end(self):
        assert self.c == self.per, (self.c, self.per)


class Phase:

    def __init__(self, nc, name):
        self.nc, self.name, self.ctx = nc, name, ExitStack()

    def __enter__(self):
        self.ctx.__enter__()
        return self

    def __exit__(self, *a):
        return self.ctx.__exit__(*a)

    def sb(self, name, shape, dt=F32):
        return self.ctx.enter_context(self.nc.sbuf_tensor(f"{self.name}_{name}", shape, dt))

    def ps(self, name, shape=(P, 512), dt=F32):
        return self.ctx.enter_context(self.nc.psum_tensor(f"{self.name}_{name}", list(shape), dt))

    def block(self):
        return self.ctx.enter_context(self.nc.Block())


def wait_apart(eng, divider, *waits):
    for sem, value in waits:
        eng.wait_ge(sem, value)
    eng.sem_inc(divider, 1)


def rows_of(dram, n):
    return dram[bass.ds(n * GW, GW), :].rearrange("(t p) c -> p t c", p=P)


def bc_rows(vec, width):
    return bass.AP(tensor=vec.tensor, offset=vec.offset, ap=[[0, P], [1, width]])


def skewed(fori, count, stages, by=2):
    most = max(lag for _, lag in stages)
    first = -(-most // by)

    def step(turn, r, fixed):
        for fn, lag in stages:
            q = (r - lag) % by
            n = by * (turn + (r - lag - q) // by) + q
            if not fixed or 0 <= n < count:
                fn(n, q)

    for j in range(first * by):
        step(j // by, j % by, True)
    if count // by - first > 1:
        with fori(first, count // by) as i:
            for r in range(by):
                step(i, r, False)
    else:
        for j in range(first * by, count):
            step(j // by, j % by, True)
    for j in range(count, count + most):
        step(j // by, j % by, True)


def uses(n, s, of=2):
    return (n - s) // of + 1


def emit_identity(nc, eng, ident, sem):
    eng.memset(ident[:, :], 0.0).then_inc(sem, 1)
    eng.wait_ge(sem, 1)
    eng.affine_select(out=ident[:, :], in_=ident[:, :], compare_op=ALU.not_equal, fill=1.0, base=0,
                      pattern=[[-1, P]], channel_multiplier=1).then_inc(sem, 1)


def emit_stats(nc, v, ch, x, st, mv, divider):
    for t in range(GT):
        ch.inc(nc.vector.bn_stats(st[:, t, :], x[:, t, :]))
    ch.wait_apart(v, divider)
    for t in range(GT):
        ch.inc(nc.vector.bn_aggr(mv[:, t, :], st[:, t, :]))


def emit_rstd(nc, g, ch, mv, rstd, power, divider, eps=LN_EPS, rms=None):
    ch.inc(nc.gpsimd.tensor_scalar(rstd[:, :], mv[:, :, 1], eps, None, ALU.add))
    ch.wait(g)
    ch.inc(nc.gpsimd.tensor_tensor(rstd[:, :], rstd[:, :], power[:, :], ALU.pow))
    if rms is not None:
        rms_eps, r = rms
        ch.wait(g)
        ch.inc(nc.gpsimd.tensor_tensor(r[:, :], mv[:, :, 1], rstd[:, :], ALU.mult))
        ch.wait(g)
        ch.inc(nc.gpsimd.tensor_tensor(r[:, :], r[:, :], rstd[:, :], ALU.mult))
        ch.wait_apart(g, divider)
        if rms_eps is None:
            ch.inc(nc.gpsimd.tensor_scalar(r[:, :], r[:, :], TINY, None, ALU.max))
        else:
            ch.inc(nc.gpsimd.tensor_scalar(r[:, :], r[:, :], rms_eps, None, ALU.add))
        ch.wait(g)
        ch.inc(nc.gpsimd.tensor_tensor(r[:, :], r[:, :], power[:, :], ALU.pow))


RSTD_STEPS, RMS_STEPS = 2, 6


def emit_apply(nc, ch, x, y, mv, rstd):
    for t in range(GT):
        ch.inc(nc.vector.tensor_scalar(y[:, t, :], x[:, t, :], mv[:, t, 0:1], rstd[:, t:t + 1],
                                       ALU.subtract, ALU.mult))


STATS_STEPS = 2 * GT


def qkv_phase(nc, sem, name, x_dram, w_qkv, q_scale, qd, kd, vd, norm_scale=None):
    rms = norm_scale is not None
    with Phase(nc, name) as ph:
        x_in = [ph.sb(f"x{s}", [P, GT, D]) for s in range(4)]
        xn = [ph.sb(f"xn{s}", [P, GT, D]) for s in range(2)]
        xr = [ph.sb(f"xr{s}", [P, GT, D]) for s in range(2)] if rms else xn
        xnT = [ph.sb(f"xnT{s}", [P, GW]) for s in range(2)]
        st = [ph.sb(f"st{s}", [P, GT, 6]) for s in range(2)]
        mv = [ph.sb(f"mv{s}", [P, GT, 2]) for s in range(2)]
        rstd = [ph.sb(f"rstd{s}", [P, GT]) for s in range(2)]
        rr = [ph.sb(f"rr{s}", [P, GT]) for s in range(2)]
        power = ph.sb("power", [P, GT])
        w = ph.sb("w", [P, 3 * D])
        ident = ph.sb("ident", [P, P])
        nscale = ph.sb("nscale", [P, 1])
        parts = [[ph.sb(f"part{s}{a}", [P, 3, GW], BF16) for a in range(2)] for s in range(2)]
        rest = [[ph.sb(f"rest{s}{a}", [P, GW]) for a in range(2)] for s in range(2)]
        v_out = [ph.sb(f"v{s}", [P, GT, D]) for s in range(2)]
        ps_t = [ph.ps(f"pst{s}") for s in range(2)]
        ps_q = [[ph.ps(f"psq{s}{a}") for a in range(2)] for s in range(2)]
        ps_v = [ph.ps(f"psv{s}") for s in range(2)]

        setup, divider = sem("setup"), sem("divider")
        w_ready = sem("w_ready")
        w_scaled = sem("w_scaled")
        x_loaded = [sem(f"x_loaded{s}") for s in range(4)]
        norm_chain = sem("norm_chain")
        t_done = sem("t_done")
        xnT_ready = sem("xnT_ready")
        qk_done = sem("qk_done")
        v_done = sem("v_done")
        high_ready = sem("high_ready")
        v_copied = sem("v_copied")
        split_chain = sem("split_chain")
        parts_stored = [sem(f"parts_stored{s}") for s in range(2)]
        v_stored = [sem(f"v_stored{s}") for s in range(2)]
        n_consts = 32 if rms else 16
        NSTORE = 16 * 6
        KN = 2 * GT if rms else GT
        KR = RMS_STEPS if rms else RSTD_STEPS
        rstd_chain = sem("rstd_chain")
        stats_chain = sem("stats_chain")
        SPLIT_STEPS = 5

        block = ph.block()

        @block.gpsimd
        def _(g):
            emit_identity(nc, g, ident, setup)
            g.memset(power[:, :], -0.5).then_inc(setup, 1)
            g.wait_ge(setup, 3)
            rc = Count(rstd_chain, KR)

            def rstds(n, quarter):
                s = quarter % 2
                wait_apart(g, divider, (stats_chain, (n + 1) * STATS_STEPS), (norm_chain, (n + 3) * KN))
                rc.start(n)
                emit_rstd(nc, g, rc, mv[s], rstd[s], power, divider, rms=(RMS_EPS, rr[s]) if rms else None)
                rc.end()

            skewed(g.Fori, NG, [(rstds, 1)], by=4)

        @block.sync
        def _(sp):
            sp.dma_start(w[:, :], w_qkv).then_inc(w_ready, 16)
            if rms:
                sp.dma_start(nscale[:, :], norm_scale.rearrange("(c a) -> c a", a=1)).then_inc(w_ready, 16)

            def load(n, quarter):
                sp.wait_ge(norm_chain, (n + 1) * KN)
                sp.dma_start(x_in[quarter][:, :, :], rows_of(x_dram, n)).then_inc(x_loaded[quarter], 16)

            def store(n, quarter):
                s = quarter % 2
                sp.wait_ge(split_chain, (n + 1) * SPLIT_STEPS)
                for a, dst in enumerate((qd, kd)):
                    for part in range(3):
                        sp.dma_start(dst[:, part * HD:(part + 1) * HD, bass.ds(n * GW, GW)],
                                     parts[s][a][:, part, :]).then_inc(parts_stored[s], 16)

            skewed(sp.Fori, NG, [(store, 4), (load, 0)], by=4)
            for s in range(2):
                sp.wait_ge(parts_stored[s], NSTORE * (NG // 2 + 1))

        @block.vector
        def _(v):
            v.sem_inc(norm_chain, 4 * KN)
            sc0 = Count(stats_chain, STATS_STEPS)
            ch = Count(norm_chain, KN, 4)
            sc = Count(split_chain, SPLIT_STEPS)
            v.wait_ge(w_ready, n_consts)
            nc.vector.tensor_scalar(w[:, 0:D], w[:, 0:D], q_scale, None, ALU.mult).then_inc(w_scaled, 1)

            def stats(n, quarter):
                s = quarter % 2
                sc0.start(n)
                v.wait_ge(x_loaded[quarter], 16 * uses(n, quarter, 4))
                emit_stats(nc, v, sc0, x_in[quarter], st[s], mv[s], divider)
                sc0.end()

            def norm(n, quarter):
                s = quarter % 2
                ch.start(n)
                v.wait_ge(rstd_chain, (n + 1) * KR)
                v.wait_ge(t_done, n + 1)
                emit_apply(nc, ch, x_in[quarter], xn[s], mv[s], rstd[s])
                if rms:
                    ch.wait(v)
                    for t in range(GT):
                        ins = nc.vector.tensor_scalar(xr[s][:, t, :], xn[s][:, t, :], rr[s][:, t:t + 1], None, ALU.mult)
                        ch.inc(ins)
                ch.end()

            def split(n, quarter):
                s = quarter % 2
                sc.start(n)
                v.wait_ge(high_ready, 2 * n + 2)
                v.wait_ge(parts_stored[s], NSTORE * uses(n, s))
                for a in range(2):
                    sc.inc(nc.vector.tensor_tensor(rest[s][a][:, :], ps_q[s][a][:, :], parts[s][a][:, 0, :],
                                                   ALU.subtract))
                sc.wait(v)
                for a in range(2):
                    sc.inc(nc.vector.tensor_copy(parts[s][a][:, 1, :], rest[s][a][:, :]))
                sc.wait(v)
                nc.vector.tensor_tensor(parts[s][0][:, 2, :], rest[s][0][:, :], parts[s][0][:, 1, :], ALU.subtract)
                sc.inc(nc.vector.tensor_tensor(parts[s][1][:, 2, :], rest[s][1][:, :], parts[s][1][:, 1, :],
                                               ALU.subtract))
                sc.end()

            skewed(v.Fori, NG, [(split, 4), (norm, 2), (stats, 1)], by=4)

        @block.scalar
        def _(a_):
            a_.wait_ge(w_ready, n_consts)

            a_.sem_inc(xnT_ready, 2)
            a_.sem_inc(v_copied, 2)

            def copies(n, quarter):
                s = quarter % 2
                a_.wait_ge(t_done, n + 3)
                a_.wait_ge(v_done, n + 1)
                if rms:
                    nc.scalar.activation(xnT[s][:, :], ps_t[s][:, :], ACT.Copy, scale=nscale[:, 0:1])\
                        .then_inc(xnT_ready, 1)
                else:
                    nc.scalar.activation(xnT[s][:, :], ps_t[s][:, :], ACT.Copy).then_inc(xnT_ready, 1)
                a_.wait_ge(parts_stored[s], NSTORE * uses(n, s))
                for a in range(2):
                    a_.wait_ge(qk_done, 2 * n + a + 1)
                    nc.scalar.activation(parts[s][a][:, 0, :], ps_q[s][a][:, :], ACT.Copy).then_inc(high_ready, 1)
                a_.wait_ge(v_done, n + 3)
                a_.wait_ge(v_stored[s], 16 * uses(n, s))
                nc.scalar.activation(v_out[s][:, :, :], ps_v[s][:, :].rearrange("p (t c) -> p t c", t=GT),
                                     ACT.Copy).then_inc(v_copied, 1)
                a_.wait_ge(v_copied, n + 3)
                a_.dma_start(rows_of(vd, n), v_out[s][:, :, :]).then_inc(v_stored[s], 16)

            skewed(a_.Fori, NG, [(copies, 3)], by=4)
            for s in range(2):
                a_.wait_ge(v_stored[s], 16 * (NG // 2 + 1))

        @block.tensor
        def _(t_):
            t_.sem_inc(t_done, 2)
            t_.sem_inc(v_done, 2)
            for s in range(2):
                t_.sem_inc(v_stored[s], 16)
                t_.sem_inc(parts_stored[s], NSTORE)
            t_.wait_ge(setup, 2)
            t_.wait_ge(w_scaled, 1)

            def transposes(n, quarter):
                s = quarter % 2
                t_.wait_ge(norm_chain, (n + 5) * KN)
                t_.wait_ge(xnT_ready, n + 1)
                for t in range(GT):
                    last = nc.tensor.transpose(ps_t[s][:, t * P:(t + 1) * P], xr[s][:, t, :], ident[:, :])
                last.then_inc(t_done, 1)

            def products(n, quarter):
                s = quarter % 2
                t_.wait_ge(xnT_ready, n + 3)
                t_.wait_ge(parts_stored[s], NSTORE * uses(n, s))
                for a in range(2):
                    nc.tensor.matmul(ps_q[s][a][:, :], w[:, a * D:(a + 1) * D], xnT[s][:, :], start=True, stop=True)\
                        .then_inc(qk_done, 1)
                t_.wait_ge(v_copied, n + 1)
                for t in range(GT):
                    last = nc.tensor.matmul(ps_v[s][:, t * D:(t + 1) * D], xnT[s][:, t * P:(t + 1) * P],
                                            w[:, 2 * D:3 * D], start=True, stop=True)
                last.then_inc(v_done, 1)

            skewed(t_.Fori, NG, [(products, 3), (transposes, 2)], by=4)


class Attention:

    def __init__(self, causal):
        self.causal = causal
        self.tiles = []
        for qb in range(TB):
            if not causal:
                k0 = max(0, qb - WB + 1)
                self.tiles += [(h, qb, k0 * P, (qb + 1 - k0) * P, True) for h in range(HG)]
            elif qb < 4:
                self.tiles += [(h, qb, 0, (qb + 1) * P, True) for h in range(HG)]
            else:
                self.tiles += [(h, qb, 0, 4 * P, False) for h in range(HG)]
                self.tiles += [(h, qb, 4 * P, (qb - 3) * P, True) for h in range(HG)]
        self.slots = []
        if causal:
            for half in range(2):
                for kb in range(4 * half + 4):
                    q0 = max(512 * half, P * kb)
                    for pair in range(2):
                        self.slots.append((kb, pair, q0, 512 * (half + 1) - q0))
        else:
            for kb in range(TB):
                q0 = kb * P
                for pair in range(2):
                    self.slots.append((kb, pair, q0, min(WB * P, S - q0)))
        self.masked = [k for k, (kb, _, q0, _) in enumerate(self.slots) if causal and q0 == kb * P]
        self.bank_end = [max(k for k, sl in enumerate(self.slots) if self.banks(sl)[b]) for b in range(2)]
        self.bank_start = [min(k for k, sl in enumerate(self.slots) if self.banks(sl)[b]) for b in range(2)]
        self.n_tiles, self.n_slots = len(self.tiles), len(self.slots)
        assert self.n_tiles % 2 == 0 and self.n_slots % 4 == 0
        self.last = self.n_slots - (10 if causal else 4)
        self.turn = self.last + (3 if causal else 1)
        starts = [sum(sl[3] for sl in self.slots[:k]) for k in range(self.n_slots + 1)]
        first, whole = starts[self.turn], starts[-1]
        room = whole - (first - starts[self.last + 1])
        total = sum(t[3] for t in self.tiles)
        self.late, self.early = [[[] for _ in self.slots] for _ in range(2)]
        done = 0
        for j, t in enumerate(self.tiles):
            at = first + room * done / total
            which, at = (self.late, at) if at < whole else (self.early, at - whole)
            which[max(k for k in range(self.n_slots) if starts[k] <= at)].append(j)
            done += t[3]

    @staticmethod
    def banks(slot):
        _, _, q0, n = slot
        out = []
        for b in range(2):
            lo, hi = max(q0, 512 * b), min(q0 + n, 512 * (b + 1))
            out.append((lo, hi) if lo < hi else None)
        return out


TABLE_PARTS = tuple((src, half) for src in range(2) for half in range(2))


def attention_phase(nc, sem, name, qd, kd, vd, att_dram, causal, bias_k=None, bias_q=None):
    plan = Attention(causal)
    pv_lag, p_bufs = (5, 8) if causal else (3, 4)
    NTL, NSL = plan.n_tiles, plan.n_slots
    TILES = NTL + 2
    NMASK = len(plan.masked)
    NGR = B * NHG
    ML = 4
    with Phase(nc, name) as ph:
        Q = [ph.sb(f"Q{g}", [P, HG, S], BF16) for g in range(NHG)]
        K = [ph.sb(f"K{g}", [P, HG, S], BF16) for g in range(NHG)]
        v_in = ph.sb("v", [P, TB, D])
        V = [ph.sb(f"V{s}", [P, TB, HG, 32]) for s in range(2)]
        probs = [ph.sb(f"probs{s}", [P, 2, 512]) for s in range(p_bufs)]
        O = [ph.sb(f"O{b}", [P, 512]) for b in range(2)]
        att = ph.sb("att", [P, TB, D])
        rec = [ph.sb(f"rec{b}", [P, GT, HG, 1]) for b in range(2)]
        part_max = ph.sb("part_max", [P, HG])
        mx = ph.sb("mx", [P, HG, TB])
        mrest = ph.sb("mrest", [P, HG * TB])
        mparts = ph.sb("mparts", [P, 3, HG * TB], BF16)
        mT = ph.sb("mT", [3 * HG * TB, P], BF16)
        ident = ph.sb("ident", [P, P])
        identb = ph.sb("identb", [P, P], BF16)
        if causal:
            mask = ph.sb("mask", [P, 512])
        else:
            tab_k = ph.sb("tab_k", [P, H, WB * P])
            tab_q = ph.sb("tab_q", [P, H, WB * P])
            raw = [ph.sb(f"raw{s}", [P, H // 2, WB * P]) for s in range(2)]
            raw_loaded = [sem(f"raw_loaded{s}") for s in range(2)]
        ps1 = [ph.ps(f"ps1{s}") for s in range(2)]
        ps2 = [ph.ps(f"ps2{s}", [P, 2, 512]) for s in range(2)]
        psO = [ph.ps(f"psO{b}") for b in range(2)]
        psT = ps1[0][:, 0:P // 2].bitcast(BF16)

        setup, divider = sem("setup"), sem("divider")
        pads = [sem(f"pads{g}") for g in range(NHG)]
        identb_ready = sem("identb_ready")
        tabs = sem("tabs")
        qk_loaded = [sem(f"qk_loaded{g}") for g in range(NHG)]
        v_loaded = sem("v_loaded")
        v_spread = sem("v_spread")
        t1_done = sem("t1_done")
        t1_read = sem("t1_read")
        m_chain = sem("m_chain")
        m_sent = [sem(f"m_sent{g}") for g in range(NHG)]
        s2_done = sem("s2_done")
        s2_read = sem("s2_read")
        exp_done = sem("exp_done")
        masked = sem("masked")
        pv_done = sem("pv_done")
        o_copied = sem("o_copied")
        oT_done = sem("oT_done")
        o_chain = sem("o_chain")
        att_stored = sem("att_stored")
        NSET = 4
        block = ph.block()

        def pad(eng, g):
            fills = [(t[g][part, :, :], 0.0) for part in (slice(32, 64), slice(64, 96)) for t in (Q, K)]
            for i, (dst, value) in enumerate(fills + [(K[g][PAD_ROWS:P, :, :], 1.0)]):
                eng.memset(dst, value).then_inc(pads[g], 1)
                eng.wait_ge(pads[g], i + 1)

        @block.sync
        def _(sp):
            sp.sem_inc(att_stored, 16)
            sp.wait_ge(setup, NSET)
            if not causal:
                for i, (src, half) in enumerate(TABLE_PARTS):
                    if i >= 2:
                        sp.wait_ge(tabs, i - 1)
                    sp.dma_start(raw[half][:, :, :], shifted_rows((bias_k, bias_q)[src], half * H // 2, H // 2))\
                        .then_inc(raw_loaded[half], 16)

            def load(n, b, g):
                sp.wait_ge(pv_done, NSL * (n + 1))
                sp.wait_ge(pads[g], 5)
                for dst, src, runs in ((Q[g], qd, Q_RUNS), (K[g], kd, K_RUNS)):
                    row = 0
                    for first, last in runs:
                        rows = (last + 1 - first) * HD
                        sp.dma_start(dst[row:row + rows, :, :],
                                     src[g * HG:(g + 1) * HG, first * HD:(last + 1) * HD, bass.ds(b * S, S)]
                                     .rearrange("h r t -> r h t")).then_inc(qk_loaded[g], 16)
                        row += rows

            def load_v(b):
                sp.wait_ge(v_spread, NHG * (b + 1))
                sp.dma_start(v_in[:, :, :], vd[bass.ds(b * S, S), :].rearrange("(t p) c -> p t c", p=P))\
                    .then_inc(v_loaded, 16)

            def store(b):
                sp.wait_ge(o_chain, 4 * (NHG * b + NHG) + 4)
                sp.dma_start(att_dram[bass.ds(b * S, S), :].rearrange("(t p) c -> p t c", p=P), att[:, :, :])\
                    .then_inc(att_stored, 16)

            def body(b, first=False, last=False):
                for g in range(NHG):
                    n = NHG * b + g
                    sp.wait_ge(t1_read, (n + 1) * TILES + 2)
                    for part in range(3):
                        sp.dma_start(Q[g][PAD_ROWS + part:PAD_ROWS + part + 1, :, :].rearrange("r h t -> r (h t)"),
                                     mT[part * HG * TB:(part + 1) * HG * TB, :]).then_inc(m_sent[g], 16)
                    if g == NHG - 1 and not last:
                        load_v(b + 1)
                    if not (last and g >= 1):
                        load(n + 3, b + (g + 3) // NHG, (g + 3) % NHG)
                    if g == 0 and not first:
                        store(b - 1)

            load(0, 0, 0)
            load_v(0)
            load(1, 0, 1)
            load(2, 0, 2)
            body(0, first=True)
            with sp.Fori(1, B - 1) as b:
                body(b)
            body(B - 1, last=True)
            store(B - 1)
            sp.wait_ge(att_stored, 16 * (B + 1))

        @block.gpsimd
        def _(g_):
            g_.sem_inc(v_spread, NHG)
            emit_identity(nc, g_, ident, setup)
            g_.memset(V[0][:, :, :, :], 0.0)
            g_.memset(V[1][:, :, :, :], 0.0).then_inc(setup, 1)
            g_.wait_ge(setup, 3)
            g_.memset(V[0][:, :, :, HD:HD + 1], 1.0)
            g_.memset(V[1][:, :, :, HD:HD + 1], 1.0).then_inc(setup, 1)
            if causal:
                g_.memset(mask[:, :], 0.0).then_inc(tabs, 1)
                g_.wait_ge(tabs, 1)
                g_.affine_select(out=mask[:, 512 - P:512], in_=mask[:, 512 - P:512], compare_op=ALU.is_ge,
                                 fill=MASKED, base=0, pattern=[[-1, P]], channel_multiplier=1).then_inc(tabs, 1)
            g_.wait_ge(setup, NSET)
            if causal:
                g_.wait_ge(tabs, 2)
            for g in range(1, NHG):
                pad(nc.gpsimd, g)
            with g_.Fori(0, B) as b:
                g_.wait_ge(v_loaded, 16 * (b + 1))
                for g in range(NHG):
                    n = NHG * b + g
                    wait_apart(g_, divider, (pv_done, NSL * (n + 3)))
                    nc.gpsimd.tensor_copy(V[g % 2][:, :, :, 0:HD],
                                          v_in[:, :, g * HG * HD:(g + 1) * HG * HD]
                                          .rearrange("p t (h d) -> p t h d", d=HD)).then_inc(v_spread, 1)
                    for k in plan.masked:
                        wait_apart(g_, divider, (exp_done, n * NSL + k + 3))
                        pt = probs[k % p_bufs]
                        nc.gpsimd.affine_select(out=pt[:, :, 0:P], in_=pt[:, :, 0:P], compare_op=ALU.is_ge,
                                                fill=0.0, base=0, pattern=[[0, 2], [1, P]],
                                                channel_multiplier=-1).then_inc(masked, 1)

        @block.scalar
        def _(a_):
            a_.sem_inc(exp_done, 2)
            if not causal:
                for i, (src, half) in enumerate(TABLE_PARTS):
                    a_.wait_ge(raw_loaded[half], 16 * (i // 2 + 1))
                    nc.scalar.activation((tab_k, tab_q)[src][:, half * H // 2:(half + 1) * H // 2, :],
                                         backwards(raw[half], H // 2), ACT.Copy).then_inc(tabs, 1)

            def copy_o(n, bank):
                a_.wait_ge(pv_done, NSL * (n + 4) + plan.bank_end[bank] + 1)
                a_.wait_ge(oT_done, 2 * n + bank + 1)
                nc.scalar.activation(O[bank][:, :], psO[bank][:, :], ACT.Copy).then_inc(o_copied, 1)

            def group(n, first=False):
                for k, (kb, pair, q0, w) in enumerate(plan.slots):
                    if causal:
                        a_.wait_ge(s2_done, n * NSL + k + 1)
                    else:
                        a_.wait_ge(s2_read, n * NSL + k + 3)
                    a_.wait_ge(pv_done, NSL * (n + 4) + k - p_bufs + 1)
                    pt = probs[k % p_bufs]
                    src = ps2[k % 2] if causal else pt
                    nc.scalar.activation(pt[:, :, 0:w], src[:, :, 0:w], ACT.Exp).then_inc(exp_done, 1)
                    if k == pv_lag and not first:
                        copy_o(n - 1, 1)
                    if k == plan.bank_end[0] + pv_lag:
                        copy_o(n, 0)

            group(0, first=True)
            with a_.Fori(0, B - 1) as b:
                for g in range(1, NHG + 1):
                    group(NHG * b + g)
            for g in range(1, NHG):
                group(NHG * (B - 1) + g)
            copy_o(NGR - 1, 1)

        @block.vector
        def _(v):
            v.sem_inc(t1_read, 2)
            v.sem_inc(s2_read, 2)
            v.sem_inc(o_chain, 4)
            pad(nc.vector, 0)
            v.wait_ge(setup, NSET)
            nc.vector.tensor_copy(identb[:, :], ident[:, :]).then_inc(identb_ready, 1)
            v.wait_ge(tabs, 2 if causal else len(TABLE_PARTS))
            mc = Count(m_chain, ML)

            def tile(n, g, j):
                h, qb, k0, w, with_mask = plan.tiles[j]
                wait_apart(v, divider, (t1_done, n * TILES + j + 1))
                src = ps1[j % 2]
                if not with_mask:
                    nc.vector.tensor_reduce(part_max[:, h:h + 1], src[:, 0:w], AX.X, ALU.max).then_inc(t1_read, 1)
                    return
                start = part_max[:, h:h + 1] if causal and k0 else 3 * MASKED
                table = mask[:, 512 - w:512] if causal else tab_q[:, g * HG + h, WB * P - w:WB * P]
                nc.vector.tensor_tensor_reduce(out=src[:, 0:w], in0=src[:, 0:w], in1=table, scale=1.0, scalar=start,
                                               op0=ALU.add, op1=ALU.max, accum_out=mx[:, h, qb:qb + 1])\
                    .then_inc(t1_read, 1)

            def maxima(n):
                mc.start(n)
                v.wait_ge(t1_read, n * TILES + NTL + 2)
                m2 = mx[:, :, :].rearrange("p h t -> p (h t)")
                mc.inc(nc.vector.tensor_scalar(mparts[:, 0, :], m2, -1.0, None, ALU.mult))
                mc.wait(v)
                mc.inc(nc.vector.scalar_tensor_tensor(out=mrest[:, :], in0=m2, scalar=-1.0, in1=mparts[:, 0, :],
                                                      op0=ALU.mult, op1=ALU.subtract))
                mc.wait(v)
                mc.inc(nc.vector.tensor_copy(mparts[:, 1, :], mrest[:, :]))
                mc.wait(v)
                mc.inc(nc.vector.tensor_tensor(mparts[:, 2, :], mrest[:, :], mparts[:, 1, :], ALU.subtract))
                mc.end()

            def copy_maxima(n, b, g):
                v.wait_ge(t1_done, n * TILES + NTL + 2)
                if g > 0:
                    v.wait_ge(m_sent[g - 1], 48 * (b + 1))
                elif not (isinstance(b, int) and b == 0):
                    v.wait_ge(m_sent[NHG - 1], 48 * b)
                nc.vector.tensor_copy(mT[:, :], psT[0:3 * HG * TB, :]).then_inc(t1_read, 2)

            def add_bias(n, g, k):
                kb, pair, q0, w = plan.slots[k]
                v.wait_ge(s2_done, n * NSL + k + 1)
                v.wait_ge(pv_done, NSL * (n + 4) + k - p_bufs + 1)
                h = g * HG + 2 * pair
                nc.vector.tensor_tensor(probs[k % p_bufs][:, :, 0:w], ps2[k % 2][:, :, 0:w], tab_k[:, h:h + 2, 0:w],
                                        ALU.add).then_inc(s2_read, 1)

            def norm(n, b, g, bank):
                v.wait_ge(oT_done, 2 * n + bank + 3)
                if g == 0 and bank == 0:
                    v.wait_ge(att_stored, 16 * (b + 1))
                src = psO[bank][:, :].rearrange("p (t h e) -> p t h e", t=GT, h=HG)
                nc.vector.reciprocal(rec[bank][:, :, :, :], src[:, :, :, HD:HD + 1]).then_inc(o_chain, 1)
                v.wait_ge(o_chain, 4 * (n + 1) + 2 * bank + 1)
                nc.vector.tensor_tensor(att[:, GT * bank:GT * (bank + 1), g * HG * HD:(g + 1) * HG * HD]
                                        .rearrange("p t (h d) -> p t h d", d=HD),
                                        src[:, :, :, 0:HD], rec[bank][:, :, :, :].to_broadcast([P, GT, HG, HD]),
                                        ALU.mult).then_inc(o_chain, 1)

            def group(this, nxt, later, prev):
                for k in range(NSL):
                    if not causal:
                        add_bias(this[0], this[2], k)
                    if nxt and k == plan.turn:
                        copy_maxima(*nxt)
                    for whose, tiles in ((nxt, plan.early[k]), (later, plan.late[k])):
                        for j in tiles if whose else ():
                            tile(whose[0], whose[2], j)
                    if nxt and k == plan.last:
                        maxima(nxt[0])
                    if prev and k == pv_lag + 2:
                        norm(*prev, 1)
                    if k == plan.bank_end[0] + pv_lag + 3:
                        norm(*this, 0)

            def before():
                for j in range(NTL):
                    tile(0, 0, j)
                maxima(0)
                copy_maxima(0, 0, 0)
                for j in range(sum(map(len, plan.late))):
                    tile(1, 1, j)

            walk(plan, B, group, before, after=lambda: norm(NGR - 1, B - 1, NHG - 1, 1), fori=v.Fori)

        @block.tensor
        def _(t_):
            t_.sem_inc(pv_done, 4 * NSL)
            t_.sem_inc(oT_done, 2)
            t_.wait_ge(setup, NSET)
            t_.wait_ge(identb_ready, 1)

            def tile(n, b, g, j):
                h, qb, k0, w, _ = plan.tiles[j]
                if j == 0:
                    t_.wait_ge(qk_loaded[g], 16 * (len(Q_RUNS) + len(K_RUNS)) * (b + 1))
                t_.wait_ge(t1_read, n * TILES + j + 1)
                nc.tensor.matmul(ps1[j % 2][:, 0:w], Q[g][0:PAD_ROWS, h, qb * P:(qb + 1) * P],
                                 K[g][0:PAD_ROWS, h, k0:k0 + w], start=True, stop=True).then_inc(t1_done, 1)

            def turn_maxima(n):
                t_.wait_ge(m_chain, ML * (n + 1))
                t_.wait_ge(t1_read, n * TILES + NTL + 1)
                nc.tensor.transpose(psT[0:3 * HG * TB, :], mparts[:, :, :].rearrange("p a b -> p (a b)"),
                                    identb[:, :]).then_inc(t1_done, 2)

            def score(n, b, g, k, hh):
                kb, pair, q0, w = plan.slots[k]
                if k == 0 and hh == 0:
                    t_.wait_ge(m_sent[g], 48 * (b + 1))
                if hh == 0:
                    t_.wait_ge(exp_done if causal else s2_read, n * NSL + k + 1)
                h = 2 * pair + hh
                last = nc.tensor.matmul(ps2[k % 2][:, hh, 0:w], K[g][0:ALL_ROWS, h, kb * P:(kb + 1) * P],
                                        Q[g][0:ALL_ROWS, h, q0:q0 + w], start=True, stop=True)
                if hh == 1:
                    last.then_inc(s2_done, 1)

            def values(n, g, k):
                kb, _, q0, w = plan.slots[k]
                if k in plan.masked:
                    t_.wait_ge(masked, n * NMASK + plan.masked.index(k) + 2)
                else:
                    t_.wait_ge(exp_done, n * NSL + k + 4)
                if k == 0:
                    t_.wait_ge(v_spread, n + NHG + 1)
                for bank in range(2):
                    if k == plan.bank_start[bank]:
                        t_.wait_ge(o_chain, 4 * n + 2 * (bank + 1))
                for bank, part in enumerate(plan.banks(plan.slots[k])):
                    if part is None:
                        continue
                    for h in range(HG):
                        last = nc.tensor.matmul(psO[bank][32 * h:32 * h + 32, part[0] - 512 * bank:part[1] - 512 * bank],
                                                V[g % 2][:, kb, h, :],
                                                probs[(k + h // 2) % p_bufs][:, h % 2, part[0] - q0:part[1] - q0],
                                                start=(k == plan.bank_start[bank]),
                                                stop=(k == plan.bank_end[bank] - 1), skip_group_check=True)
                last.then_inc(pv_done, 2)

            def turn_outputs(n, bank):
                t_.wait_ge(o_copied, 2 * n + bank + 1)
                for t in range(GT):
                    last = nc.tensor.transpose(psO[bank][:, t * P:(t + 1) * P], O[bank][:, t * P:(t + 1) * P],
                                               ident[:, :])
                last.then_inc(oT_done, 1)

            def group(this, nxt, later, prev):
                n, b, g = this
                for k in range(NSL):
                    tiles = [(nxt, j) for j in plan.early[k]] if nxt else []
                    tiles += [(later, j) for j in plan.late[k]] if later else []
                    parts = 3 if k % 2 else 2
                    if causal and nxt and k == plan.turn:
                        turn_maxima(nxt[0])
                    for i in range(parts):
                        if i < 2:
                            score(n, b, g, k, i)
                        elif k >= pv_lag:
                            values(n, g, k - pv_lag)
                        elif prev:
                            values(prev[0], prev[2], NSL + k - pv_lag)
                        if not causal and nxt and k == plan.turn and i == 1:
                            turn_maxima(nxt[0])
                        if causal:
                            first, end = i * len(tiles) // parts, (i + 1) * len(tiles) // parts
                        else:
                            first, end = (0, len(tiles)) if i == parts - 1 else (0, 0)
                        for whose, j in tiles[first:end]:
                            tile(*whose, j)
                    if prev and k == pv_lag + 1:
                        turn_outputs(prev[0], 1)
                    if k == plan.bank_end[0] + pv_lag + 2:
                        turn_outputs(n, 0)

            def before():
                for j in range(NTL):
                    tile(0, 0, 0, j)
                turn_maxima(0)
                for j in range(sum(map(len, plan.late))):
                    tile(1, 0, 1, j)

            def finish():
                for k in range(NSL + 1 - pv_lag, NSL, 2):
                    values(NGR - 1, NHG - 1, k)
                turn_outputs(NGR - 1, 1)

            walk(plan, B, group, before, after=finish, fori=t_.Fori)


def walk(plan, n_seq, group, before, after, fori):
    def at(b, g):
        if g < 0:
            return (NHG * b + g, b - 1, NHG + g)
        return (NHG * b + g, b + g // NHG, g % NHG)

    def step(b, g, end=None, first=False):
        nxt, later = [at(b, g + i) if end is None or g + i < end else None for i in (1, 2)]
        group(at(b, g), nxt, later, None if first else at(b, g - 1))

    before()
    step(0, 0, first=True)
    with fori(0, n_seq - 1) as b:
        for g in range(1, NHG + 1):
            step(b, g)
    for g in range(1, NHG):
        step(n_seq - 1, g, end=NHG)
    after()


def mix_phase(nc, sem, x_dram, att_dram, w_out, gate_w, x1_all, xn_dram, sorted_dram, onehot_all, weight_all):
    with Phase(nc, "mix") as ph:
        def two(name, shape, dt=F32):
            return [ph.sb(f"{name}{s}", shape, dt) for s in range(2)]
        x_in, a_in = [[ph.sb(f"{k}{s}", [P, GT, D]) for s in range(4)] for k in "xa"]
        aT, xn, xnT = two("aT", [P, GW]), two("xn", [P, GT, D]), two("xnT", [P, GW])
        st, mv, rstd = two("st", [P, GT, 6]), two("mv", [P, GT, 2]), two("rstd", [P, GT])
        top, diff, ex = two("top", [P, GT, 1]), two("diff", [P, GT, NE]), two("ex", [P, GT, NE])
        tot, pick, best = two("tot", [P, GT, 1]), two("pick", [P, GT, NE]), two("best", [P, GT, 1])
        wo, gw = ph.sb("wo", [P, D]), ph.sb("gw", [P, NE])
        ident, power = ph.sb("ident", [P, P]), ph.sb("power", [P, GT])
        order_i, order = ph.sb("order_i", [P, GT, NE], I32), ph.sb("order", [P, GT, NE])
        psA, psO, psT, psR = [[ph.ps(f"{k}{s}") for s in range(2)] for k in "AOTR"]
        zeros = ph.sb("zeros", [P, 8, D])
        zeroed, cleared = sem("zeroed"), sem("cleared")

        setup, weights = sem("setup"), sem("weights")
        divider = sem("divider")
        in_loaded = [sem(f"in_loaded{s}") for s in range(4)]
        aT_done, aT_copied, out_done = sem("aT_done"), sem("aT_copied"), sem("out_done")
        norm_chain, rstd_chain, apply_done = sem("norm_chain"), sem("rstd_chain"), sem("apply_done")
        xT_done, xT_copied, logits_done = sem("xT_done"), sem("xT_copied"), sem("logits_done")
        diff_chain, ex_done, pick_chain = sem("diff_chain"), sem("ex_done"), sem("pick_chain")
        stored = [sem(f"stored{s}") for s in range(2)]
        NST = 1 + STATS_STEPS
        NPICK = 5
        block = ph.block()

        @block.sync
        def _(sp):
            for s in range(2):
                sp.sem_inc(stored[s], 16)
            sp.dma_start(wo[:, :], w_out).then_inc(weights, 16)
            sp.dma_start(gw[:, :], gate_w).then_inc(weights, 16)

            def load(n, q):
                if not (isinstance(n, int) and n < 4):
                    sp.wait_ge(norm_chain, (n - 1) * NST)
                    sp.wait_ge(aT_done, n - 1)
                sp.dma_start(x_in[q][:, :, :], rows_of(x_dram, n)).then_inc(in_loaded[q], 16)
                sp.dma_start(a_in[q][:, :, :], rows_of(att_dram, n)).then_inc(in_loaded[q], 16)

            def store(n, q):
                s = q % 2
                sp.wait_ge(apply_done, n + 3)
                sp.dma_start(rows_of(xn_dram, n), xn[s][:, :, :]).then_inc(stored[s], 16)

            skewed(sp.Fori, NG, [(store, 4), (load, 0)], by=4)
            for s in range(2):
                sp.wait_ge(stored[s], 16 * (NG // 2 + 1))
            sp.wait_ge(cleared, 16 * (SORTED_TILES // 8))

        @block.gpsimd
        def _(g):
            emit_identity(nc, g, ident, setup)
            g.memset(zeros[:, :, :], 0.0).then_inc(zeroed, 1)
            g.memset(power[:, :], -0.5).then_inc(setup, 1)
            g.iota(order_i[:, :, :], pattern=[[0, GT], [-1, NE]], base=NE, channel_multiplier=0).then_inc(setup, 1)
            g.wait_ge(setup, 4)
            g.tensor_copy(order[:, :, :], order_i[:, :, :]).then_inc(setup, 1)
            rc = Count(rstd_chain, RSTD_STEPS)

            def rstds(n, q):
                s = q % 2
                wait_apart(g, divider, (norm_chain, (n + 3) * NST), (apply_done, n + 1))
                rc.start(n)
                emit_rstd(nc, g, rc, mv[s], rstd[s], power, divider)
                rc.end()

            skewed(g.Fori, NG, [(rstds, 2)], by=4)

        @block.scalar
        def _(a_):
            a_.wait_ge(zeroed, 1)
            for k in range(SORTED_TILES // 8):
                a_.dma_start(sorted_dram[k * 8 * P:(k + 1) * 8 * P, :].rearrange("(t p) c -> p t c", p=P),
                             zeros[:, :, :]).then_inc(cleared, 16)

            def copy_a(n, q):
                s = q % 2
                a_.wait_ge(aT_done, n + 3)
                a_.wait_ge(out_done, n + 1)
                nc.scalar.activation(aT[s][:, :], psA[s][:, :], ACT.Copy).then_inc(aT_copied, 1)

            def copy_x(n, q):
                s = q % 2
                a_.wait_ge(xT_done, n + 3)
                a_.wait_ge(logits_done, n + 1)
                nc.scalar.activation(xnT[s][:, :], psT[s][:, :], ACT.Copy).then_inc(xT_copied, 1)

            def exps(n, q):
                s = q % 2
                a_.wait_ge(diff_chain, 2 * (n + 1))
                a_.wait_ge(pick_chain, NPICK * (n + 1))
                nc.scalar.activation(ex[s][:, :, :], diff[s][:, :, :], ACT.Exp).then_inc(ex_done, 1)

            skewed(a_.Fori, NG, [(exps, 5), (copy_x, 4), (copy_a, 1)], by=4)

        @block.vector
        def _(v):
            v.sem_inc(norm_chain, 2 * NST)
            v.sem_inc(apply_done, 2)
            v.sem_inc(pick_chain, 2 * NPICK)
            ch = Count(norm_chain, NST, 2)
            dc = Count(diff_chain, 2)
            pc = Count(pick_chain, NPICK, 2)
            v.wait_ge(setup, 5)

            def residual(n, q):
                s = q % 2
                x1 = x1_all[:, bass.ds(n * GT, GT), :]
                ch.start(n)
                v.wait_ge(in_loaded[q], 32 * uses(n, q, 4))
                v.wait_ge(out_done, n + 3)
                ch.inc(nc.vector.tensor_tensor(x1, x_in[q][:, :, :],
                                               psO[s][:, :].rearrange("p (t c) -> p t c", t=GT), ALU.add))
                ch.wait_apart(v, divider)
                for t in range(GT):
                    ch.inc(nc.vector.bn_stats(st[s][:, t, :],
                                              x1_all[:, bass.ds(n * GT + t, 1), :].rearrange("p a c -> p (a c)")))
                ch.wait_apart(v, divider)
                for t in range(GT):
                    ch.inc(nc.vector.bn_aggr(mv[s][:, t, :], st[s][:, t, :]))
                ch.end()

            def normalise(n, q):
                s = q % 2
                v.wait_ge(rstd_chain, RSTD_STEPS * (n + 1))
                v.wait_ge(stored[s], 16 * uses(n, s))
                v.wait_ge(xT_done, n + 1)
                for t in range(GT):
                    last = nc.vector.tensor_scalar(xn[s][:, t, :],
                                                   x1_all[:, bass.ds(n * GT + t, 1), :].rearrange("p a c -> p (a c)"),
                                                   mv[s][:, t, 0:1],
                                                   rstd[s][:, t:t + 1], ALU.subtract, ALU.mult)
                last.then_inc(apply_done, 1)

            def logits(n, q):
                s = q % 2
                lg = psR[s][:, 0:GT * NE].rearrange("p (t e) -> p t e", t=GT)
                dc.start(n)
                v.wait_ge(logits_done, n + 3)
                dc.inc(nc.vector.tensor_reduce(top[s][:, :, 0], lg, AX.X, ALU.max))
                dc.wait(v)
                dc.inc(nc.vector.tensor_tensor(diff[s][:, :, :], lg, top[s][:, :, :].to_broadcast([P, GT, NE]),
                                               ALU.subtract))
                dc.end()

            def choose(n, q):
                s = q % 2
                pc.start(n)
                v.wait_ge(ex_done, n + 1)
                pc.inc(nc.vector.tensor_reduce(tot[s][:, :, 0], ex[s][:, :, :], AX.X, ALU.add))
                pc.inc(nc.vector.scalar_tensor_tensor(out=pick[s][:, :, :], in0=diff[s][:, :, :], scalar=0.0,
                                                      in1=order[:, :, :], op0=ALU.is_ge, op1=ALU.mult))
                pc.wait(v)
                pc.inc(nc.vector.reciprocal(weight_all[:, bass.ds(n * GT, GT)], tot[s][:, :, 0]))
                pc.inc(nc.vector.tensor_reduce(best[s][:, :, 0], pick[s][:, :, :], AX.X, ALU.max))
                pc.wait(v)
                pc.inc(nc.vector.tensor_tensor(onehot_all[:, bass.ds(n * GT, GT), :], pick[s][:, :, :],
                                               best[s][:, :, :].to_broadcast([P, GT, NE]), ALU.is_equal))
                pc.end()

            skewed(v.Fori, NG, [(choose, 6), (logits, 5), (normalise, 3), (residual, 2)], by=4)

        @block.tensor
        def _(t_):
            for q in (aT_done, out_done, xT_done, logits_done):
                t_.sem_inc(q, 2)
            t_.wait_ge(setup, 2)
            t_.wait_ge(weights, 32)

            def turn_a(n, q):
                s = q % 2
                t_.wait_ge(in_loaded[q], 32 * uses(n, q, 4))
                for t in range(GT):
                    last = nc.tensor.transpose(psA[s][:, t * P:(t + 1) * P], a_in[q][:, t, :], ident[:, :])
                last.then_inc(aT_done, 1)

            def out(n, q):
                s = q % 2
                t_.wait_ge(aT_copied, n + 1)
                t_.wait_ge(norm_chain, NST * (n + 1))
                for t in range(GT):
                    last = nc.tensor.matmul(psO[s][:, t * D:(t + 1) * D], aT[s][:, t * P:(t + 1) * P], wo[:, :],
                                            start=True, stop=True)
                last.then_inc(out_done, 1)

            def turn_x(n, q):
                s = q % 2
                t_.wait_ge(apply_done, n + 3)
                for t in range(GT):
                    last = nc.tensor.transpose(psT[s][:, t * P:(t + 1) * P], xn[s][:, t, :], ident[:, :])
                last.then_inc(xT_done, 1)

            def route(n, q):
                s = q % 2
                t_.wait_ge(xT_copied, n + 1)
                t_.wait_ge(pick_chain, NPICK * (n + 1))
                for t in range(GT):
                    last = nc.tensor.matmul(psR[s][:, t * NE:(t + 1) * NE], xnT[s][:, t * P:(t + 1) * P], gw[:, :],
                                            start=True, stop=True)
                last.then_inc(logits_done, 1)

            skewed(t_.Fori, NG, [(route, 5), (turn_x, 4), (out, 2), (turn_a, 1)], by=4)


SORTED_TILES = (T + NE * (P - 1)) // P + 1
SORTED_TILES += SORTED_TILES % 2


def place_phase(nc, sem, onehot_all, place_all, expert_row):
    with Phase(nc, "place") as ph:
        before = ph.sb("before", [P, P])
        ones = ph.sb("ones", [P, P])
        rank = ph.sb("rank", [P, NT, NE])
        total = ph.sb("total", [P, NE * NT])
        cum = ph.sb("cum", [P, NE * NT])
        excl = ph.sb("excl", [P, NE * NT])
        zeros = ph.sb("zeros", [P, NE * NT])
        marks_i, marks = ph.sb("marks_i", [P, NT], I32), ph.sb("marks", [P, NT])
        tiles_i, tiles = ph.sb("tiles_i", [P, SORTED_TILES], I32), ph.sb("tiles", [P, SORTED_TILES])
        count = ph.sb("count", [P, NE, 1])
        over = ph.sb("over", [P, NE, NT])
        blocks, end = ph.sb("blocks", [P, NE]), ph.sb("end", [P, NE])
        adj = ph.sb("adj", [P, NE, 1])
        past = ph.sb("past", [P, SORTED_TILES, NE])
        which = ph.sb("which", [P, SORTED_TILES])
        spot = ph.sb("spot", [P, NT])
        ps_rank, ps_total = ph.ps("ps_rank"), ph.ps("ps_total")
        setup, ready, counted, chain = sem("setup"), sem("ready"), sem("counted"), sem("chain")
        block = ph.block()

        @block.gpsimd
        def _(g):
            g.memset(before[:, :], 1.0).then_inc(setup, 1)
            g.memset(ones[:, :], 1.0)
            g.memset(zeros[:, :], 0.0)
            g.iota(marks_i[:, :], pattern=[[P, NT]], base=0, channel_multiplier=0)
            g.iota(tiles_i[:, :], pattern=[[1, SORTED_TILES]], base=0, channel_multiplier=0).then_inc(setup, 1)
            g.wait_ge(setup, 2)
            g.tensor_copy(marks[:, :], marks_i[:, :])
            g.tensor_copy(tiles[:, :], tiles_i[:, :])
            g.affine_select(out=before[:, :], in_=before[:, :], compare_op=ALU.is_gt, fill=0.0, base=0,
                            pattern=[[1, P]], channel_multiplier=-1).then_inc(ready, 1)

        @block.tensor
        def _(t_):
            t_.wait_ge(ready, 1)
            flat = onehot_all[:, :, :].rearrange("p t e -> p (t e)")
            nc.tensor.matmul(ps_rank[:, :], before[:, :], flat, start=True, stop=True).then_inc(counted, 1)
            nc.tensor.matmul(ps_total[:, :], ones[:, :], flat, start=True, stop=True).then_inc(counted, 1)

        @block.vector
        def _(v):
            c = Count(chain, 0)

            def link(ins):
                c.inc(ins)
                c.wait(v)

            v.wait_ge(counted, 2)
            v.wait_ge(ready, 1)
            link(nc.vector.tensor_copy(total[:, :].rearrange("p (e t) -> p e t", e=NE),
                                       ps_total[:, :].rearrange("p (t e) -> p e t", e=NE)))
            link(nc.vector.tensor_tensor_scan(cum[:, :], total[:, :], zeros[:, :], 0.0, ALU.add, ALU.add))
            link(nc.vector.tensor_tensor(excl[:, :], cum[:, :], total[:, :], ALU.subtract))
            cum3 = cum[:, :].rearrange("p (e t) -> p e t", e=NE)
            excl3 = excl[:, :].rearrange("p (e t) -> p e t", e=NE)
            link(nc.vector.tensor_tensor(count[:, :, :], cum3[:, :, NT - 1:NT], excl3[:, :, 0:1], ALU.subtract))
            link(nc.vector.tensor_tensor(over[:, :, :], count[:, :, :].to_broadcast([P, NE, NT]),
                                         marks[:, :].unsqueeze(1).to_broadcast([P, NE, NT]), ALU.is_gt))
            link(nc.vector.tensor_reduce(blocks[:, :], over[:, :, :], AX.X, ALU.add))
            link(nc.vector.tensor_tensor_scan(end[:, :], blocks[:, :], zeros[:, 0:NE], 0.0, ALU.add, ALU.add))
            link(nc.vector.tensor_tensor(adj[:, :, 0], end[:, :], blocks[:, :], ALU.subtract))
            link(nc.vector.scalar_tensor_tensor(out=adj[:, :, :], in0=adj[:, :, :], scalar=float(P),
                                                in1=excl3[:, :, 0:1], op0=ALU.mult, op1=ALU.subtract))
            link(nc.vector.tensor_tensor(excl3, excl3, adj[:, :, :].to_broadcast([P, NE, NT]), ALU.add))
            link(nc.vector.tensor_tensor(rank[:, :, :], ps_rank[:, :].rearrange("p (t e) -> p t e", e=NE),
                                         excl[:, :].rearrange("p (e t) -> p t e", e=NE), ALU.add))
            link(nc.vector.tensor_tensor(rank[:, :, :], rank[:, :, :], onehot_all[:, :, :], ALU.mult))
            link(nc.vector.tensor_reduce(spot[:, :], rank[:, :, :], AX.X, ALU.add))
            link(nc.vector.tensor_copy(place_all[:, :], spot[:, :]))
            link(nc.vector.tensor_tensor(past[:, :, :], tiles[:, :].unsqueeze(2).to_broadcast([P, SORTED_TILES, NE]),
                                         end[:, :].unsqueeze(1).to_broadcast([P, SORTED_TILES, NE]), ALU.is_ge))
            link(nc.vector.tensor_reduce(which[:, :], past[:, :, :], AX.X, ALU.add))
            link(nc.vector.tensor_scalar(which[:, :], which[:, :], float(NE - 1), None, ALU.min))
            link(nc.vector.tensor_copy(expert_row[:, :], which[:, :]))


def scatter_phase(nc, sem, xn_dram, sorted_dram, place_all, weight_loads, weights, beside):
    with Phase(nc, "scat") as ph:
        rows = [ph.sb(f"rows{s}", [P, GT, D]) for s in range(2)]
        loaded = [sem(f"loaded{s}") for s in range(2)]
        sent = [sem(f"sent{s}") for s in range(2)]
        block = ph.block()
        beside(block)

        @block.sync
        def _(sp):
            for n in range(NG):
                s = n % 2
                if n >= 2:
                    sp.wait_ge(sent[s], 16 * GT * (n // 2))
                sp.dma_start(rows[s][:, :, :], rows_of(xn_dram, n)).then_inc(loaded[s], 16)
                if n < len(weight_loads):
                    sp.dma_start(*weight_loads[n]).then_inc(weights, 16)
            sp.wait_ge(weights, 16 * len(weight_loads))

        @block.gpsimd
        def _(g):
            for n in range(NG):
                s = n % 2
                g.wait_ge(loaded[s], 16 * (n // 2 + 1))
                for t in range(GT):
                    g.indirect_dma_start(sorted_dram[:, :], bass.IndirectOffsetOnAxis(
                        ap=place_all[:, n * GT + t:n * GT + t + 1], axis=0), rows[s][:, t, :], None)\
                        .then_inc(sent[s], 16)
            for s in range(2):
                g.wait_ge(sent[s], 16 * GT * (NG // 2))


FC = FF // P


def expert_weights(keep, w1, b1, w2, b2):
    w1_sb, w2_sb = keep("w1", [P, NE, FF]), keep("w2", [P, NE, FC * D])
    b1_sb, b2_sb = keep("b1", [P, NE, FF]), keep("b2", [P, NE, D])
    return (w1_sb, b1_sb, w2_sb, b2_sb), [
        (w1_sb[:, :, :], w1.rearrange("e c f -> c e f")),
        (b1_sb[:, :, :], bass.AP(tensor=b1.tensor, offset=0, ap=[[0, P], [FF, NE], [1, FF]])),
        (w2_sb[:, :, :].rearrange("p e (m c) -> p e m c", m=FC), w2.rearrange("e (m p) c -> p e m c", p=P)),
        (b2_sb[:, :, :], bass.AP(tensor=b2.tensor, offset=0, ap=[[0, P], [D, NE], [1, D]]))]


def experts_phase(nc, sem, sorted_dram, y_dram, tables, expert_row):
    w1_sb, b1_sb, w2_sb, b2_sb = tables
    with Phase(nc, "moe") as ph:
        def two(name, shape, dt=F32):
            return [ph.sb(f"{name}{s}", shape, dt) for s in range(2)]
        ident = ph.sb("ident", [P, P])
        x = [ph.sb(f"x{s}", [P, D]) for s in range(4)]
        xT, hb, h = two("xT", [P, P]), two("hb", [P, FF]), two("h", [P, FF])
        hT, y = two("hT", [P, FF]), two("y", [P, D])
        psX, psH, psT, psY = [[ph.ps(f"{k}{s}") for s in range(2)] for k in "XHTY"]
        setup = sem("setup")
        loaded = [sem(f"loaded{s}") for s in range(4)]
        stored = [sem(f"stored{s}") for s in range(2)]
        xT_done, xT_copied, up_done, biased, gelu_done = [sem(k) for k in
                                                          ("xT_done", "xT_copied", "up_done", "biased", "gelu_done")]
        hT_done, hT_copied, down_done, y_done = [sem(k) for k in ("hT_done", "hT_copied", "down_done", "y_done")]
        block = ph.block()

        def expert(eng, n):
            return eng.value_load(expert_row[0:1, bass.ds(n, 1)], min_val=0, max_val=NE - 1)

        @block.sync
        def _(sp):
            for s in range(2):
                sp.sem_inc(stored[s], 16)

            def load(n, q):
                if not (isinstance(n, int) and n < 4):
                    sp.wait_ge(xT_done, n - 1)
                sp.dma_start(x[q][:, :], sorted_dram[bass.ds(n * P, P), :]).then_inc(loaded[q], 16)

            def store(n, q):
                s = q % 2
                sp.wait_ge(y_done, n + 3)
                sp.dma_start(y_dram[bass.ds(n * P, P), :], y[s][:, :]).then_inc(stored[s], 16)

            skewed(sp.Fori, SORTED_TILES, [(store, 11), (load, 0)], by=4)
            for s in range(2):
                sp.wait_ge(stored[s], 16 * (SORTED_TILES // 2 + 1))

        @block.gpsimd
        def _(g):
            emit_identity(nc, g, ident, setup)

        @block.scalar
        def _(a_):
            a_.sem_inc(gelu_done, 2)
            a_.sem_inc(xT_copied, 2)

            def copy_x(n, q):
                s = q % 2
                a_.wait_ge(xT_done, n + 3)
                a_.wait_ge(up_done, n + 1)
                nc.scalar.activation(xT[s][:, :], psX[s][:, 0:P], ACT.Copy).then_inc(xT_copied, 1)

            def gelu(n, q):
                s = q % 2
                a_.wait_ge(biased, n + 3)
                a_.wait_ge(hT_done, n + 1)
                nc.scalar.activation(h[s][:, :], hb[s][:, :], ACT.Gelu).then_inc(gelu_done, 1)

            skewed(a_.Fori, SORTED_TILES, [(gelu, 6), (copy_x, 3)], by=4)

        @block.vector
        def _(v):
            for q in (biased, hT_copied, y_done):
                v.sem_inc(q, 2)

            def bias_up(n, q):
                s = q % 2
                e = expert(v, n)
                v.wait_ge(up_done, n + 3)
                v.wait_ge(gelu_done, n + 1)
                nc.vector.tensor_tensor(hb[s][:, :].unsqueeze(1), psH[s][:, :].unsqueeze(1), b1_sb[:, bass.ds(e, 1), :],
                                        ALU.add).then_inc(biased, 1)

            def copy_h(n, q):
                s = q % 2
                v.wait_ge(hT_done, n + 3)
                v.wait_ge(down_done, n + 1)
                nc.vector.tensor_copy(hT[s][:, :], psT[s][:, :]).then_inc(hT_copied, 1)

            def bias_down(n, q):
                s = q % 2
                e = expert(v, n)
                v.wait_ge(down_done, n + 3)
                v.wait_ge(stored[s], 16 * uses(n, s))
                nc.vector.tensor_tensor(y[s][:, :].unsqueeze(1), psY[s][:, 0:D].unsqueeze(1), b2_sb[:, bass.ds(e, 1), :],
                                        ALU.add).then_inc(y_done, 1)

            skewed(v.Fori, SORTED_TILES, [(bias_down, 10), (copy_h, 8), (bias_up, 5)], by=4)

        @block.tensor
        def _(t_):
            for q in (xT_done, up_done, hT_done, down_done):
                t_.sem_inc(q, 2)
            t_.wait_ge(setup, 2)

            def turn_x(n, q):
                s = q % 2
                t_.wait_ge(loaded[q], 16 * uses(n, q, 4))
                t_.wait_ge(xT_copied, n + 1)
                nc.tensor.transpose(psX[s][:, 0:P], x[q][:, :], ident[:, :]).then_inc(xT_done, 1)

            def up(n, q):
                s = q % 2
                e = expert(t_, n)
                t_.wait_ge(xT_copied, n + 3)
                t_.wait_ge(biased, n + 1)
                nc.tensor.matmul(psH[s][:, :], xT[s][:, :], w1_sb[:, bass.ds(e, 1), :].rearrange("p a f -> p (a f)"),
                                 start=True, stop=True).then_inc(up_done, 1)

            def turn_h(n, q):
                s = q % 2
                t_.wait_ge(gelu_done, n + 3)
                t_.wait_ge(hT_copied, n + 1)
                for m in range(FC):
                    last = nc.tensor.transpose(psT[s][:, m * P:(m + 1) * P], h[s][:, m * P:(m + 1) * P], ident[:, :])
                last.then_inc(hT_done, 1)

            def down(n, q):
                s = q % 2
                e = expert(t_, n)
                t_.wait_ge(hT_copied, n + 3)
                t_.wait_ge(y_done, n + 1)
                for m in range(FC):
                    last = nc.tensor.matmul(psY[s][:, 0:D], hT[s][:, m * P:(m + 1) * P],
                                            w2_sb[:, bass.ds(e, 1), m * D:(m + 1) * D].rearrange("p a f -> p (a f)"),
                                            start=(m == 0), stop=(m == FC - 1))
                last.then_inc(down_done, 1)

            skewed(t_.Fori, SORTED_TILES, [(down, 9), (turn_h, 7), (up, 4), (turn_x, 2)], by=4)


def gather_phase(nc, sem, x1_all, y_dram, place_all, weight_all, x2_dram):
    with Phase(nc, "gath") as ph:
        y = [ph.sb(f"y{s}", [P, GT, D]) for s in range(2)]
        x2 = [ph.sb(f"o{s}", [P, GT, D]) for s in range(2)]
        gathered = [sem(f"gathered{s}") for s in range(2)]
        stored = [sem(f"stored{s}") for s in range(2)]
        summed = sem("summed")
        block = ph.block()

        @block.sync
        def _(sp):
            for s in range(2):
                sp.wait_ge(stored[s], 16 * (NG // 2))

        @block.gpsimd
        def _(g):
            for n in range(NG):
                s = n % 2
                if n >= 2:
                    g.wait_ge(summed, n - 1)
                for t in range(GT):
                    g.indirect_dma_start(y[s][:, t, :], None, y_dram[:, :], bass.IndirectOffsetOnAxis(
                        ap=place_all[:, n * GT + t:n * GT + t + 1], axis=0)).then_inc(gathered[s], 16)

        @block.vector
        def _(v):
            for n in range(NG):
                s = n % 2
                v.wait_ge(gathered[s], 16 * GT * (n // 2 + 1))
                if n >= 2:
                    v.wait_ge(stored[s], 16 * (n // 2))
                for t in range(GT):
                    last = nc.vector.scalar_tensor_tensor(
                        out=x2[s][:, t, :], in0=y[s][:, t, :], scalar=weight_all[:, n * GT + t:n * GT + t + 1],
                        in1=x1_all[:, n * GT + t, :], op0=ALU.mult, op1=ALU.add)
                last.then_inc(summed, 1)

        @block.scalar
        def _(a_):
            for n in range(NG):
                s = n % 2
                a_.wait_ge(summed, n + 1)
                a_.dma_start(rows_of(x2_dram, n), x2[s][:, :, :]).then_inc(stored[s], 16)


def bias_phase(nc, sem, block, offsets, pos_bias, fwd_dram, rev_dram):
    NCH = WINDOW // P
    with Phase(nc, "bias") as ph:
        off_i, off = ph.sb("off_i", [P, NOFF], I32), ph.sb("off", [P, NOFF])
        pb = ph.sb("pb", [P, NOFF, H])
        dist_i, dist = ph.sb("dist_i", [P, 2 * NCH], I32), ph.sb("dist", [P, 2 * NCH])
        off_mask = ph.sb("off_mask", [P, NOFF])
        val = ph.sb("val", [P, H, NOFF])
        top, tot = ph.sb("top", [P, H, 1]), ph.sb("tot", [P, H])
        res = ph.sb("res", [P, H])
        ident = ph.sb("ident", [P, P])
        rows = [ph.sb(f"rows{k}", [H, 2 * WINDOW]) for k in range(2)]
        psT = ph.ps("psT")
        setup, loaded, chain, shifted, exp_done, ln_done, turned, stored = [sem(k) for k in (
            "setup", "loaded", "chain", "shifted", "exp_done", "ln_done", "turned", "stored")]

        @block.gpsimd
        def _(g):
            emit_identity(nc, g, ident, setup)
            for k in range(NCH):
                g.iota(dist_i[:, k:k + 1], pattern=[[0, 1]], base=k * P, channel_multiplier=1)
                last = g.iota(dist_i[:, NCH + k:NCH + k + 1], pattern=[[0, 1]], base=WINDOW - 1 - k * P,
                              channel_multiplier=-1)
            last.then_inc(setup, 1)
            for k in range(2):
                last = g.memset(rows[k][:, :], MASKED)
            last.then_inc(setup, 1)

        @block.vector
        def _(v):
            c = Count(chain, 0)

            def link(ins):
                c.inc(ins)
                c.wait(v)

            v.wait_ge(setup, 4)
            v.wait_ge(loaded, 32)
            link(nc.vector.tensor_copy(dist[:, :], dist_i[:, :]))
            link(nc.vector.tensor_copy(off[:, :], off_i[:, :]))
            for k in range(2 * NCH):
                link(nc.vector.tensor_scalar(off_mask[:, :], off[:, :], dist[:, k:k + 1], MASKED, ALU.not_equal, ALU.mult))
                link(nc.vector.tensor_tensor(val[:, :, :], pb[:, :, :].rearrange("p o h -> p h o"),
                                             off_mask[:, :].unsqueeze(1).to_broadcast([P, H, NOFF]), ALU.add))
                link(nc.vector.tensor_reduce(top[:, :, 0], val[:, :, :], AX.X, ALU.max))
                nc.vector.tensor_tensor(val[:, :, :], val[:, :, :], top[:, :, :].to_broadcast([P, H, NOFF]),
                                        ALU.subtract).then_inc(shifted, 1)
                v.wait_ge(exp_done, k + 1)
                nc.vector.tensor_reduce(tot[:, :], val[:, :, :], AX.X, ALU.add).then_inc(shifted, 1)
                v.wait_ge(ln_done, k + 1)
                link(nc.vector.tensor_tensor(res[:, :], tot[:, :], top[:, :, 0], ALU.add))
                v.wait_ge(turned, k + 1)
                at = (P - 1 if k < NCH else P) + (k % NCH) * P
                link(nc.vector.tensor_copy(rows[k // NCH][:, at:at + P], psT[0:H, 0:P]))

        @block.scalar
        def _(a_):
            a_.dma_start(off_i[:, :], bass.AP(tensor=offsets.tensor, offset=0, ap=[[0, P], [1, NOFF]])).then_inc(loaded, 16)
            a_.dma_start(pb[:, :, :], bass.AP(tensor=pos_bias.tensor, offset=0, ap=[[0, P], [H, NOFF], [1, H]]))\
                .then_inc(loaded, 16)
            for k in range(2 * NCH):
                a_.wait_ge(shifted, 2 * k + 1)
                nc.scalar.activation(val[:, :, :], val[:, :, :], ACT.Exp).then_inc(exp_done, 1)
                a_.wait_ge(shifted, 2 * k + 2)
                nc.scalar.activation(tot[:, :], tot[:, :], ACT.Ln).then_inc(ln_done, 1)
            a_.wait_ge(chain, 2 + 5 * 2 * NCH)
            a_.dma_start(fwd_dram, rows[0][:, :]).then_inc(stored, 16)
            a_.dma_start(rev_dram, rows[1][:, :]).then_inc(stored, 16)
            a_.wait_ge(stored, 32)

        @block.tensor
        def _(t_):
            t_.wait_ge(setup, 2)
            for k in range(2 * NCH):
                t_.wait_ge(chain, 2 + 5 * k + 4)
                nc.tensor.transpose(psT[0:H, 0:P], res[:, :], ident[:, :]).then_inc(turned, 1)


def shifted_rows(bias_dram, h0, n_heads):
    return bass.AP(tensor=bias_dram.tensor, offset=bias_dram.offset + h0 * 2 * WINDOW,
                   ap=[[1, P], [2 * WINDOW, n_heads], [1, WB * P]])


def backwards(t, n_heads):
    whole = t[:, :, :]
    return bass.AP(tensor=whole.tensor, offset=whole.offset + WB * P - 1,
                   ap=[list(whole.ap[0]), [WB * P, n_heads], [-1, WB * P]])


def gated_phase(nc, sem, x_dram, att_dram, w_gate, b_gate, norm1, w_out, sum_all, xr_dram):
    with Phase(nc, "gate") as ph:
        def two(name, shape, dt=F32):
            return [ph.sb(f"{name}{s}", shape, dt) for s in range(2)]
        x_in = [ph.sb(f"x{s}", [P, GT, D]) for s in range(8)]
        a_in = [ph.sb(f"a{s}", [P, GT, D]) for s in range(8)]
        y = [ph.sb(f"y{s}", [P, GT, D]) for s in range(4)]
        xr, xT, gate, ag = two("xr", [P, GT, D]), two("xT", [P, GW]), two("gate", [P, GW]), two("ag", [P, GW])
        yy = two("yy", [P, GT, D])
        xr2, junk = two("xr2", [P, GT, D]), two("junk", [P, D])
        st, mv, rstd, rr = two("st", [P, GT, 6]), two("mv", [P, GT, 2]), two("rstd", [P, GT]), two("rr", [P, GT])
        sq, r2 = two("sq", [P, GT]), two("r2", [P, GT])
        wg, wo, bg, n1 = ph.sb("wg", [P, D]), ph.sb("wo", [P, D]), ph.sb("bg", [P, 1]), ph.sb("n1", [P, 1])
        ident, power = ph.sb("ident", [P, P]), ph.sb("power", [P, GT])
        psT, psG, psA, psO = [[ph.ps(f"{k}{s}") for s in range(2)] for k in "TGAO"]
        setup, weights = sem("setup"), sem("weights")
        divider = sem("divider")
        loaded = [sem(f"loaded{s}") for s in range(8)]
        stored = [sem(f"stored{s}") for s in range(2)]
        stats_chain, rstd_chain, y_chain = sem("stats_chain"), sem("rstd_chain"), sem("y_chain")
        turned, xT_copied, gate_done, sig_done = sem("turned"), sem("xT_copied"), sem("gate_done"), sem("sig_done")
        ag_done, out_done, sq_chain, r2_chain, xr2_done = [sem(k) for k in ("ag_done", "out_done", "sq_chain", "r2_chain", "xr2_done")]
        NY, NSQ = 2 * GT, 2 + GT
        block = ph.block()

        @block.sync
        def _(sp):
            for s in range(2):
                sp.sem_inc(stored[s], 16)
            for dst, src in ((wg[:, :], w_gate), (wo[:, :], w_out), (bg[:, :], b_gate.rearrange("(c a) -> c a", a=1)),
                             (n1[:, :], norm1.rearrange("(c a) -> c a", a=1))):
                sp.dma_start(dst, src).then_inc(weights, 16)

            def load(n, q):
                sp.wait_ge(sq_chain, NSQ * (n + 1))
                sp.dma_start(x_in[q][:, :, :], rows_of(x_dram, n)).then_inc(loaded[q], 16)
                sp.dma_start(a_in[q][:, :, :], rows_of(att_dram, n)).then_inc(loaded[q], 16)

            def store(n, q):
                s = q % 2
                sp.wait_ge(xr2_done, n + 3)
                sp.dma_start(rows_of(xr_dram, n), xr2[s][:, :, :]).then_inc(stored[s], 16)

            skewed(sp.Fori, NG, [(store, 6), (load, 0)], by=8)
            for s in range(2):
                sp.wait_ge(stored[s], 16 * (NG // 2 + 1))

        @block.gpsimd
        def _(g):
            g.sem_inc(r2_chain, 4)
            emit_identity(nc, g, ident, setup)
            g.memset(power[:, :], -0.5).then_inc(setup, 1)
            g.wait_ge(setup, 3)
            rc = Count(rstd_chain, RMS_STEPS)

            def rstds(n, q):
                s = q % 2
                wait_apart(g, divider, (stats_chain, (n + 1) * STATS_STEPS), (y_chain, (n + 1) * NY))
                rc.start(n)
                emit_rstd(nc, g, rc, mv[s], rstd[s], power, divider, rms=(RMS_EPS, rr[s]))
                rc.end()

            def second(n, q):
                s = q % 2
                wait_apart(g, divider, (sq_chain, (n + 9) * NSQ), (xr2_done, n + 1))
                g.tensor_scalar(r2[s][:, :], sq[s][:, :], 1.0 / D, RMS_EPS, ALU.mult, ALU.add).then_inc(r2_chain, 1)
                g.wait_ge(r2_chain, 2 * n + 5)
                g.tensor_tensor(r2[s][:, :], r2[s][:, :], power[:, :], ALU.pow).then_inc(r2_chain, 1)

            skewed(g.Fori, NG, [(second, 5), (rstds, 1)], by=8)

        @block.vector
        def _(v):
            v.sem_inc(y_chain, 2 * NY)
            v.sem_inc(sq_chain, 8 * NSQ)
            v.sem_inc(xr2_done, 2)
            v.sem_inc(ag_done, 2)
            c1 = Count(stats_chain, STATS_STEPS)
            c2 = Count(y_chain, NY, 2)
            c3 = Count(sq_chain, NSQ, 8)

            def stats(n, q):
                s = q % 2
                c1.start(n)
                v.wait_ge(loaded[q], 32 * uses(n, q, 8))
                emit_stats(nc, v, c1, x_in[q], st[s], mv[s], divider)
                c1.end()

            def norm(n, q):
                s = q % 2
                c2.start(n)
                v.wait_ge(rstd_chain, (n + 1) * RMS_STEPS)
                v.wait_ge(turned, n + 1)
                emit_apply(nc, c2, x_in[q], y[q % 4], mv[s], rstd[s])
                c2.wait(v)
                for t in range(GT):
                    c2.inc(nc.vector.tensor_scalar(xr[s][:, t, :], y[q % 4][:, t, :], rr[s][:, t:t + 1], None, ALU.mult))
                c2.end()

            def gating(n, q):
                s = q % 2
                v.wait_ge(sig_done, n + 1)
                v.wait_ge(out_done, n + 1)
                nc.vector.tensor_tensor(ag[s][:, :], psA[s][:, :], gate[s][:, :], ALU.mult).then_inc(ag_done, 1)

            def residual(n, q):
                s = q % 2
                c3.start(n)
                v.wait_ge(out_done, n + 3)
                c3.inc(nc.vector.tensor_tensor(yy[s][:, :, :], y[q % 4][:, :, :],
                                               psO[s][:, :].rearrange("p (t c) -> p t c", t=GT), ALU.add))
                c3.wait(v)
                c3.inc(nc.vector.tensor_tensor(sum_all[:, bass.ds(n * GT, GT), :], yy[s][:, :, :], x_in[q][:, :, :], ALU.add))
                for t in range(GT):
                    if t >= 2:
                        v.wait_ge(c3.sem, c3.base + c3.c - 1)
                    c3.inc(nc.vector.tensor_tensor_reduce(out=junk[t % 2][:, :], in0=yy[s][:, t, :], in1=yy[s][:, t, :],
                                                          scale=1.0, scalar=0.0, op0=ALU.mult, op1=ALU.add,
                                                          accum_out=sq[s][:, t:t + 1]))
                c3.end()

            def scale(n, q):
                s = q % 2
                v.wait_ge(r2_chain, 2 * n + 6)
                v.wait_ge(stored[s], 16 * uses(n, s))
                for t in range(GT):
                    last = nc.vector.tensor_scalar(xr2[s][:, t, :], yy[s][:, t, :], r2[s][:, t:t + 1], None, ALU.mult)
                last.then_inc(xr2_done, 1)

            skewed(v.Fori, NG, [(scale, 6), (residual, 5), (gating, 3), (norm, 2), (stats, 1)], by=8)

        @block.scalar
        def _(a_):
            a_.wait_ge(weights, 64)

            def copy(n, q):
                s = q % 2
                a_.wait_ge(turned, n + 3)
                a_.wait_ge(gate_done, n + 1)
                nc.scalar.activation(xT[s][:, :], psT[s][:, :], ACT.Copy, scale=n1[:, 0:1]).then_inc(xT_copied, 1)

            def sigmoid(n, q):
                s = q % 2
                a_.wait_ge(gate_done, n + 3)
                a_.wait_ge(ag_done, n + 1)
                nc.scalar.activation(gate[s][:, :], psG[s][:, :], ACT.Sigmoid, bias=bg[:, 0:1]).then_inc(sig_done, 1)

            skewed(a_.Fori, NG, [(sigmoid, 3), (copy, 2)], by=8)

        @block.tensor
        def _(t_):
            for q in (turned, gate_done, out_done):
                t_.sem_inc(q, 2)
            t_.wait_ge(setup, 2)
            t_.wait_ge(weights, 64)

            def turn(n, q):
                s = q % 2
                t_.wait_ge(ag_done, n + 1)
                t_.wait_ge(loaded[q], 32 * uses(n, q, 8))
                for t in range(GT):
                    nc.tensor.transpose(psA[s][:, t * P:(t + 1) * P], a_in[q][:, t, :], ident[:, :])
                t_.wait_ge(y_chain, (n + 3) * NY)
                for t in range(GT):
                    last = nc.tensor.transpose(psT[s][:, t * P:(t + 1) * P], xr[s][:, t, :], ident[:, :])
                last.then_inc(turned, 1)

            def gate_product(n, q):
                s = q % 2
                t_.wait_ge(xT_copied, n + 1)
                if not (isinstance(n, int) and n < 2):
                    t_.wait_ge(sig_done, n - 1)
                nc.tensor.matmul(psG[s][:, :], wg[:, :], xT[s][:, :], start=True, stop=True).then_inc(gate_done, 1)

            def out_product(n, q):
                s = q % 2
                t_.wait_ge(ag_done, n + 3)
                t_.wait_ge(sq_chain, NSQ * (n + 7))
                for t in range(GT):
                    last = nc.tensor.matmul(psO[s][:, t * D:(t + 1) * D], ag[s][:, t * P:(t + 1) * P], wo[:, :],
                                            start=True, stop=True)
                last.then_inc(out_done, 1)

            skewed(t_.Fori, NG, [(out_product, 4), (gate_product, 3), (turn, 2)], by=8)


def swiglu_phase(nc, sem, xr_dram, sum_all, norm2, w_gate, w_up, w_down, x_dram):
    NC = len(F_CHUNKS)
    with Phase(nc, "swi") as ph:
        def two(name, shape, dt=F32):
            return [ph.sb(f"{name}{s}", shape, dt) for s in range(2)]
        xr = two("xr", [P, GT, D])
        xT, x3 = two("xT", [P, GW]), two("x3", [P, GT, D])
        sg = two("sg", [P, GW])
        h = [[ph.sb(f"h{s}{c}", [P, GW]) for c in range(NC)] for s in range(2)]
        wg, wu, n2 = ph.sb("wg", [P, FFN1]), ph.sb("wu", [P, FFN1]), ph.sb("n2", [P, 1])
        wd = ph.sb("wd", [P, NC, D])
        ident = ph.sb("ident", [P, P])
        psT, psG, psU, psD = [[ph.ps(f"{k}{s}") for s in range(2)] for k in "TGUD"]
        setup, weights = sem("setup"), sem("weights")
        loaded = [sem(f"loaded{s}") for s in range(4)]
        stored = [sem(f"stored{s}") for s in range(2)]
        turned, xT_copied, up_done, silu_done, h_done, down_done, x3_done = [sem(k) for k in (
            "turned", "xT_copied", "up_done", "silu_done", "h_done", "down_done", "x3_done")]
        block = ph.block()

        @block.sync
        def _(sp):
            for s in range(2):
                sp.sem_inc(stored[s], 16)
            for dst, src in ((wg[:, :], w_gate), (wu[:, :], w_up), (n2[:, :], norm2.rearrange("(c a) -> c a", a=1))):
                sp.dma_start(dst, src).then_inc(weights, 16)
            for c, (f0, fw) in enumerate(F_CHUNKS):
                sp.dma_start(wd[0:fw, c, :], w_down[f0:f0 + fw, :]).then_inc(weights, 16)

            def load(n, q):
                sp.wait_ge(turned, n + 1)
                sp.dma_start(xr[q % 2][:, :, :], rows_of(xr_dram, n)).then_inc(loaded[q], 16)

            def store(n, q):
                sp.wait_ge(x3_done, n + 5)
                sp.dma_start(rows_of(x_dram, n), x3[q % 2][:, :, :]).then_inc(stored[q % 2], 16)

            skewed(sp.Fori, NG, [(store, 3), (load, 0)], by=4)
            for s in range(2):
                sp.wait_ge(stored[s], 16 * (NG // 2 + 1))

        @block.gpsimd
        def _(g):
            emit_identity(nc, g, ident, setup)

        @block.scalar
        def _(a_):
            a_.sem_inc(silu_done, 2)
            a_.sem_inc(xT_copied, 2)
            a_.wait_ge(weights, 96)

            def copy(n, q):
                a_.wait_ge(turned, n + 3)
                a_.wait_ge(up_done, NC * (n + 1))
                nc.scalar.activation(xT[q % 2][:, :], psT[q % 2][:, :], ACT.Copy, scale=n2[:, 0:1]).then_inc(xT_copied, 1)

            def silu(n, q):
                for c, (f0, fw) in enumerate(F_CHUNKS):
                    a_.wait_ge(up_done, NC * (n + 2) + c + 1)
                    a_.wait_ge(h_done, NC * n + c + 1)
                    k = (NC * q + c) % 2
                    nc.scalar.activation(sg[k][0:fw, :], psG[k][0:fw, :], ACT.Silu).then_inc(silu_done, 1)

            skewed(a_.Fori, NG, [(silu, 2), (copy, 1)], by=4)

        @block.vector
        def _(v):
            v.sem_inc(h_done, 2)
            v.sem_inc(x3_done, 4)

            def mult(n, q):
                v.wait_ge(down_done, n + 1)
                for c, (f0, fw) in enumerate(F_CHUNKS):
                    k = (NC * q + c) % 2
                    v.wait_ge(silu_done, NC * n + c + 3)
                    nc.vector.tensor_tensor(h[q % 2][c][0:fw, :], psU[k][0:fw, :], sg[k][0:fw, :], ALU.mult)\
                        .then_inc(h_done, 1)

            def finish(n, q):
                s = q % 2
                v.wait_ge(down_done, n + 3)
                v.wait_ge(stored[s], 16 * uses(n, s))
                nc.vector.tensor_tensor(x3[s][:, :, :], sum_all[:, bass.ds(n * GT, GT), :],
                                        psD[s][:, :].rearrange("p (t c) -> p t c", t=GT), ALU.add).then_inc(x3_done, 1)

            skewed(v.Fori, NG, [(finish, 3), (mult, 2)], by=4)

        @block.tensor
        def _(t_):
            t_.sem_inc(turned, 2)
            t_.sem_inc(up_done, 2 * NC)
            t_.sem_inc(down_done, 2)
            t_.wait_ge(setup, 2)
            t_.wait_ge(weights, 96)

            def turn(n, q):
                t_.wait_ge(loaded[q], 16 * uses(n, q, 4))
                t_.wait_ge(xT_copied, n + 1)
                for t in range(GT):
                    last = nc.tensor.transpose(psT[q % 2][:, t * P:(t + 1) * P], xr[q % 2][:, t, :], ident[:, :])
                last.then_inc(turned, 1)

            def up(n, q):
                t_.wait_ge(xT_copied, n + 3)
                for c, (f0, fw) in enumerate(F_CHUNKS):
                    k = (NC * q + c) % 2
                    t_.wait_ge(h_done, NC * n + c + 1)
                    nc.tensor.matmul(psG[k][0:fw, :], wg[:, f0:f0 + fw], xT[q % 2][:, :], start=True, stop=True)
                    nc.tensor.matmul(psU[k][0:fw, :], wu[:, f0:f0 + fw], xT[q % 2][:, :], start=True, stop=True)\
                        .then_inc(up_done, 1)

            def down(n, q):
                t_.wait_ge(h_done, NC * n + NC + 2)
                t_.wait_ge(x3_done, n + 3)
                for t in range(GT):
                    for c, (f0, fw) in enumerate(F_CHUNKS):
                        last = nc.tensor.matmul(psD[q % 2][:, t * D:(t + 1) * D], h[q % 2][c][0:fw, t * P:(t + 1) * P],
                                                wd[0:fw, c, :], start=(c == 0), stop=(c == NC - 1))
                last.then_inc(down_done, 1)

            skewed(t_.Fori, NG, [(down, 3), (up, 2), (turn, 1)], by=4)


LIGHT, HEAVY = D // 2, 4 * D
E_CAP = 20.0
TOP = 128
FETCH = 9.0 / 8.0 * TOP
DESCENTS = 50
STEPS = 7
ROUNDS = (DESCENTS - 1) // STEPS


def two_branch_phase(nc, sem, x_dram, token, light, heavy, base_all, heavy_all, s_all):
    HC = HEAVY // P
    with Phase(nc, "two") as ph:
        def two(name, shape, dt=F32):
            return [ph.sb(f"{name}{s}", shape, dt) for s in range(2)]
        x_in = [ph.sb(f"x{s}", [P, GT, D]) for s in range(8)]
        y, z, zT = two("y", [P, GT, D]), two("z", [P, GT, D]), two("zT", [P, GW])
        hl, hh = two("hl", [LIGHT, GW]), two("hh", [P, HC, GW])
        junk = two("junk", [P, D])
        st, mv, rstd, rr = two("st", [P, GT, 6]), two("mv", [P, GT, 2]), two("rstd", [P, GT]), two("rr", [P, GT])
        w1l, w1h = ph.sb("w1l", [P, LIGHT]), ph.sb("w1h", [P, HEAVY])
        w2l, w2h = ph.sb("w2l", [LIGHT, D]), ph.sb("w2h", [P, HC, D])
        gl, gh = ph.sb("gl", [P, 1]), ph.sb("gh", [P, 1])
        b1l, b1h = ph.sb("b1l", [LIGHT, 1]), ph.sb("b1h", [P, HC])
        b2l, b2h, tok = ph.sb("b2l", [P, 1, D]), ph.sb("b2h", [P, 1, D]), ph.sb("tok", [P, D])
        ident, power = ph.sb("ident", [P, P]), ph.sb("power", [P, GT])
        psT = [ph.ps("psT0")]
        psL = [ph.ps("psL0")]
        psH = [ph.ps(f"psH{s}") for s in range(2)]
        psDL, psDH = [[ph.ps(f"{k}{s}") for s in range(2)] for k in ("DL", "DH")]
        setup, weights, scaled = sem("setup"), sem("weights"), sem("scaled")
        divider = sem("divider")
        loaded = [sem(f"loaded{s}") for s in range(8)]
        stats_chain, rstd_chain, y_chain, turned, zT_copied = [sem(k) for k in (
            "stats_chain", "rstd_chain", "y_chain", "turned", "zT_copied")]
        up_done, gelu_done, down_done, out_done = [sem(k) for k in ("up_done", "gelu_done", "down_done", "out_done")]
        base_step = sem("base_step")
        NY = 3 * GT
        UP = HC + 1
        block = ph.block()
        one = lambda a: a.rearrange("(c a) -> c a", a=1)
        loads = [(w1l[:, :], light[1]), (w1h[:, :], heavy[1]), (w2l[:, :], light[3]),
                 (w2h[:, :, :], heavy[3].rearrange("(m p) c -> p m c", p=P)), (gl[:, :], one(light[0])),
                 (gh[:, :], one(heavy[0])), (b1l[:, :], one(light[2])), (b2l[:, 0, :], bc_rows(light[4], D)),
                 (b2h[:, 0, :], bc_rows(heavy[4], D)), (tok[:, :], bc_rows(token, D))]
        loads += [(b1h[:, m:m + 1], one(heavy[2][m * P:(m + 1) * P])) for m in range(HC)]
        NW = 16 * len(loads)

        @block.sync
        def _(sp):
            for dst, src in loads:
                sp.dma_start(dst, src).then_inc(weights, 16)

            def load(n, q):
                sp.wait_ge(out_done, n + 1)
                sp.dma_start(x_in[q][:, :, :], rows_of(x_dram, n)).then_inc(loaded[q], 16)

            skewed(sp.Fori, NG, [(load, 0)], by=8)

        @block.gpsimd
        def _(g):
            emit_identity(nc, g, ident, setup)
            g.memset(power[:, :], -0.5).then_inc(setup, 1)
            g.wait_ge(setup, 3)
            rc = Count(rstd_chain, RMS_STEPS)

            def rstds(n, q):
                s = q % 2
                wait_apart(g, divider, (stats_chain, (n + 1) * STATS_STEPS), (y_chain, (n + 1) * NY))
                rc.start(n)
                emit_rstd(nc, g, rc, mv[s], rstd[s], power, divider, rms=(None, rr[s]))
                rc.end()

            skewed(g.Fori, NG, [(rstds, 1)], by=8)

        @block.vector
        def _(v):
            v.sem_inc(y_chain, 2 * NY)
            v.sem_inc(out_done, 8)
            c1 = Count(stats_chain, STATS_STEPS)
            c2 = Count(y_chain, NY, 2)
            v.wait_ge(weights, NW)
            nc.vector.tensor_scalar(w1l[:, :], w1l[:, :], gl[:, 0:1], None, ALU.mult).then_inc(scaled, 1)
            nc.vector.tensor_scalar(w1h[:, :], w1h[:, :], gh[:, 0:1], None, ALU.mult).then_inc(scaled, 1)

            def stats(n, q):
                s = q % 2
                c1.start(n)
                v.wait_ge(loaded[q], 16 * uses(n, q, 8))
                emit_stats(nc, v, c1, x_in[q], st[s], mv[s], divider)
                c1.end()

            def norm(n, q):
                s = q % 2
                c2.start(n)
                v.wait_ge(rstd_chain, (n + 1) * RMS_STEPS)
                v.wait_ge(turned, n + 1)
                emit_apply(nc, c2, x_in[q], y[s], mv[s], rstd[s])
                c2.wait(v)
                for t in range(GT):
                    c2.inc(nc.vector.tensor_scalar(z[s][:, t, :], y[s][:, t, :], rr[s][:, t:t + 1], None, ALU.mult))
                for t in range(GT):
                    if t >= 2:
                        v.wait_ge(c2.sem, c2.base + c2.c - 1)
                    c2.inc(nc.vector.tensor_tensor_reduce(out=junk[t % 2][:, :], in0=y[s][:, t, :], in1=tok[:, :],
                                                          scale=1.0, scalar=0.0, op0=ALU.mult, op1=ALU.add,
                                                          accum_out=s_all[:, bass.ds(n * GT + t, 1)]))
                c2.end()

            def finish(n, q):
                s = q % 2
                base, hv = [t[:, bass.ds(n * GT, GT), :] for t in (base_all, heavy_all)]
                v.wait_ge(down_done, n + 3)
                nc.vector.tensor_tensor(base, x_in[q][:, :, :],
                                        psDL[s][:, :].rearrange("p (t c) -> p t c", t=GT), ALU.add).then_inc(base_step, 1)
                nc.vector.tensor_tensor(hv, psDH[s][:, :].rearrange("p (t c) -> p t c", t=GT),
                                        b2h[:, :, :].to_broadcast([P, GT, D]), ALU.add)
                v.wait_ge(base_step, n + 1)
                nc.vector.tensor_tensor(base, base, b2l[:, :, :].to_broadcast([P, GT, D]), ALU.add).then_inc(out_done, 1)

            skewed(v.Fori, NG, [(finish, 5), (norm, 2), (stats, 1)], by=8)

        @block.scalar
        def _(a_):
            a_.sem_inc(gelu_done, 2 * UP)
            a_.wait_ge(weights, NW)

            def gelus(n, q):
                s = q % 2
                a_.wait_ge(down_done, n + 1)
                for c in range(UP):
                    a_.wait_ge(up_done, UP * n + c + 1)
                    if c == 0:
                        ins = nc.scalar.activation(hl[s][:, :], psL[0][0:LIGHT, :], ACT.Gelu, bias=b1l[:, 0:1])
                    else:
                        ins = nc.scalar.activation(hh[s][:, c - 1, :], psH[c % 2][:, :], ACT.Gelu, bias=b1h[:, c - 1:c])
                    ins.then_inc(gelu_done, 1)

            def copy(n, q):
                a_.wait_ge(turned, n + 3)
                if not (isinstance(n, int) and n < 2):
                    a_.wait_ge(up_done, UP * (n - 1))
                nc.scalar.activation(zT[q % 2][:, :], psT[0][:, :], ACT.Copy).then_inc(zT_copied, 1)

            skewed(a_.Fori, NG, [(gelus, 4), (copy, 3)], by=8)

        @block.tensor
        def _(t_):
            t_.sem_inc(turned, 2)
            t_.sem_inc(down_done, 2)
            t_.wait_ge(setup, 2)
            t_.wait_ge(scaled, 2)

            def turn(n, q):
                t_.wait_ge(y_chain, (n + 3) * NY)
                if not (isinstance(n, int) and n == 0):
                    t_.wait_ge(zT_copied, n)
                for t in range(GT):
                    last = nc.tensor.transpose(psT[0][:, t * P:(t + 1) * P], z[q % 2][:, t, :], ident[:, :])
                last.then_inc(turned, 1)

            def up(n, q):
                t_.wait_ge(zT_copied, n + 1)
                for c in range(UP):
                    if c == 0:
                        t_.wait_ge(gelu_done, UP * (n + 1) + 1)
                        ins = nc.tensor.matmul(psL[0][0:LIGHT, :], w1l[:, :], zT[q % 2][:, :], start=True, stop=True)
                    else:
                        t_.wait_ge(gelu_done, UP * (n + 1) + c + 2 if c <= 2 else UP * (n + 2) + c - 1)
                        ins = nc.tensor.matmul(psH[c % 2][:, :], w1h[:, (c - 1) * P:c * P], zT[q % 2][:, :],
                                               start=True, stop=True)
                    ins.then_inc(up_done, 1)

            def down(n, q):
                s = q % 2
                t_.wait_ge(gelu_done, UP * (n + 3))
                t_.wait_ge(out_done, n + 7)
                for t in range(GT):
                    nc.tensor.matmul(psDL[s][:, t * D:(t + 1) * D], hl[s][:, t * P:(t + 1) * P], w2l[:, :],
                                     start=True, stop=True)
                for t in range(GT):
                    for m in range(HC):
                        last = nc.tensor.matmul(psDH[s][:, t * D:(t + 1) * D], hh[s][:, m, t * P:(t + 1) * P],
                                                w2h[:, m, :], start=(m == 0), stop=(m == HC - 1))
                last.then_inc(down_done, 1)

            skewed(t_.Fori, NG, [(down, 5), (up, 4), (turn, 3)], by=8)


def descent_phase(nc, sem, s_all, coef_all):
    assert DESCENTS - 1 == ROUNDS * STEPS and STEPS * math.log(S / FETCH) < E_CAP
    assert STEPS * math.log(FETCH) < 40.0
    ROWS = NT
    LOGK = math.log(FETCH)
    with Phase(nc, "desc") as ph:
        s64, t64, e64 = ph.sb("s64", [ROWS, P]), ph.sb("t64", [ROWS, P]), ph.sb("e64", [ROWS, P])
        s8, key8, work = ph.sb("s8", [B, S]), ph.sb("key8", [B, S]), [ph.sb(f"work{k}", [B, S]) for k in range(2)]
        sc8, gt8, eq8, cum8, zeros = [ph.sb(k, [B, S]) for k in ("sc8", "gt8", "eq8", "cum8", "zeros")]
        key64, low64 = ph.sb("key64", [ROWS, P]), ph.sb("low64", [ROWS, P])
        coef64 = ph.sb("coef64", [ROWS, P])
        top8 = ph.sb("top8", [B, 8])
        smax8, smax, nega, M, lnz, acc = [ph.sb(k, [ROWS, 1]) for k in ("smax8", "smax", "nega", "M", "lnz", "acc")]
        need = ph.sb("need", [B, 1])
        spread, same, ident = ph.sb("spread", [B, B, 8]), ph.sb("same", [ROWS, B, 8]), ph.sb("ident", [P, P])
        psA, psB = ph.ps("psA"), ph.ps("psB")
        divider, summed = sem("divider"), sem("summed")
        setup, turned, chain, moved, zed, expd, lnd, dd = [sem(k) for k in (
            "setup", "turned", "chain", "moved", "zed", "expd", "lnd", "dd")]
        block = ph.block()

        @block.gpsimd
        def _(g):
            emit_identity(nc, g, ident, setup)
            g.memset(spread[:, :, :], 0.0)
            g.memset(same[:, :, :], 1.0 / FETCH)
            g.memset(zeros[:, :], 0.0).then_inc(setup, 1)
            g.wait_ge(setup, 3)
            g.affine_select(out=spread[:, :, :], in_=spread[:, :, :], compare_op=ALU.not_equal, fill=1.0, base=0,
                            pattern=[[-1, B], [0, 8]], channel_multiplier=1)
            g.affine_select(out=same[:, :, :], in_=same[:, :, :], compare_op=ALU.is_ge, fill=0.0, base=0,
                            pattern=[[-8, B], [0, 8]], channel_multiplier=1).then_inc(setup, 1)
            g.wait_ge(setup, 4)
            g.affine_select(out=same[:, :, :], in_=same[:, :, :], compare_op=ALU.is_ge, fill=0.0, base=7,
                            pattern=[[8, B], [0, 8]], channel_multiplier=-1).then_inc(setup, 1)

        @block.tensor
        def _(t_):
            t_.wait_ge(setup, 5)
            nc.tensor.transpose(psA[0:ROWS, 0:P], s_all[:, :], ident[:, :]).then_inc(turned, 1)
            t_.wait_ge(chain, 2)
            nc.tensor.matmul(psB[0:ROWS, 0:1], spread[:, :, :].rearrange("b c j -> b (c j)"), smax8[0:B, :],
                             start=True, stop=True).then_inc(turned, 1)
            with t_.Fori(0, ROUNDS) as r:
                for j in range(STEPS):
                    wait_apart(t_, divider, (summed, STEPS * r + j + 1))
                    nc.tensor.matmul(psA[0:ROWS, 256:257], same[:, :, :].rearrange("b c j -> b (c j)"), acc[:, :],
                                     start=True, stop=True).then_inc(zed, 1)
            t_.wait_ge(moved, 48)
            nc.tensor.transpose(psB[:, 128:128 + ROWS], coef64[:, :], ident[0:ROWS, 0:ROWS]).then_inc(turned, 1)

        @block.scalar
        def _(a_):
            with a_.Fori(0, ROUNDS) as r:
                a_.wait_ge(dd, 3 * r + 3)
                nc.scalar.activation(e64[:, :], t64[:, :], ACT.Exp).then_inc(expd, 1)
                a_.wait_ge(zed, STEPS * r + STEPS)
                nc.scalar.activation(lnz[:, :], psA[0:ROWS, 256:257], ACT.Ln).then_inc(lnd, 1)
            a_.wait_ge(moved, 32)
            nc.scalar.activation(sc8[:, :], key8[:, :], ACT.Exp).then_inc(expd, 1)

        @block.sync
        def _(sp):
            sp.wait_ge(chain, 1)
            sp.dma_start(s8[:, :], s64[:, :]).then_inc(moved, 16)
            sp.wait_ge(chain, 5)
            sp.dma_start(key8[:, :], key64[:, :]).then_inc(moved, 16)
            sp.wait_ge(lnd, ROUNDS + 1)
            sp.dma_start(coef64[:, :], gt8[:, :]).then_inc(moved, 16)

        @block.vector
        def _(v):
            c = Count(chain, 0)

            def link(ins):
                c.inc(ins)
                c.wait(v)

            v.wait_ge(turned, 1)
            link(nc.vector.tensor_copy(s64[:, :], psA[0:ROWS, 0:P]))
            v.wait_ge(moved, 16)
            link(nc.vector.tensor_reduce(smax8[0:B, :], s8[:, :], AX.X, ALU.max))
            v.wait_ge(turned, 2)
            link(nc.vector.tensor_copy(smax[:, :], psB[0:ROWS, 0:1]))
            nc.vector.memset(nega[:, :], math.log(S) - LOGK).then_inc(dd, 1)
            with v.Fori(0, ROUNDS) as r:
                v.wait_ge(dd, 3 * r + 1)
                nc.vector.tensor_tensor(M[:, :], smax[:, :], nega[:, :], ALU.min).then_inc(dd, 1)
                v.wait_ge(dd, 3 * r + 2)
                nc.vector.tensor_scalar(t64[:, :], s64[:, :], M[:, 0:1], E_CAP, ALU.subtract, ALU.min).then_inc(dd, 1)
                for j in range(STEPS):
                    if j == 0:
                        v.wait_ge(expd, r + 1)
                    else:
                        v.wait_ge(zed, STEPS * r + j)
                    nc.vector.tensor_scalar(low64[:, :], e64[:, :], psA[0:ROWS, 256:257] if j else 1.0, 0.0, ALU.min,
                                            ALU.add, accum_out=acc[:, :]).then_inc(summed, 1)
                v.wait_ge(lnd, r + 1)
                nc.vector.tensor_tensor(nega[:, :], lnz[:, :], M[:, :], ALU.add).then_inc(dd, 1)
            v.wait_ge(dd, 3 * ROUNDS + 1)
            link(nc.vector.tensor_scalar(key64[:, :], s64[:, :], nega[:, 0:1], 0.0, ALU.subtract, ALU.min))
            link(nc.vector.tensor_scalar(key64[:, :], key64[:, :], -104.0, None, ALU.max))
            v.wait_ge(moved, 32)
            cur = key8
            for r in range(TOP // 8):
                link(nc.vector.max(top8[:, :], cur[:, :]))
                if r < TOP // 8 - 1:
                    link(nc.vector.match_replace(work[r % 2][:, :], top8[:, :], cur[:, :], -1.0e30))
                    cur = work[r % 2]
            bar = top8[:, 7:8]
            link(nc.vector.tensor_scalar(gt8[:, :], key8[:, :], bar, None, ALU.is_gt))
            link(nc.vector.tensor_scalar(eq8[:, :], key8[:, :], bar, None, ALU.is_equal))
            link(nc.vector.tensor_reduce(need[:, :], gt8[:, :], AX.X, ALU.add))
            link(nc.vector.tensor_scalar(need[:, :], need[:, :], -1.0, float(TOP), ALU.mult, ALU.add))
            link(nc.vector.tensor_tensor_scan(cum8[:, :], eq8[:, :], zeros[:, :], 0.0, ALU.add, ALU.add))
            link(nc.vector.scalar_tensor_tensor(out=eq8[:, :], in0=cum8[:, :], scalar=need[:, 0:1], in1=eq8[:, :],
                                                op0=ALU.is_le, op1=ALU.mult))
            link(nc.vector.tensor_tensor(gt8[:, :], gt8[:, :], eq8[:, :], ALU.add))
            v.wait_ge(expd, ROUNDS + 1)
            link(nc.vector.tensor_scalar(eq8[:, :], sc8[:, :], -1.0, 1.0, ALU.mult, ALU.add))
            link(nc.vector.tensor_tensor(eq8[:, :], eq8[:, :], sc8[:, :], ALU.add))
            nc.vector.tensor_tensor(gt8[:, :], gt8[:, :], eq8[:, :], ALU.mult).then_inc(lnd, 1)
            v.wait_ge(turned, 3)
            nc.vector.tensor_copy(coef_all[:, :], psB[:, 128:128 + ROWS]).then_inc(dd, 1)


def last_phase(nc, sem, base_all, heavy_all, coef_all, out_dram):
    with Phase(nc, "last") as ph:
        out = [ph.sb(f"o{s}", [P, GT, D]) for s in range(2)]
        stored = [sem(f"stored{s}") for s in range(2)]
        summed = sem("summed")
        block = ph.block()

        @block.vector
        def _(v):
            def total(n, s):
                v.wait_ge(stored[s], 16 * uses(n, s))
                for t in range(GT):
                    last = nc.vector.scalar_tensor_tensor(
                        out=out[s][:, t, :], in0=heavy_all[:, bass.ds(n * GT + t, 1), :].rearrange("p a c -> p (a c)"),
                        scalar=coef_all[:, bass.ds(n * GT + t, 1)],
                        in1=base_all[:, bass.ds(n * GT + t, 1), :].rearrange("p a c -> p (a c)"),
                        op0=ALU.mult, op1=ALU.add)
                last.then_inc(summed, 1)

            skewed(v.Fori, NG, [(total, 0)])

        @block.sync
        def _(sp):
            for s in range(2):
                sp.sem_inc(stored[s], 16)

            def store(n, s):
                sp.wait_ge(summed, n + 1)
                sp.dma_start(rows_of(out_dram, n), out[s][:, :, :]).then_inc(stored[s], 16)

            skewed(sp.Fori, NG, [(store, 0)])
            for s in range(2):
                sp.wait_ge(stored[s], 16 * (NG // 2 + 1))


def program(nc, x, i, out):
    U32 = mybir.dt.uint32
    phase_name, used = [""], []

    def sem(name):
        used.append(nc.alloc_semaphore(name=f"{phase_name[0]}_{name}"))
        return used[-1]

    def give_back():
        nc.clear_and_free_semaphores(used)
        nc.all_engine_barrier()
        used.clear()

    def dram(name, shape, dt=F32):
        return nc.dram_tensor(name, shape, dt, kind="Internal").ap()

    qd, kd = [dram(k, [H, 3 * HD, T], BF16) for k in ("q_parts", "k_parts")]
    vd, att = dram("values", [T, D]), dram("attention", [T, D])
    xn, x2, x3 = dram("xn", [T, D]), dram("x2", [T, D]), dram("x3", [T, D])
    xsorted, ysorted = dram("x_sorted", [SORTED_TILES * P, D]), dram("y_sorted", [SORTED_TILES * P, D])
    fwd, rev = dram("bias_fwd", [H, 2 * WINDOW]), dram("bias_rev", [H, 2 * WINDOW])

    phase_name[0] = "qkv0"
    qkv_phase(nc, sem, "qkv0", x, i["L0_attn_w_qkv"], HD ** -0.5, qd, kd, vd)
    phase_name[0] = "att0"
    attention_phase(nc, sem, "att0", qd, kd, vd, att, True)
    with ExitStack() as moe:
        def keep(name, shape, dt=F32):
            return moe.enter_context(nc.sbuf_tensor(name, shape, dt))
        onehot, weight = keep("onehot", [P, NT, NE]), keep("weight", [P, NT])
        x1 = keep("x1", [P, NT, D])
        place, expert_row = keep("place", [P, NT], U32), keep("expert_row", [P, SORTED_TILES], I32)
        phase_name[0] = "mix"
        mix_phase(nc, sem, x, att, i["L0_attn_w_out"], i["L0_ffn_gate_w"], x1, xn, xsorted, onehot, weight)
        phase_name[0] = "place"
        place_phase(nc, sem, onehot, place, expert_row)
        phase_name[0] = "scatter"
        weights = sem("weights")
        tables, loads = expert_weights(keep, i["L0_ffn_w1"], i["L0_ffn_b1"], i["L0_ffn_w2"], i["L0_ffn_b2"])
        scatter_phase(nc, sem, xn, xsorted, place, loads, weights, beside=lambda block: bias_phase(
            nc, sem, block, i["L1_attn_offsets"], i["L1_attn_pos_bias"], fwd, rev))
        phase_name[0] = "experts"
        experts_phase(nc, sem, xsorted, ysorted, tables, expert_row)
        phase_name[0] = "gather"
        gather_phase(nc, sem, x1, ysorted, place, weight, x2)
    give_back()
    phase_name[0] = "qkv1"
    qkv_phase(nc, sem, "qkv1", x2, i["L1_attn_w_qkv"], HD ** -0.5, qd, kd, vd, i["L1_attn_norm1_scale"])
    phase_name[0] = "att1"
    attention_phase(nc, sem, "att1", qd, kd, vd, att, False, rev, fwd)
    with nc.sbuf_tensor("sum", [P, NT, D], F32) as total:
        phase_name[0] = "gated"
        gated_phase(nc, sem, x2, att, i["L1_attn_w_gate"], i["L1_attn_b_gate"], i["L1_attn_norm1_scale"],
                    i["L1_attn_w_out"], total, xn)
        phase_name[0] = "swiglu"
        swiglu_phase(nc, sem, xn, total, i["L1_attn_norm2_scale"], i["L1_attn_w_ffn_gate"],
                     i["L1_attn_w_ffn_up"], i["L1_attn_w_ffn_down"], x3)
    with ExitStack() as route:
        s_all = route.enter_context(nc.sbuf_tensor("s_all", [P, NT], F32))
        coef = route.enter_context(nc.sbuf_tensor("coef", [P, NT], F32))
        base, heavy = [route.enter_context(nc.sbuf_tensor(k, [P, NT, D], F32)) for k in ("base", "heavy")]
        phase_name[0] = "two"
        two_branch_phase(nc, sem, x3, i["L1_ffn_routing_token"],
                         [i[f"L1_ffn_light_{k}"] for k in ("gamma", "w1", "b1", "w2", "b2")],
                         [i[f"L1_ffn_heavy_{k}"] for k in ("gamma", "w1", "b1", "w2", "b2")], base, heavy, s_all)
        phase_name[0] = "descent"
        descent_phase(nc, sem, s_all, coef)
        phase_name[0] = "last"
        last_phase(nc, sem, base, heavy, coef, out)


def kernel(**inputs):
    import numpy as np
    import concourse.bacc as bacc
    from concourse.bass_utils import run_bass_kernel_spmd

    nc = bacc.Bacc("TRN2", target_bir_lowering=False, num_devices=1)
    arrays, given = {}, {}
    for name, a in inputs.items():
        a = np.ascontiguousarray(a)
        if name == "L0_attn_x":
            a = a.reshape(T, D)
        arrays[f"in_{name}"] = a
        given[name] = nc.dram_tensor(f"in_{name}", a.shape, mybir.dt.from_np(a.dtype), kind="ExternalInput").ap()
    out = nc.dram_tensor("out", (T, D), F32, kind="ExternalOutput").ap()
    program(nc, given["L0_attn_x"], given, out)
    r = run_bass_kernel_spmd(nc, [arrays], core_ids=[0])
    return r.results[0]["out"].reshape(B, S, D)
```
